# Optimizing a Trainium2 kernel written in Bass

```python
import numpy as np
import jax
import jax.numpy as jnp

def _softmax(x, axis=-1):
    return jax.nn.softmax(x, axis=axis)

def _gelu(x):
    return jax.nn.gelu(x, approximate=True)

def _silu(x):
    return jax.nn.silu(x)

def _sigmoid(x):
    return jax.nn.sigmoid(x)

def _layernorm(x, axis=-1, eps=1e-05):
    m = jnp.mean(x, axis=axis, keepdims=True)
    v = jnp.var(x, axis=axis, keepdims=True)
    return (x - m) / jnp.sqrt(v + eps)

def _scatter_add(tgt, idx, src, axis=0):
    return tgt.at[idx].add(src)

def _segment_sum(src, seg, n):
    return jax.ops.segment_sum(src, seg, n)
kernel_name = 'mk_recurrent_d2_jaxref_r8_c1b32c'

def setup_inputs(seed: int=0):
    np.random.seed(seed)
    _w = jnp.asarray

    def _L0_attn_setup():
        import jax, jax.numpy as jnp
        import numpy as np
        B, T, DIM = (2, 128, 128)
        H, D = (16, 64)
        key = jax.random.key(seed)
        k1, k2, k3, k4 = jax.random.split(key, 4)
        s = DIM ** (-0.5)
        return {'x': jax.random.normal(k1, (B, T, DIM), jnp.float32), 'w_qkv': jax.random.normal(k2, (DIM, 3 * H * D), jnp.float32) * s, 'w_gate': jax.random.normal(k3, (DIM, H * D), jnp.float32) * s, 'w_out': jax.random.normal(k4, (H * D, DIM), jnp.float32) * s}
    _L0_attn_in = _L0_attn_setup()

    def _L0_ffn_setup():
        import jax, jax.numpy as jnp
        import numpy as np
        B, S, D, E, TOP_K = (2, 128, 128, 8, 2)
        H = 4 * D
        key = jax.random.key(seed)
        ks = jax.random.split(key, 12)
        sc = 0.02
        return {'x': jax.random.normal(ks[0], (B, S, D), jnp.float32), 'Wg': jax.random.normal(ks[1], (E, D), jnp.float32) * sc, 'bg': jnp.zeros((E,), jnp.float32), 'bias': jnp.zeros((E,), jnp.float32), 'W1': jax.random.normal(ks[2], (E, H, D), jnp.float32) * sc, 'b1': jnp.zeros((E, H), jnp.float32), 'W2': jax.random.normal(ks[3], (E, D, H), jnp.float32) * sc, 'b2': jnp.zeros((E, D), jnp.float32), 'Ws1': jax.random.normal(ks[4], (H, D), jnp.float32) * sc, 'bs1': jnp.zeros((H,), jnp.float32), 'Ws2': jax.random.normal(ks[5], (D, H), jnp.float32) * sc, 'bs2': jnp.zeros((D,), jnp.float32)}
    _L0_ffn_in = _L0_ffn_setup()

    def _L1_attn_setup():
        import jax, jax.numpy as jnp
        import numpy as np
        D_MODEL = 128
        D_STATE = 64
        D_CONV = 4
        EXPAND = 2
        HEADDIM = 64
        D_INNER = EXPAND * D_MODEL
        NHEADS = D_INNER // HEADDIM
        CONV_DIM = D_INNER + 2 * D_STATE
        D_IN_PROJ = 2 * D_INNER + 2 * D_STATE + NHEADS
        BATCH, SEQLEN = (4, 256)
        DT_MIN, DT_MAX = (0.05, 1.0)
        EPS = 1e-05

        def _make_params(key, prefix):
            ks = jax.random.split(key, 5)
            p = {}
            p[prefix + 'in_w'] = jax.random.normal(ks[0], (D_IN_PROJ, D_MODEL), jnp.float32) * D_MODEL ** (-0.5)
            p[prefix + 'conv_w'] = jax.random.normal(ks[1], (CONV_DIM, D_CONV), jnp.float32) * D_CONV ** (-0.5)
            p[prefix + 'conv_b'] = jnp.zeros((CONV_DIM,), jnp.float32)
            u = jax.random.uniform(ks[2], (NHEADS,), jnp.float32)
            dt = jnp.exp(u * (np.log(DT_MAX) - np.log(DT_MIN)) + np.log(DT_MIN))
            p[prefix + 'dt_bias'] = dt + jnp.log(-jnp.expm1(-dt)) + 1.0
            p[prefix + 'A_log'] = jnp.log(jax.random.uniform(ks[3], (NHEADS,), jnp.float32, minval=1.0, maxval=16.0))
            p[prefix + 'Dp'] = jnp.ones((NHEADS,), jnp.float32)
            p[prefix + 'norm_w'] = jnp.ones((D_INNER,), jnp.float32)
            p[prefix + 'out_w'] = jax.random.normal(ks[4], (D_MODEL, D_INNER), jnp.float32) * D_INNER ** (-0.5)
            return p

        def _dconv(x, w, b):
            xt = x.transpose(0, 2, 1)
            out = jax.lax.conv_general_dilated(xt, w[:, None, :], (1,), [(D_CONV - 1, 0)], feature_group_count=CONV_DIM)
            return (out + b[:, None]).transpose(0, 2, 1)

        def _ssd(dt, A, xh, Bm, Cm):
            dA = jnp.exp(dt * A)

            def step(S, inp):
                dA_t, dt_t, x_t, B_t, C_t = inp
                S = S * dA_t[:, :, None, None] + (dt_t[:, :, None] * x_t)[..., None] * B_t[:, None, None, :]
                y = jnp.einsum('bhpn,bn->bhp', S, C_t)
                return (S, y)
            S0 = jnp.zeros((dt.shape[0], NHEADS, HEADDIM, D_STATE), dt.dtype)
            xs = (dA.swapaxes(0, 1), dt.swapaxes(0, 1), xh.swapaxes(0, 1), Bm.swapaxes(0, 1), Cm.swapaxes(0, 1))
            _, ys = jax.lax.scan(step, S0, xs)
            return ys.swapaxes(0, 1)

        def _mamba2(x, in_w, conv_w, conv_b, dt_bias, A_log, Dp, norm_w, out_w):
            Bsz, L, _ = x.shape
            zxbcdt = x @ in_w.T
            z = zxbcdt[..., :D_INNER]
            xBC = zxbcdt[..., D_INNER:D_INNER + CONV_DIM]
            dt = jax.nn.softplus(zxbcdt[..., D_INNER + CONV_DIM:] + dt_bias)
            xBC = jax.nn.silu(_dconv(xBC, conv_w, conv_b))
            xh = xBC[..., :D_INNER].reshape(Bsz, L, NHEADS, HEADDIM)
            Bm = xBC[..., D_INNER:D_INNER + D_STATE]
            Cm = xBC[..., D_INNER + D_STATE:]
            A = -jnp.exp(A_log)
            y = _ssd(dt, A, xh, Bm, Cm) + Dp[None, None, :, None] * xh
            y = y.reshape(Bsz, L, D_INNER) * jax.nn.silu(z)
            y = y * jax.lax.rsqrt(jnp.mean(y * y, -1, keepdims=True) + EPS) * norm_w
            return y @ out_w.T
        key = jax.random.key(seed)
        k1, k2, k3 = jax.random.split(key, 3)
        inp = {'x': jax.random.normal(k1, (BATCH, SEQLEN, D_MODEL), jnp.float32)}
        inp.update(_make_params(k2, 'f_'))
        inp.update(_make_params(k3, 'b_'))
        return inp
    _L1_attn_in = _L1_attn_setup()

    def _L1_ffn_setup():
        import jax, jax.numpy as jnp
        import numpy as np
        H = 128
        I = 512
        E = 4
        LN_EPS = 1e-12

        def _layer_norm(x, gamma, beta, eps=LN_EPS):
            mu = jnp.mean(x, axis=-1, keepdims=True)
            var = jnp.mean(jnp.square(x - mu), axis=-1, keepdims=True)
            return (x - mu) * jax.lax.rsqrt(var + eps) * gamma + beta
        key = jax.random.key(seed)
        ks = jax.random.split(key, 8)
        B, S = (4, 64)
        scale = 0.02
        return {'hidden_states': jax.random.normal(ks[0], (B, S, H), jnp.float32), 'W_router': jax.random.normal(ks[1], (H, E), jnp.float32) * scale, 'W1': jax.random.normal(ks[2], (E, H, I), jnp.float32) * scale, 'b1': jax.random.normal(ks[3], (E, I), jnp.float32) * scale, 'Wo': jax.random.normal(ks[4], (I, H), jnp.float32) * scale, 'bo': jax.random.normal(ks[5], (H,), jnp.float32) * scale, 'ln_gamma': jnp.ones((H,), jnp.float32), 'ln_beta': jnp.zeros((H,), jnp.float32)}
    _L1_ffn_in = _L1_ffn_setup()
    _d = {'L0_attn_x': _L0_attn_in['x'], 'L0_attn_w_qkv': _L0_attn_in['w_qkv'], 'L0_attn_w_gate': _L0_attn_in['w_gate'], 'L0_attn_w_out': _L0_attn_in['w_out'], 'L0_ffn_Wg': _L0_ffn_in['Wg'], 'L0_ffn_bg': _L0_ffn_in['bg'], 'L0_ffn_bias': _L0_ffn_in['bias'], 'L0_ffn_W1': _L0_ffn_in['W1'], 'L0_ffn_b1': _L0_ffn_in['b1'], 'L0_ffn_W2': _L0_ffn_in['W2'], 'L0_ffn_b2': _L0_ffn_in['b2'], 'L0_ffn_Ws1': _L0_ffn_in['Ws1'], 'L0_ffn_bs1': _L0_ffn_in['bs1'], 'L0_ffn_Ws2': _L0_ffn_in['Ws2'], 'L0_ffn_bs2': _L0_ffn_in['bs2'], 'L1_attn_f_in_w': _L1_attn_in['f_in_w'], 'L1_attn_f_conv_w': _L1_attn_in['f_conv_w'], 'L1_attn_f_conv_b': _L1_attn_in['f_conv_b'], 'L1_attn_f_dt_bias': _L1_attn_in['f_dt_bias'], 'L1_attn_f_A_log': _L1_attn_in['f_A_log'], 'L1_attn_f_Dp': _L1_attn_in['f_Dp'], 'L1_attn_f_norm_w': _L1_attn_in['f_norm_w'], 'L1_attn_f_out_w': _L1_attn_in['f_out_w'], 'L1_attn_b_in_w': _L1_attn_in['b_in_w'], 'L1_attn_b_conv_w': _L1_attn_in['b_conv_w'], 'L1_attn_b_conv_b': _L1_attn_in['b_conv_b'], 'L1_attn_b_dt_bias': _L1_attn_in['b_dt_bias'], 'L1_attn_b_A_log': _L1_attn_in['b_A_log'], 'L1_attn_b_Dp': _L1_attn_in['b_Dp'], 'L1_attn_b_norm_w': _L1_attn_in['b_norm_w'], 'L1_attn_b_out_w': _L1_attn_in['b_out_w'], 'L1_ffn_W_router': _L1_ffn_in['W_router'], 'L1_ffn_W1': _L1_ffn_in['W1'], 'L1_ffn_b1': _L1_ffn_in['b1'], 'L1_ffn_Wo': _L1_ffn_in['Wo'], 'L1_ffn_bo': _L1_ffn_in['bo'], 'L1_ffn_ln_gamma': _L1_ffn_in['ln_gamma'], 'L1_ffn_ln_beta': _L1_ffn_in['ln_beta']}
    _x0 = _d['L0_attn_x']
    _d['L0_attn_x'] = jax.random.normal(jax.random.fold_in(jax.random.key(seed), 1), (2, 1024, 128), dtype=_x0.dtype)
    del _x0
    return _d

def reference(L0_attn_x, L0_attn_w_qkv, L0_attn_w_gate, L0_attn_w_out, L0_ffn_Wg, L0_ffn_bg, L0_ffn_bias, L0_ffn_W1, L0_ffn_b1, L0_ffn_W2, L0_ffn_b2, L0_ffn_Ws1, L0_ffn_bs1, L0_ffn_Ws2, L0_ffn_bs2, L1_attn_f_in_w, L1_attn_f_conv_w, L1_attn_f_conv_b, L1_attn_f_dt_bias, L1_attn_f_A_log, L1_attn_f_Dp, L1_attn_f_norm_w, L1_attn_f_out_w, L1_attn_b_in_w, L1_attn_b_conv_w, L1_attn_b_conv_b, L1_attn_b_dt_bias, L1_attn_b_A_log, L1_attn_b_Dp, L1_attn_b_norm_w, L1_attn_b_out_w, L1_ffn_W_router, L1_ffn_W1, L1_ffn_b1, L1_ffn_Wo, L1_ffn_bo, L1_ffn_ln_gamma, L1_ffn_ln_beta):

    def _L0_attn_ref(x, w_qkv, w_gate, w_out):
        import jax, jax.numpy as jnp
        import numpy as np
        B, T, DIM = (2, 128, 128)
        H, D = (16, 64)
        b, t, c = x.shape
        qkv = (x @ w_qkv).reshape(b, t, 3, H, D)
        q, k, v = (qkv[:, :, 0], qkv[:, :, 1], qkv[:, :, 2])
        gate = jax.nn.sigmoid((x @ w_gate).reshape(b, t, H, D))
        q = jax.nn.elu(q) + 1.0
        k = jax.nn.elu(k) + 1.0
        k_cum = jnp.cumsum(k, axis=1)
        kv = jnp.cumsum(k[..., None, :] * v[..., :, None], axis=1)
        numerator = jnp.einsum('bthj,bthij->bthi', q, kv)
        denominator = jnp.einsum('bthj,bthj->bth', q, k_cum)
        out = numerator / (denominator[..., None] + 1e-06)
        out = out * gate
        return out.reshape(b, t, H * D) @ w_out

    def _L0_ffn_ref(x, Wg, bg, bias, W1, b1, W2, b2, Ws1, bs1, Ws2, bs2):
        import jax, jax.numpy as jnp
        import numpy as np
        B, S, D, E, TOP_K = (2, 128, 128, 8, 2)
        H = 4 * D
        b, s, d = x.shape
        xf = x.reshape(-1, d)
        T = xf.shape[0]
        scores = jax.nn.sigmoid(xf @ Wg.T + bg + bias)
        top_scores, top_idx = jax.lax.top_k(scores, TOP_K)
        weights = jnp.zeros((T, E), scores.dtype)
        weights = weights.at[jnp.arange(T)[:, None], top_idx].add(top_scores)
        h = jax.nn.gelu(jnp.einsum('td,ehd->teh', xf, W1) + b1, approximate=False)
        eo = jnp.einsum('teh,edh->ted', h, W2) + b2
        combined = jnp.einsum('ted,te->td', eo, weights)
        shared = jax.nn.gelu(xf @ Ws1.T + bs1, approximate=False) @ Ws2.T + bs2
        return (shared + combined).reshape(b, s, d)

    def _L1_attn_ref(x, f_in_w, f_conv_w, f_conv_b, f_dt_bias, f_A_log, f_Dp, f_norm_w, f_out_w, b_in_w, b_conv_w, b_conv_b, b_dt_bias, b_A_log, b_Dp, b_norm_w, b_out_w):
        import jax, jax.numpy as jnp
        import numpy as np
        D_MODEL = 128
        D_STATE = 64
        D_CONV = 4
        EXPAND = 2
        HEADDIM = 64
        D_INNER = EXPAND * D_MODEL
        NHEADS = D_INNER // HEADDIM
        CONV_DIM = D_INNER + 2 * D_STATE
        D_IN_PROJ = 2 * D_INNER + 2 * D_STATE + NHEADS
        BATCH, SEQLEN = (4, 256)
        DT_MIN, DT_MAX = (0.05, 1.0)
        EPS = 1e-05

        def _make_params(key, prefix):
            ks = jax.random.split(key, 5)
            p = {}
            p[prefix + 'in_w'] = jax.random.normal(ks[0], (D_IN_PROJ, D_MODEL), jnp.float32) * D_MODEL ** (-0.5)
            p[prefix + 'conv_w'] = jax.random.normal(ks[1], (CONV_DIM, D_CONV), jnp.float32) * D_CONV ** (-0.5)
            p[prefix + 'conv_b'] = jnp.zeros((CONV_DIM,), jnp.float32)
            u = jax.random.uniform(ks[2], (NHEADS,), jnp.float32)
            dt = jnp.exp(u * (np.log(DT_MAX) - np.log(DT_MIN)) + np.log(DT_MIN))
            p[prefix + 'dt_bias'] = dt + jnp.log(-jnp.expm1(-dt)) + 1.0
            p[prefix + 'A_log'] = jnp.log(jax.random.uniform(ks[3], (NHEADS,), jnp.float32, minval=1.0, maxval=16.0))
            p[prefix + 'Dp'] = jnp.ones((NHEADS,), jnp.float32)
            p[prefix + 'norm_w'] = jnp.ones((D_INNER,), jnp.float32)
            p[prefix + 'out_w'] = jax.random.normal(ks[4], (D_MODEL, D_INNER), jnp.float32) * D_INNER ** (-0.5)
            return p

        def _dconv(x, w, b):
            xt = x.transpose(0, 2, 1)
            out = jax.lax.conv_general_dilated(xt, w[:, None, :], (1,), [(D_CONV - 1, 0)], feature_group_count=CONV_DIM)
            return (out + b[:, None]).transpose(0, 2, 1)

        def _ssd(dt, A, xh, Bm, Cm):
            dA = jnp.exp(dt * A)

            def step(S, inp):
                dA_t, dt_t, x_t, B_t, C_t = inp
                S = S * dA_t[:, :, None, None] + (dt_t[:, :, None] * x_t)[..., None] * B_t[:, None, None, :]
                y = jnp.einsum('bhpn,bn->bhp', S, C_t)
                return (S, y)
            S0 = jnp.zeros((dt.shape[0], NHEADS, HEADDIM, D_STATE), dt.dtype)
            xs = (dA.swapaxes(0, 1), dt.swapaxes(0, 1), xh.swapaxes(0, 1), Bm.swapaxes(0, 1), Cm.swapaxes(0, 1))
            _, ys = jax.lax.scan(step, S0, xs)
            return ys.swapaxes(0, 1)

        def _mamba2(x, in_w, conv_w, conv_b, dt_bias, A_log, Dp, norm_w, out_w):
            Bsz, L, _ = x.shape
            zxbcdt = x @ in_w.T
            z = zxbcdt[..., :D_INNER]
            xBC = zxbcdt[..., D_INNER:D_INNER + CONV_DIM]
            dt = jax.nn.softplus(zxbcdt[..., D_INNER + CONV_DIM:] + dt_bias)
            xBC = jax.nn.silu(_dconv(xBC, conv_w, conv_b))
            xh = xBC[..., :D_INNER].reshape(Bsz, L, NHEADS, HEADDIM)
            Bm = xBC[..., D_INNER:D_INNER + D_STATE]
            Cm = xBC[..., D_INNER + D_STATE:]
            A = -jnp.exp(A_log)
            y = _ssd(dt, A, xh, Bm, Cm) + Dp[None, None, :, None] * xh
            y = y.reshape(Bsz, L, D_INNER) * jax.nn.silu(z)
            y = y * jax.lax.rsqrt(jnp.mean(y * y, -1, keepdims=True) + EPS) * norm_w
            return y @ out_w.T
        out_fwd = _mamba2(x, f_in_w, f_conv_w, f_conv_b, f_dt_bias, f_A_log, f_Dp, f_norm_w, f_out_w)
        x_rev = jnp.flip(x, 1)
        out_bwd = _mamba2(x_rev, b_in_w, b_conv_w, b_conv_b, b_dt_bias, b_A_log, b_Dp, b_norm_w, b_out_w)
        return out_fwd + jnp.flip(out_bwd, 1)

    def _L1_ffn_ref(hidden_states, W_router, W1, b1, Wo, bo, ln_gamma, ln_beta):
        import jax, jax.numpy as jnp
        import numpy as np
        H = 128
        I = 512
        E = 4
        LN_EPS = 1e-12

        def _layer_norm(x, gamma, beta, eps=LN_EPS):
            mu = jnp.mean(x, axis=-1, keepdims=True)
            var = jnp.mean(jnp.square(x - mu), axis=-1, keepdims=True)
            return (x - mu) * jax.lax.rsqrt(var + eps) * gamma + beta
        B, S, _ = hidden_states.shape
        x = hidden_states.reshape(-1, H)
        logits = x @ W_router
        expert_idx = jnp.argmax(logits, axis=-1)
        h = jnp.einsum('th,ehi->tei', x, W1) + b1
        h = jax.nn.gelu(h, approximate=False)
        onehot = jax.nn.one_hot(expert_idx, E, dtype=x.dtype)
        intermediate = jnp.einsum('te,tei->ti', onehot, h)
        y = intermediate @ Wo + bo + x
        y = _layer_norm(y, ln_gamma, ln_beta)
        return y.reshape(B, S, H)
    x = L0_attn_x
    xn = _layernorm(x, axis=-1)
    s = _L0_attn_ref(xn, L0_attn_w_qkv, L0_attn_w_gate, L0_attn_w_out)
    g = _silu(_L0_ffn_ref(xn, L0_ffn_Wg, L0_ffn_bg, L0_ffn_bias, L0_ffn_W1, L0_ffn_b1, L0_ffn_W2, L0_ffn_b2, L0_ffn_Ws1, L0_ffn_bs1, L0_ffn_Ws2, L0_ffn_bs2))
    x = x + s * g
    xn = _layernorm(x, axis=-1)
    s = _L1_attn_ref(xn, L1_attn_f_in_w, L1_attn_f_conv_w, L1_attn_f_conv_b, L1_attn_f_dt_bias, L1_attn_f_A_log, L1_attn_f_Dp, L1_attn_f_norm_w, L1_attn_f_out_w, L1_attn_b_in_w, L1_attn_b_conv_w, L1_attn_b_conv_b, L1_attn_b_dt_bias, L1_attn_b_A_log, L1_attn_b_Dp, L1_attn_b_norm_w, L1_attn_b_out_w)
    g = _silu(_L1_ffn_ref(xn, L1_ffn_W_router, L1_ffn_W1, L1_ffn_b1, L1_ffn_Wo, L1_ffn_bo, L1_ffn_ln_gamma, L1_ffn_ln_beta))
    x = x + s * g
    return x

_drawn_inputs = setup_inputs


def setup_inputs(seed=0):
    import zlib

    import numpy as np

    out = dict(_drawn_inputs(seed))
    spreads = {'L0_ffn_bg': (0.0, 0.8),
     'L0_ffn_bias': (0.0, 0.8),
     'L0_ffn_b1': (0.0, 0.8),
     'L0_ffn_b2': (0.0, 0.8),
     'L0_ffn_bs1': (0.0, 0.8),
     'L0_ffn_bs2': (0.0, 0.725),
     'L1_attn_f_conv_b': (0.0, 0.759),
     'L1_attn_f_Dp': (1.0, 0.6),
     'L1_attn_f_norm_w': (1.0, 0.6),
     'L1_attn_b_conv_b': (0.0, 0.77),
     'L1_attn_b_Dp': (1.0, 0.6),
     'L1_attn_b_norm_w': (1.0, 0.6),
     'L1_ffn_ln_gamma': (1.0, 0.567),
     'L1_ffn_ln_beta': (0.0, 0.8)}
    factors = {'L0_attn_w_qkv': 3.47,
     'L0_attn_w_gate': 8.0,
     'L0_attn_w_out': 3.486,
     'L0_ffn_Wg': 6.519,
     'L0_ffn_W1': 8.0,
     'L0_ffn_W2': 8.0,
     'L0_ffn_Ws1': 8.0,
     'L0_ffn_Ws2': 7.89,
     'L1_ffn_b1': 64.0,
     'L1_ffn_bo': 25.864,
     'L1_attn_f_A_log': 8.0,
     'L1_attn_b_dt_bias': 3.36,
     'L1_attn_b_A_log': 43.096,
     'L1_ffn_W_router': 8.0,
     'L1_ffn_W1': 8.0,
     'L1_ffn_Wo': 8.0}
    for name, (base, spread) in spreads.items():
        noise = np.random.default_rng([zlib.crc32(name.encode()), seed]).standard_normal(out[name].shape)
        drawn = base * np.exp(spread * noise) if base else spread * noise
        out[name] = jnp.asarray(drawn.astype(out[name].dtype))
    for name, factor in factors.items():
        out[name] = (out[name] * factor).astype(out[name].dtype)
    return out
```

```python
from contextlib import ExitStack

import concourse.bass as bass
from concourse import mybir

F32 = mybir.dt.float32
ALU = mybir.AluOpType
ACT = mybir.ActivationFunctionType
AX = mybir.AxisListType

P = 128
B, T, D = 2, 1024, 128
NT = T // P
GT = 4
GW = GT * P
NG = NT // GT
H, HD = 16, 64
NP = H // 2
E0, HT = 8, 4
HA = HD + 1
E1 = 4
MH, MN = 4, 64
DI = MH * 64
TAP = 4
CW = P + TAP - 1
NB = 8
HUGE = 2.0 ** 64
START = 1


class Jobs:

    def __init__(self, names, base):
        self.at = {name: i for i, name in enumerate(names)}
        assert len(self.at) == len(names)
        self.per = [len(range(k, len(names), NB)) for k in range(NB)]
        self.base = base

    def bank(self, name):
        return self.at[name] % NB

    def count(self, name, it, before=0):
        k = self.bank(name)
        return it * self.per[k] + (self.base[k] + self.at[name] // NB + 1 - before * self.per[k])

    def after(self, iterations):
        return [b + iterations * n for b, n in zip(self.base, self.per)]


def attention_jobs():
    names = []
    for u in range(NG):
        names += [("xT", u), ("router", u)]
        names += [("qk", u, j) for j in range(2 * NP)]
        names += [("wT", u)]
        names += [("v", u, k, i) for k in range(GT) for i in range(2)]
        names += [("gate", u, k, i) for k in range(GT) for i in range(2)]
        names += [("bias2", u)]
        for p in range(NP):
            names += [("kt", u, p), ("score", u, p, 0), ("score", u, p, 1), ("h", u, p, 0), ("h", u, p, 1),
                      ("kv", u, p, 0), ("kv", u, p, 1), ("h", u, p, 2), ("h", u, p, 3)]
            if p:
                names += [("oT", u, p - 1)]
            names += [("o", u, p, 0), ("o", u, p, 1), ("ffn", u, p)]
        names += [("h", u, E0, i) for i in range(HT)]
        names += [("oT", u, NP - 1), ("ffn", u, E0), ("attn", u)]
        names += [("x2f", u), ("x2r", u), ("dt", u)]
    return names


def mamba_jobs():
    names = [("L", d, b) for d in range(2) for b in range(B)]
    names += [("conv", d, i) for d in range(2) for i in range(3)]
    names += [("z", d) for d in range(2)]
    names += [("P", d) for d in range(2)]
    names += [("tr", d, b) for d in range(2) for b in range(B)]
    names += [("G", d) for d in range(2)]
    for d in range(2):
        names += [("y", d, b) for b in range(B)]
        names += [("S", d)]
    names += [("yT", d) for d in range(2)]
    return names


def last_jobs():
    names = []
    for u in range(NG):
        names += [("ohT", u)] + [("mask", u, e) for e in range(E1)]
        names += [("sT", u)] + [("h", u, i) for i in range(HT)]
        names += [("s", u), ("ffn", u)]
    return names


def mean_and_variance(dve, stats, mean, part, var_eps, eps, then):
    even, odd = stats[:, :, 1], stats[:, :, 4]
    dve.tensor_tensor(part[:, 0, :], even, odd, ALU.subtract)
    dve.tensor_tensor(part[:, 1, :], stats[:, :, 2], stats[:, :, 5], ALU.add)
    then(dve.tensor_tensor(mean[:, :], even, odd, ALU.add))
    dve.tensor_tensor(part[:, 0, :], part[:, 0, :], part[:, 0, :], ALU.mult)
    dve.tensor_scalar(mean[:, :], mean[:, :], 0.5, None, ALU.mult)
    then(dve.tensor_scalar(part[:, 1, :], part[:, 1, :], 1.0 / D, eps, ALU.mult, ALU.add))
    return dve.scalar_tensor_tensor(out=var_eps[:, :], in0=part[:, 0, :], scalar=0.25, in1=part[:, 1, :],
                                    op0=ALU.mult, op1=ALU.add)


def build(nc, a, out):
    pairs_ready = NP * NG
    with ExitStack() as ctx:
        def sb(name, *shape, stack=ctx, dt=F32):
            return stack.enter_context(nc.sbuf_tensor(name, list(shape), dt))

        def sem(name):
            return ctx.enter_context(nc.semaphore(name))

        bank = [ctx.enter_context(nc.psum_tensor(f"bank{k}", [P, 512], F32)) for k in range(NB)]
        bank_full = [sem(f"bank_full{k}") for k in range(NB)]
        bank_done = [sem(f"bank_done{k}") for k in range(NB)]

        x_all = sb("x_all", P, B, NT, D)
        xn2_all = sb("xn2_all", P, B, NT, D)
        xTf_all = sb("xTf_all", P, B, TAP - 1 + T)
        xTr_all = sb("xTr_all", P, B, TAP - 1 + T)
        dtf_all = sb("dtf_all", P, B, NT, 2 * MH)
        dtr_all = sb("dtr_all", P, B, NT, MH)
        ident = sb("ident", P, P)
        flip = sb("flip", P, P)
        ident4 = sb("ident4", P, 4, P)
        causal = sb("causal", P, P)
        ones = sb("ones", P, P)
        before = sb("before", P, 8, 8)
        minus_half = sb("minus_half", P, 8)
        dtw = sb("dtw", P, 3 * MH)

        const_ready, credit = sem("const_ready"), sem("credit")
        w_x, w_qk, w_vg, w_router, w_ffn, w_b, w_out_s = (sem(n) for n in (
            "x_loaded", "qk_loaded", "vg_loaded", "router_loaded", "ffn_loaded", "b_loaded", "wout_loaded"))
        l1_loaded = sem("l1_loaded")

        ahead = {n: sem(n) for n in ("og_ready", "x1_ready", "pool_copied", "xE_ready", "yn_ready", "yg_ready",
                                     "xD_ready", "pool1")}
        og_ready, x1_ready, pool_copied, xE_ready, yn_ready, yg_ready, xD_ready, pool1 = ahead.values()
        out_stored = [sem(f"out_stored{u}") for u in range(NG)]

        L0 = Jobs(attention_jobs(), None)
        L0.base = list(L0.per)
        L1 = Jobs(mamba_jobs(), L0.after(B))
        L2 = Jobs(last_jobs(), L1.after(NT))

        def awaiting(jobs):
            def await_full(eng, it, *name, before=0):
                eng.wait_ge(bank_full[jobs.bank(name)], jobs.count(name, it, before))

            def await_done(eng, it, *name, before=0):
                eng.wait_ge(bank_done[jobs.bank(name)], jobs.count(name, it, before))

            def opened(eng, it, *name):
                k = jobs.bank(name)
                eng.wait_ge(bank_done[k], it * jobs.per[k] + (jobs.base[k] + jobs.at[name] // NB))
                return bank[k]

            def psum(*name):
                return bank[jobs.bank(name)]

            def filled(ins, *name):
                ins.then_inc(bank_full[jobs.bank(name)], 1)

            def taken(ins, *name):
                ins.then_inc(bank_done[jobs.bank(name)], 1)

            return await_full, await_done, opened, psum, filled, taken

        with nc.Block() as block:
            @block.gpsimd
            def _(pool):
                pool.memset(ident[:, :], 0.0).then_inc(const_ready, 1)
                pool.memset(flip[:, :], 0.0).then_inc(const_ready, 1)
                pool.memset(causal[:, :], 1.0).then_inc(const_ready, 1)
                pool.memset(before[:, :, :], 1.0).then_inc(const_ready, 1)
                pool.memset(ones[:, :], 1.0)
                pool.memset(minus_half[:, :], -0.5)
                pool.memset(xTf_all[:, :, 0:TAP - 1], 0.0)
                pool.memset(xTr_all[:, :, 0:TAP - 1], 0.0)
                pool.wait_ge(const_ready, 4)
                pool.affine_select(out=ident[:, :], in_=ident[:, :], compare_op=ALU.not_equal, fill=1.0,
                                   base=0, pattern=[[-1, P]], channel_multiplier=1).then_inc(const_ready, 1)
                pool.affine_select(out=flip[:, :], in_=flip[:, :], compare_op=ALU.not_equal, fill=1.0,
                                   base=1 - P, pattern=[[1, P]], channel_multiplier=1)
                pool.affine_select(out=causal[:, :], in_=causal[:, :], compare_op=ALU.is_ge, fill=0.0,
                                   base=0, pattern=[[1, P]], channel_multiplier=-1)
                pool.affine_select(out=before[:, :, :], in_=before[:, :, :], compare_op=ALU.is_gt, fill=0.0,
                                   base=0, pattern=[[1, 8], [-1, 8]], channel_multiplier=0)
                pool.wait_ge(const_ready, 5)
                for h in range(4):
                    pool.tensor_copy(ident4[:, h, :], ident[:, :])

            @block.sync
            def _(sp):
                for k in range(NB):
                    sp.sem_inc(bank_full[k], L0.per[k])
                    sp.sem_inc(bank_done[k], L0.per[k])
                for s in ahead.values():
                    sp.sem_inc(s, START)
                for u in range(NG):
                    sp.sem_inc(out_stored[u], 16)
                for b in range(B):
                    for u in range(NG):
                        sp.dma_start(x_all[:, b, u * GT:(u + 1) * GT, :],
                                     a["x"][b, u * GW:(u + 1) * GW, :].rearrange("(k p) d -> p k d", p=P)
                                     ).then_inc(w_x, 16)

        with ExitStack() as l0:
            def s0(name, *shape):
                return sb(name, *shape, stack=l0)

            wqkv = s0("wqkv", P, 3 * H * HD)
            wgate = s0("wgate", P, H * HD)
            wout = s0("wout", P, NP, D)
            w1 = s0("w1", P, E0 + 1, 512)
            w2 = s0("w2", P, E0 + 1, HT, D)
            b1 = s0("b1", P, E0 + 1, HT)
            b2 = s0("b2", E0 + 1, D)
            wg = s0("wg", P, E0)
            bg_b = s0("bg_b", P, E0)
            bias_b = s0("bias_b", P, E0)

            xn_g = s0("xn_g", P, GT, D)
            xT_g = s0("xT_g", P, GW)
            stats = s0("stats", P, GT, 6)
            mean = s0("mean", P, GT)
            part = s0("part", P, 2, GT)
            vareps = s0("vareps", P, GT)
            rstd = s0("rstd", P, GT)
            logit = s0("logit", P, GT, E0)
            sexp = s0("sexp", P, GT, E0)
            score = s0("score", P, GT, E0)
            gt3 = s0("gt3", P, GT, E0, E0)
            eq3 = s0("eq3", P, GT, E0, E0)
            rank = s0("rank", P, GT, E0)
            w9 = s0("w9", P, GT, E0 + 1)
            wT9 = s0("wT9", E0 + 1, GW)
            ebuf = s0("ebuf", P, 2, GW)
            qT = s0("qT", P, NP, GW)
            kT = s0("kT", P, NP, GW)
            v1 = s0("v1", P, GT, H, HA)
            gate = s0("gate", P, GT, H * HD)
            ktok = s0("ktok", P, GT, P)
            sm = s0("sm", P, 2, GT, P)
            kvc = s0("kvc", P, NP, 2, HA)
            kvw = s0("kvw", P, GT - 1, 2, HA)
            rden = s0("rden", P, GT, 2)
            o_g = s0("o_g", P, GT, P)
            og_g = s0("og_g", P, GT, P)
            oT = qT
            hT = s0("hT", P, HT, GW)
            facc = s0("facc", P, GT, D)
            th = xn_g
            sg = o_g
            x1_g = s0("x1_g", P, GT, D)
            xn2_g = s0("xn2_g", P, GT, D)
            x2f_g = s0("x2f_g", P, GW)
            x2r_g = s0("x2r_g", P, GW)

            var_ready, rstd_ready, xn_ready = sem("var_ready"), sem("rstd_ready"), sem("xn_ready")
            sexp_ready, w9_ready = sem("sexp_ready"), sem("w9_ready")
            exp_ready, kv_ready = sem("exp_ready"), sem("kv_ready")
            th_ready = sem("th_ready")
            dve0 = sem("dve0")
            await_full, await_done, opened, psum, filled, taken = awaiting(L0)
            MW = 64

            with nc.Block() as block:
                @block.sync
                def _(sp):
                    sp.dma_start(wg[:, :], a["wg"]).then_inc(w_router, 16)
                    sp.dma_start(bg_b[:, :], a["bg"].partition_broadcast(P)).then_inc(w_router, 16)
                    sp.dma_start(bias_b[:, :], a["bias"].partition_broadcast(P)).then_inc(w_router, 16)
                    sp.dma_start(wqkv[:, 0:2048], a["w_qkv"][:, 0:2048]).then_inc(w_qk, 16)
                    sp.dma_start(wqkv[:, 2048:3072], a["w_qkv"][:, 2048:3072]).then_inc(w_vg, 16)
                    sp.dma_start(wgate[:, :], a["w_gate"]).then_inc(w_vg, 16)
                    sp.dma_start(b1[:, 0:E0, :], a["b1"]).then_inc(w_b, 16)
                    sp.dma_start(b1[:, E0, :], a["bs1"]).then_inc(w_b, 16)
                    sp.dma_start(b2[0:E0, :], a["b2"]).then_inc(w_b, 16)
                    sp.dma_start(b2[E0:E0 + 1, :], a["bs2"]).then_inc(w_b, 16)
                    for e in range(E0 + 1):
                        sp.dma_start(w1[:, e, :], a["w1"][e] if e < E0 else a["ws1"]).then_inc(w_ffn, 16)
                        sp.dma_start(w2[:, e, :, :], a["w2"][e] if e < E0 else a["ws2"]).then_inc(w_ffn, 16)
                    sp.wait_ge(w_ffn, 16 * 2 * (E0 + 1))
                    sp.dma_start(wout[:, :, :], a["w_out"]).then_inc(w_out_s, 16)
                    sp.dma_start(dtw[:, :], a["dtw"]).then_inc(w_router, 16)

                @block.tensor
                def _(pe):
                    def layer(b):
                        def h_job(u, e, i):
                            pe.wait_ge(w_ffn, 32 * (E0 + 1))
                            o = opened(pe, b, "h", u, e, i)
                            filled(pe.matmul(o[:, :], w1[:, e, i * P:(i + 1) * P], xT_g[:, :],
                                             start=True, stop=True), "h", u, e, i)

                        def ffn_job(u, e):
                            o = opened(pe, b, "ffn", u, e)
                            for i in range(HT):
                                await_done(pe, b, "h", u, e, i)
                            for k in range(GT):
                                for i in range(HT):
                                    m = pe.matmul(o[:, k * P:(k + 1) * P], hT[:, i, k * P:(k + 1) * P],
                                                  w2[:, e, i, :], start=(i == 0), stop=(i == HT - 1))
                            filled(m, "ffn", u, e)

                        def oT_job(u, p):
                            o = opened(pe, b, "oT", u, p)
                            pe.wait_ge(og_ready, b * pairs_ready + (u * NP + p + 1) + START)
                            for k in range(GT):
                                m = pe.transpose(o[:, k * P:(k + 1) * P], og_g[:, k, :], ident[:, :])
                            filled(m, "oT", u, p)

                        for u in range(NG):
                            o = opened(pe, b, "xT", u)
                            pe.wait_ge(xn_ready, b * NG * 2 + (2 * u + 1))
                            for k in range(GT):
                                m = pe.transpose(o[:, k * P:(k + 1) * P], xn_g[:, k, :], ident[:, :])
                            filled(m, "xT", u)
                            await_done(pe, b, "xT", u)
                            pe.wait_ge(w_router, 48)
                            o = opened(pe, b, "router", u)
                            for k in range(GT):
                                m = pe.matmul(o[:, k * E0:(k + 1) * E0], xT_g[:, k * P:(k + 1) * P], wg[:, :],
                                              start=True, stop=True)
                            filled(m, "router", u)
                            pe.wait_ge(w_qk, 16)
                            for j in range(2 * NP):
                                p, which = j // 2, j % 2
                                o = opened(pe, b, "qk", u, j)
                                c = which * H * HD + p * P
                                filled(pe.matmul(o[:, :], wqkv[:, c:c + P], xT_g[:, :], start=True, stop=True),
                                       "qk", u, j)
                            o = opened(pe, b, "wT", u)
                            pe.wait_ge(w9_ready, b * NG + (u + 1))
                            for k in range(GT):
                                m = pe.transpose(o[0:E0 + 1, k * P:(k + 1) * P], w9[:, k, :], ident[:, :])
                            filled(m, "wT", u)
                            pe.wait_ge(w_vg, 32)
                            for name, w, c0 in (("v", wqkv, 2 * H * HD), ("gate", wgate, 0)):
                                for k in range(GT):
                                    for i in range(2):
                                        o = opened(pe, b, name, u, k, i)
                                        filled(pe.matmul(o[:, :], xT_g[:, k * P:(k + 1) * P],
                                                         w[:, c0 + i * 512:c0 + (i + 1) * 512],
                                                         start=True, stop=True), name, u, k, i)
                            o = opened(pe, b, "bias2", u)
                            await_done(pe, b, "wT", u)
                            pe.wait_ge(w_b, 64)
                            for k in range(GT):
                                m = pe.matmul(o[:, k * P:(k + 1) * P], wT9[:, k * P:(k + 1) * P], b2[:, :],
                                              start=True, stop=True)
                            filled(m, "bias2", u)
                            for p in range(NP):
                                await_done(pe, b, "qk", u, 2 * p)
                                await_done(pe, b, "qk", u, 2 * p + 1)
                                o = opened(pe, b, "kt", u, p)
                                for k in range(GT):
                                    m = pe.transpose(o[:, k * P:(k + 1) * P], kT[:, p, k * P:(k + 1) * P],
                                                     ident[:, :])
                                filled(m, "kt", u, p)
                                for hh in range(2):
                                    r = slice(MW * hh, MW * hh + HD)
                                    o = opened(pe, b, "score", u, p, hh)
                                    for k in range(GT):
                                        c = slice(k * P, (k + 1) * P)
                                        m = pe.matmul(o[:, c], kT[r, p, c], qT[r, p, c], start=True, stop=True)
                                    filled(m, "score", u, p, hh)
                                h_job(u, p, 0)
                                h_job(u, p, 1)
                                await_done(pe, b, "kt", u, p)
                                if p == 0:
                                    for k in range(GT):
                                        for i in range(2):
                                            await_done(pe, b, "v", u, k, i)
                                for i in range(2):
                                    o = opened(pe, b, "kv", u, p, i)
                                    for kk in range(2):
                                        k = 2 * i + kk
                                        m = pe.matmul(o[:, kk * 2 * HA:(kk + 1) * 2 * HA], ktok[:, k, :],
                                                      v1[:, k, 2 * p:2 * p + 2, :].rearrange("s h i -> s (h i)"),
                                                      start=True, stop=True)
                                    filled(m, "kv", u, p, i)
                                h_job(u, p, 2)
                                h_job(u, p, 3)
                                if p:
                                    oT_job(u, p - 1)
                                await_done(pe, b, "score", u, p, 0)
                                await_done(pe, b, "score", u, p, 1)
                                pe.wait_ge(kv_ready, b * pairs_ready + (u * NP + p + 1))
                                for i in range(2):
                                    o = opened(pe, b, "o", u, p, i)
                                    for kk in range(2):
                                        k = 2 * i + kk
                                        c = slice(k * P, (k + 1) * P)
                                        state = kvc[:, p, :, :] if k == 0 else kvw[:, k - 1, :, :]
                                        pe.matmul(o[:, kk * 2 * HA:(kk + 1) * 2 * HA], qT[:, p, c],
                                                  state.rearrange("j h i -> j (h i)"), start=True, stop=True)
                                        for hh in range(2):
                                            c0 = (2 * kk + hh) * HA
                                            m = pe.matmul(o[:, c0:c0 + HA], sm[:, hh, k, :], v1[:, k, 2 * p + hh, :],
                                                          start=False, stop=True, skip_group_check=True)
                                    filled(m, "o", u, p, i)
                                ffn_job(u, p)
                            for i in range(HT):
                                h_job(u, E0, i)
                            oT_job(u, NP - 1)
                            ffn_job(u, E0)
                            o = opened(pe, b, "attn", u)
                            for p in range(NP):
                                await_done(pe, b, "oT", u, p)
                            pe.wait_ge(w_out_s, 16)
                            for k in range(GT):
                                for p in range(NP):
                                    m = pe.matmul(o[:, k * P:(k + 1) * P], oT[:, p, k * P:(k + 1) * P],
                                                  wout[:, p, :], start=(p == 0), stop=(p == NP - 1))
                            filled(m, "attn", u)
                            o = opened(pe, b, "x2f", u)
                            pe.wait_ge(xn_ready, b * NG * 2 + (2 * u + 2))
                            for k in range(GT):
                                m = pe.transpose(o[:, k * P:(k + 1) * P], xn2_g[:, k, :], ident[:, :])
                            filled(m, "x2f", u)
                            o = opened(pe, b, "x2r", u)
                            for k in range(GT):
                                kr = GT - 1 - k
                                m = pe.transpose(o[:, kr * P:(kr + 1) * P], xn2_g[:, k, :], flip[:, :])
                            filled(m, "x2r", u)
                            o = opened(pe, b, "dt", u)
                            await_done(pe, b, "x2f", u)
                            await_done(pe, b, "x2r", u)
                            pe.wait_ge(w_router, 64)
                            for k in range(GT):
                                c = slice(k * P, (k + 1) * P)
                                pe.matmul(o[:, 8 * k:8 * k + 8], x2f_g[:, c], dtw[:, 0:8], start=True, stop=True)
                                m = pe.matmul(o[:, 32 + 4 * k:36 + 4 * k], x2r_g[:, c], dtw[:, 8:12],
                                              start=True, stop=True)
                            filled(m, "dt", u)

                    with pe.Fori(0, B) as b:
                        layer(b)

                @block.scalar
                def _(act):
                    def layer(b):
                        for u in range(NG):
                            await_full(act, b, "xT", u)
                            taken(act.activation(xT_g[:, :], psum("xT", u)[:, :], ACT.Copy), "xT", u)
                            await_done(act, b, "router", u)
                            act.activation(sexp[:, :, :], logit[:, :, :], ACT.Exp, scale=-1.0).then_inc(sexp_ready, 1)
                            for j in range(2 * NP):
                                await_full(act, b, "qk", u, j)
                                if j >= 2:
                                    await_done(act, b, "qk", u, j - 2)
                                else:
                                    await_done(act, b, "qk", (u + 1) % 2, 2 * NP - 2 + j, before=1 - u)
                                act.activation(ebuf[:, j % 2, :], psum("qk", u, j)[:, :], ACT.Exp
                                               ).then_inc(exp_ready, 1)
                            await_full(act, b, "wT", u)
                            taken(act.activation(wT9[:, :], psum("wT", u)[0:E0 + 1, :], ACT.Copy), "wT", u)
                            for k in range(GT):
                                for i in range(2):
                                    await_full(act, b, "v", u, k, i)
                                    src = psum("v", u, k, i)[:, :].rearrange("t (h i) -> t h i", i=HD)
                                    taken(act.activation(v1[:, k, 8 * i:8 * i + 8, 0:HD], src, ACT.Copy),
                                          "v", u, k, i)
                            act.wait_ge(og_ready, b * pairs_ready + u * NP + START)
                            for k in range(GT):
                                for i in range(2):
                                    await_full(act, b, "gate", u, k, i)
                                    taken(act.activation(gate[:, k, 512 * i:512 * i + 512],
                                                         psum("gate", u, k, i)[:, :], ACT.Sigmoid), "gate", u, k, i)
                            act.wait_ge(x1_ready, b * NG + u + START)
                            await_full(act, b, "bias2", u)
                            taken(act.activation(facc[:, :, :], psum("bias2", u)[:, :].rearrange("t (k d) -> t k d", k=GT),
                                                 ACT.Copy), "bias2", u)

                            def gelu(e, i):
                                await_full(act, b, "h", u, e, i)
                                taken(act.activation(hT[:, i, :], psum("h", u, e, i)[:, :], ACT.Gelu,
                                                     bias=b1[:, e, i:i + 1]), "h", u, e, i)

                            def oT_copy(p):
                                await_full(act, b, "oT", u, p)
                                taken(act.activation(oT[:, p, :], psum("oT", u, p)[:, :], ACT.Copy), "oT", u, p)

                            act.wait_ge(w_b, 64)
                            for p in range(NP):
                                await_full(act, b, "kt", u, p)
                                taken(act.activation(ktok[:, :, :], psum("kt", u, p)[:, :].rearrange("t (k d) -> t k d", k=GT),
                                                     ACT.Copy), "kt", u, p)
                                for i in range(HT):
                                    gelu(p, i)
                                if p:
                                    oT_copy(p - 1)
                            for i in range(HT):
                                gelu(E0, i)
                            oT_copy(NP - 1)
                            await_done(act, b, "ffn", u, E0)
                            act.activation(th[:, :, :], facc[:, :, :], ACT.Tanh, scale=0.5).then_inc(th_ready, 1)
                            act.wait_ge(pool_copied, b * NG + u + START)
                            await_full(act, b, "x2f", u)
                            taken(act.activation(x2f_g[:, :], psum("x2f", u)[:, :], ACT.Copy), "x2f", u)
                            await_full(act, b, "x2r", u)
                            taken(act.activation(x2r_g[:, :], psum("x2r", u)[:, :], ACT.Copy), "x2r", u)

                    with act.Fori(0, B) as b:
                        layer(b)

                @block.gpsimd
                def _(pool):
                    def layer(b):
                        for u in range(NG):
                            pool.wait_ge(var_ready, b * NG * 2 + (2 * u + 1))
                            pool.tensor_tensor(rstd[:, :], vareps[:, :], minus_half[:, 0:GT], ALU.pow
                                               ).then_inc(rstd_ready, 1)
                            for p in range(NP):
                                await_done(pool, b, "o", u, p, 0)
                                await_done(pool, b, "o", u, p, 1)
                                if p == 0:
                                    for k in range(GT):
                                        for i in range(2):
                                            await_done(pool, b, "gate", u, k, i)
                                    await_full(pool, b, "oT", 1 - u, NP - 1, before=1 - u)
                                else:
                                    await_full(pool, b, "oT", u, p - 1)
                                pool.tensor_tensor(og_g[:, :, :], o_g[:, :, :], gate[:, :, p * P:(p + 1) * P],
                                                   ALU.mult).then_inc(og_ready, 1)
                            pool.wait_ge(var_ready, b * NG * 2 + (2 * u + 2))
                            pool.tensor_tensor(rstd[:, :], vareps[:, :], minus_half[:, 0:GT], ALU.pow
                                               ).then_inc(rstd_ready, 1)
                            pool.tensor_copy(x_all[:, b, u * GT:(u + 1) * GT, :], x1_g[:, :, :])
                            pool.wait_ge(xn_ready, b * NG * 2 + (2 * u + 2))
                            pool.tensor_copy(xn2_all[:, b, u * GT:(u + 1) * GT, :], xn2_g[:, :, :])
                            await_done(pool, b, "x2f", u)
                            c0 = TAP - 1 + u * GW
                            pool.tensor_copy(xTf_all[:, b, c0:c0 + GW], x2f_g[:, :])
                            await_done(pool, b, "x2r", u)
                            c0 = TAP - 1 + (NG - 1 - u) * GW
                            pool.tensor_copy(xTr_all[:, b, c0:c0 + GW], x2r_g[:, :]).then_inc(pool_copied, 1)

                    with pool.Fori(0, B) as b:
                        layer(b)

                STEPS = 1 + NG * (2 * 3 + 8 + 2 * NP + 4 * NP + 1)

                @block.vector
                def _(dve):
                    n = [0]

                    def layer(b):
                        def step(ins):
                            ins.then_inc(dve0, 1)
                            n[0] += 1
                            return n[0]

                        def after(count):
                            dve.wait_ge(dve0, b * STEPS + count)

                        def normalised(u, which, src, dst, half):
                            for k in range(GT):
                                m = dve.bn_stats(stats[:, k, :], src(k))
                            after(step(m))
                            mean_and_variance(dve, stats, mean, part, vareps, 1e-5, lambda m: after(step(m))
                                              ).then_inc(var_ready, 1)
                            dve.wait_ge(rstd_ready, b * NG * 2 + (2 * u + 1 + half))
                            for k in range(GT):
                                m = dve.tensor_scalar(dst[:, k, :], src(k), mean[:, k:k + 1], rstd[:, k:k + 1],
                                                      ALU.subtract, ALU.mult)
                            m.then_inc(xn_ready, 1)

                        kvc_zero = step(dve.memset(kvc[:, :, :, :], 0.0))
                        for u in range(NG):
                            normalised(u, "x", lambda k: x_all[:, b, u * GT + k, :], xn_g, 0)
                            await_full(dve, b, "router", u)
                            dve.wait_ge(w_router, 48)
                            lg = psum("router", u)[:, 0:GT * E0].rearrange("t (k e) -> t k e", k=GT)
                            s = step(dve.tensor_tensor(logit[:, :, :], lg, bg_b[:, :].unsqueeze(1).broadcast_to([P, GT, E0]), ALU.add))
                            after(s)
                            taken(dve.tensor_tensor(logit[:, :, :], logit[:, :, :],
                                                    bias_b[:, :].unsqueeze(1).broadcast_to([P, GT, E0]), ALU.add),
                                  "router", u)
                            dve.wait_ge(sexp_ready, b * NG + (u + 1))
                            after(step(dve.tensor_scalar(sexp[:, :, :], sexp[:, :, :], 1.0, None, ALU.add)))
                            after(step(dve.reciprocal(score[:, :, :], sexp[:, :, :])))
                            sj = score[:, :, :].unsqueeze(2).broadcast_to([P, GT, E0, E0])
                            se = score[:, :, :].unsqueeze(3).broadcast_to([P, GT, E0, E0])
                            s = step(dve.tensor_tensor(gt3[:, :, :, :], sj, se, ALU.is_gt))
                            after(step(dve.tensor_tensor(eq3[:, :, :, :], sj, se, ALU.is_equal)))
                            bf = before[:, :, :].rearrange("p e j -> p (e j)").unsqueeze(1).broadcast_to([P, GT, E0 * E0])
                            after(step(dve.tensor_tensor(eq3[:, :, :, :].rearrange("p k e j -> p k (e j)"),
                                                         eq3[:, :, :, :].rearrange("p k e j -> p k (e j)"), bf, ALU.mult)))
                            after(step(dve.tensor_tensor(gt3[:, :, :, :], gt3[:, :, :, :], eq3[:, :, :, :], ALU.add)))
                            after(step(dve.tensor_reduce(rank[:, :, :], gt3[:, :, :, :], AX.X, ALU.add)))
                            dve.scalar_tensor_tensor(out=w9[:, :, 0:E0], in0=rank[:, :, :], scalar=2.0,
                                                     in1=score[:, :, :], op0=ALU.is_lt, op1=ALU.mult
                                                     ).then_inc(w9_ready, 1)
                            for j in range(2 * NP):
                                dve.wait_ge(exp_ready, b * NG * 2 * NP + (u * 2 * NP + j + 1))
                                after(step(dve.tensor_scalar(ebuf[:, j % 2, :], ebuf[:, j % 2, :], 1.0, None, ALU.min)))
                                dst = (qT, kT)[j % 2]
                                taken(dve.scalar_tensor_tensor(out=dst[:, j // 2, :], in0=psum("qk", u, j)[:, :],
                                                               scalar=1.0, in1=ebuf[:, j % 2, :],
                                                               op0=ALU.add, op1=ALU.max), "qk", u, j)

                            def ffn_add(e):
                                if e == 0:
                                    await_done(dve, b, "bias2", u)
                                    dve.wait_ge(w9_ready, b * NG + (u + 1))
                                else:
                                    await_done(dve, b, "ffn", u, e - 1)
                                await_full(dve, b, "ffn", u, e)
                                for k in range(GT):
                                    m = dve.scalar_tensor_tensor(out=facc[:, k, :], in0=psum("ffn", u, e)[:, k * P:(k + 1) * P],
                                                                 scalar=w9[:, k, e:e + 1], in1=facc[:, k, :],
                                                                 op0=ALU.mult, op1=ALU.add)
                                taken(m, "ffn", u, e)

                            def add_state(p, k, dst, src):
                                i, kk = k // 2, k % 2
                                for hh in range(2):
                                    r = slice(MW * hh, MW * hh + HD)
                                    c0 = (2 * kk + hh) * HA
                                    m = dve.tensor_tensor(dst[r, hh, :], psum("kv", u, p, i)[r, c0:c0 + HA], src[r, hh, :],
                                                          ALU.add)
                                return m

                            if u == 0:
                                after(kvc_zero)
                            for p in range(NP):
                                for hh in range(2):
                                    await_full(dve, b, "score", u, p, hh)
                                    taken(dve.tensor_tensor(sm[:, hh, :, :],
                                                            psum("score", u, p, hh)[:, :].rearrange("s (k t) -> s k t", k=GT),
                                                            causal[:, :].unsqueeze(1).broadcast_to([P, GT, P]), ALU.mult),
                                          "score", u, p, hh)
                                await_full(dve, b, "kv", u, p, 0)
                                carry = kvc[:, p, :, :]
                                s = step(add_state(p, 0, kvw[:, 0, :, :], carry))
                                after(s)
                                m = add_state(p, 1, kvw[:, 1, :, :], kvw[:, 0, :, :])
                                taken(m, "kv", u, p, 0)
                                await_done(dve, b, "kv", u, p, 0)
                                await_full(dve, b, "kv", u, p, 1)
                                add_state(p, 2, kvw[:, 2, :, :], kvw[:, 1, :, :]).then_inc(kv_ready, 1)
                                for i in range(2):
                                    await_full(dve, b, "o", u, p, i)
                                    den = psum("o", u, p, i)[:, 0:4 * HA].rearrange("t (c i) -> t c i", i=HA)[:, :, HD]
                                    s = step(dve.tensor_scalar(rden[:, 2 * i:2 * i + 2, :].rearrange("t k h -> t (k h)"), den,
                                                               1e-6, None, ALU.add))
                                after(s)
                                after(step(dve.reciprocal(rden[:, :, :], rden[:, :, :])))
                                dve.wait_ge(og_ready, b * pairs_ready + (u * NP + p) + START)
                                for i in range(2):
                                    src = psum("o", u, p, i)[:, 0:4 * HA].rearrange("t (c i) -> t c i", i=HA)[:, :, 0:HD]
                                    m = dve.tensor_tensor(
                                        o_g[:, 2 * i:2 * i + 2, :].rearrange("t k (h i) -> t (k h) i", h=2), src,
                                        rden[:, 2 * i:2 * i + 2, :].rearrange("t k h -> t (k h)").unsqueeze(2).broadcast_to([P, 4, HD]),
                                        ALU.mult)
                                    taken(m, "o", u, p, i)
                                await_done(dve, b, "o", u, p, 0)
                                await_done(dve, b, "o", u, p, 1)
                                dve.wait_ge(kv_ready, b * pairs_ready + (u * NP + p + 1))
                                s = add_state(p, 3, kvc[:, p, :, :], kvw[:, 2, :, :])
                                taken(s, "kv", u, p, 1)
                                ffn_add(p)
                            ffn_add(E0)
                            await_done(dve, b, "ffn", u, E0)
                            dve.wait_ge(th_ready, b * NG + (u + 1))
                            dve.wait_ge(og_ready, b * pairs_ready + (u + 1) * NP + START)
                            after(step(dve.scalar_tensor_tensor(out=sg[:, :, :], in0=th[:, :, :], scalar=1.0, in1=facc[:, :, :],
                                                                op0=ALU.add, op1=ALU.mult)))
                            await_full(dve, b, "attn", u)
                            taken(dve.tensor_tensor(sg[:, :, :], psum("attn", u)[:, :].rearrange("t (k d) -> t k d", k=GT),
                                                    sg[:, :, :], ALU.mult), "attn", u)
                            await_done(dve, b, "attn", u)
                            dve.wait_ge(pool_copied, b * NG + u + START)
                            dve.scalar_tensor_tensor(out=x1_g[:, :, :], in0=sg[:, :, :], scalar=0.5,
                                                     in1=x_all[:, b, u * GT:(u + 1) * GT, :],
                                                     op0=ALU.mult, op1=ALU.add).then_inc(x1_ready, 1)
                            dve.wait_ge(x1_ready, b * NG + (u + 1) + START)
                            normalised(u, "x1", lambda k: x1_g[:, k, :], xn2_g, 1)
                            await_full(dve, b, "dt", u)
                            dt = psum("dt", u)
                            dve.tensor_copy(dtf_all[:, b, u * GT:(u + 1) * GT, :], dt[:, 0:32].rearrange("t (k c) -> t k c", k=GT))
                            ur = NG - 1 - u
                            taken(dve.tensor_copy(dtr_all[:, b, ur * GT:(ur + 1) * GT, :],
                                                  dt[:, 32:48].rearrange("t (k c) -> t k c", k=GT)), "dt", u)

                    dve.memset(kvw[:, :, :, :], 0.0)
                    dve.memset(v1[:, :, :, HD:HA], 1.0)
                    dve.memset(w9[:, :, E0:E0 + 1], 1.0)
                    dve.wait_ge(w_x, 16 * B * NG)
                    with dve.Fori(0, B) as b:
                        layer(b)
                    assert n[0] == STEPS, n[0]

        with ExitStack() as l1:
            def s1(name, *shape):
                return sb(name, *shape, stack=l1)

            inw = s1("inw", P, 2, 3 * P)
            zw = s1("zw", P, 2, DI)
            convw = s1("convw", P, 2, 3, TAP)
            convb = s1("convb", P, 2, 3)
            dtb = s1("dtb", P, 2, MH)
            alog = s1("alog", P, 2, MH)
            dskip = s1("dskip", P, 2, MH)
            outw = s1("outw", P, 2, 2, D)
            normw = s1("normw", P, 2, 2)
            e1w1 = s1("e1w1", P, E1, 512)
            e1b1 = s1("e1b1", E1, 512)
            e1wo = s1("e1wo", P, HT, D)
            bo_b = s1("bo_b", P, D)
            gamma_b = s1("gamma_b", P, D)
            beta_b = s1("beta_b", P, D)

            yT_all = s1("yT_all", P, 2, 2, B, T)
            z_dt = s1("z_dt", P, 2, B, NT, MH)
            u_dt = s1("u_dt", P, 2, B, NT, MH)
            w_dt = s1("w_dt", P, 2, B, NT, MH)
            r_dt = s1("r_dt", P, 2, B, NT, MH)
            l_dt = s1("l_dt", P, 2, B, NT, MH)
            dt_all = s1("dt_all", P, 2, B, NT, MH)
            dA_all = s1("dA_all", P, 2, B, NT, MH)
            dAz_all = s1("dAz_all", P, 2, B, NT, MH)
            expA = s1("expA", P, 2, MH)
            dskip2 = s1("dskip2", P, 2, B, MH)
            oh_all = s1("oh_all", P, B, NT, E1)
            rgt = s1("rgt", P, B * NT, E1, E1)
            req = s1("req", P, B * NT, E1, E1)
            rrank = s1("rrank", P, B * NT, E1)

            xc = s1("xc", P, 2, B, CW)
            dt_c = s1("dt_c", P, 2, B, MH)
            dA_c = s1("dA_c", P, 2, B, MH)
            dAz_c = s1("dAz_c", P, 2, B, MH)
            cv = s1("cv", P, 2, 3, B, P)
            xs = s1("xs", P, 2, 2, B, P)
            BT = s1("BT", MN, 2, B, P)
            CT = s1("CT", MN, 2, B, P)
            zs = s1("zs", P, 2, B, DI)
            xtok = s1("xtok", P, 2, B, DI)
            Btok = s1("Btok", P, 2, B, MN)
            Lm = s1("Lm", P, 2, B, MH, P)
            Mm = s1("Mm", P, 2, B, MH, P)
            xdt = s1("xdt", P, 2, B, DI)
            xE = s1("xE", P, 2, B, DI)
            xD = s1("xD", P, 2, B, DI)
            Pc = s1("Pc", P, 2, B, MH)
            prow = s1("prow", 1, 2, B, MH)
            Pend = s1("Pend", MN, 2, B, MH)
            S = s1("S", MN, 2, B, DI)
            S2 = s1("S2", MN, 2, B, DI)
            yt = s1("yt", P, 2, B, DI)
            yg = s1("yg", P, 2, B, DI)
            ysq = s1("ysq", P, 2, B, DI)
            yn = s1("yn", P, 2, B, DI)
            ss = s1("ss", P, 2, B)
            ms = s1("ms", P, 2, B)
            rs = s1("rs", P, 2, B)

            oh_g = s1("oh_g", P, GT, E1)
            ohT = s1("ohT", E1, GW)
            xm = s1("xm", P, E1, GW)
            h1T = s1("h1T", P, HT, GW)
            sT = s1("sT", P, GW)
            y_g = s1("y_g", P, GT, D)
            yh_g = s1("yh_g", P, GT, D)
            th1 = s1("th1", P, GT, D)
            sg1 = s1("sg1", P, GT, D)
            out_g = s1("out_g", P, NG, GT, D)
            stats1 = s1("stats1", P, GT, 6)
            mean1 = s1("mean1", P, GT)
            part1 = s1("part1", P, 2, GT)
            ve1 = s1("ve1", P, GT)
            rstd1 = s1("rstd1", P, GT)

            (w_mamba, w_small, w_last, u_ready, u_made, ln_ready, a_ready, dA_ready, dve1, dve2, dve3) = (sem(n) for n in (
                "mamba_w_loaded", "small_w_loaded", "last_w_loaded", "u_ready", "u_made", "ln_ready", "a_ready", "dA_ready",
                "dve1", "dve2", "dve3"))
            (alog_ready, expA_ready, setup_ready, chunk_ready, tap0_ready, bc_ready, xdt_ready, prow_ready, S2_ready,
             ss_ready, rs_ready) = (sem(n) for n in (
                "alog_ready", "expA_ready", "setup_ready", "chunk_ready", "tap0_ready", "bc_ready", "xdt_ready",
                "prow_ready", "S2_ready", "ss_ready", "rs_ready"))
            (oh_ready, ve1_ready, rstd1_ready, g_ready, th1_ready, out_ready) = (sem(n) for n in (
                "oh_ready", "ve1_ready", "rstd1_ready", "g_ready", "th1_ready", "out_ready"))

            full1, done1, opened1, psum1, filled1, taken1 = awaiting(L1)
            full2, done2, opened2, psum2, filled2, taken2 = awaiting(L2)
            heads = lambda ap: ap.rearrange("p b (h i) -> p (b h) i", i=HD)
            per_head = lambda ap: ap.rearrange("p b h -> p (b h)").unsqueeze(2).broadcast_to([ap.shape[0], B * MH, HD])

            with nc.Block() as block:
                @block.sync
                def _(sp):
                    for dst, src in ((inw[:, :, :], "inw"), (convw[:, :, :, :], "convw"), (convb[:, :, :], "convb"),
                                     (zw[:, :, :], "zw"), (outw[:, :, :, :], "outw"), (normw[:, :, :], "normw")):
                        sp.dma_start(dst, a[src]).then_inc(w_mamba, 16)
                    for dst, src in ((dtb, "dt_bias"), (alog, "A_log"), (dskip, "Dp")):
                        sp.dma_start(dst[:, :, :], a[src].partition_broadcast(P)).then_inc(w_small, 16)
                    for dst, src in ((e1w1[:, :, :], "e1w1"), (e1b1[:, :], "e1b1"), (e1wo[:, :, :], "e1wo")):
                        sp.dma_start(dst, a[src]).then_inc(w_last, 16)
                    for dst, src in ((bo_b, "bo"), (gamma_b, "gamma"), (beta_b, "beta")):
                        sp.dma_start(dst[:, :], a[src].partition_broadcast(P)).then_inc(w_last, 16)
                    with sp.Fori(0, B) as b:
                        for u in range(NG):
                            sp.wait_ge(out_ready, b * NG + (u + 1))
                            sp.dma_start(out[bass.ds(b, 1), u * GW:(u + 1) * GW, :].rearrange("o (k p) d -> p (o k) d", p=P),
                                         out_g[:, u, :, :]).then_inc(out_stored[u], 16)
                    for u in range(NG):
                        sp.wait_ge(out_stored[u], 16 * B + 16)

                @block.tensor
                def _(pe):
                    def chunk(c):
                        pe.wait_ge(chunk_ready, c + 1)
                        for d in range(2):
                            for b in range(B):
                                o = opened1(pe, c, "L", d, b)
                                for h in range(MH):
                                    m = pe.transpose(o[:, h * P:(h + 1) * P],
                                                     dAz_c[:, d, b, h:h + 1].broadcast_to([P, P]), ident[:, :])
                                filled1(m, "L", d, b)
                        for d in range(2):
                            for i in range(3):
                                o = opened1(pe, c, "conv", d, i)
                                filled1(pe.matmul(o[:, 0:B * CW], inw[:, d, i * P:(i + 1) * P],
                                                  xc[:, d, :, :].rearrange("p b t -> p (b t)"), start=True, stop=True),
                                        "conv", d, i)
                        for d in range(2):
                            o = opened1(pe, c, "z", d)
                            for b in range(B):
                                m = pe.matmul(o[:, b * DI:(b + 1) * DI], xc[:, d, b, TAP - 1:CW], zw[:, d, :],
                                              start=True, stop=True)
                            filled1(m, "z", d)
                        for d in range(2):
                            o = opened1(pe, c, "P", d)
                            pe.wait_ge(prow_ready, 2 * c + (d + 1))
                            for b in range(B):
                                for h in range(MH):
                                    pe.matmul(o[:, b * MH + h:b * MH + h + 1], Lm[0:1, d, b, h, :], dA_c[0:1, d, b, h:h + 1],
                                              start=True, stop=True)
                            filled1(pe.matmul(o[0:MN, 8:16], ones[0:1, 0:MN], prow[0:1, d, :, :].rearrange("p b h -> p (b h)"),
                                              start=True, stop=True), "P", d)
                        for d in range(2):
                            pe.wait_ge(bc_ready, 2 * c + (d + 1))
                            for b in range(B):
                                o = opened1(pe, c, "tr", d, b)
                                for i in range(2):
                                    pe.transpose(o[:, i * P:(i + 1) * P], xs[:, d, i, b, :], ident[:, :])
                                filled1(pe.transpose(o[:, DI:DI + MN], BT[:, d, b, :], ident[0:MN, 0:MN]), "tr", d, b)
                        for d in range(2):
                            o = opened1(pe, c, "G", d)
                            for b in range(B):
                                m = pe.matmul(o[:, b * P:(b + 1) * P], BT[:, d, b, :], CT[:, d, b, :],
                                              start=True, stop=True)
                            filled1(m, "G", d)
                        for d in range(2):
                            pe.wait_ge(xdt_ready, 2 * c + (d + 1))
                            done1(pe, c, "G", d)
                            if d == 0:
                                pe.wait_ge(setup_ready, 1)
                            done1(pe, c, "S", d, before=1)
                            for b in range(B):
                                o = opened1(pe, c, "y", d, b)
                                for h in range(MH):
                                    pe.matmul(o[:, h * HD:(h + 1) * HD], Mm[:, d, b, h, :], xdt[:, d, b, h * HD:(h + 1) * HD],
                                              start=True, stop=True)
                                filled1(pe.matmul(o[:, DI:2 * DI], CT[:, d, b, :], S[:, d, b, :], start=True, stop=True),
                                        "y", d, b)
                            o = opened1(pe, c, "S", d)
                            pe.wait_ge(xE_ready, 2 * c + (d + 1) + START)
                            for b in range(B):
                                done1(pe, c, "tr", d, b)
                                m = pe.matmul(o[0:MN, b * DI:(b + 1) * DI], Btok[:, d, b, :], xE[:, d, b, :],
                                              start=True, stop=True)
                            filled1(m, "S", d)
                        for d in range(2):
                            o = opened1(pe, c, "yT", d)
                            pe.wait_ge(yn_ready, 2 * c + (d + 1) + START)
                            for i in range(2):
                                for b in range(B):
                                    m = pe.transpose(o[:, (i * B + b) * P:(i * B + b + 1) * P], yn[:, d, b, i * P:(i + 1) * P],
                                                     (ident, flip)[d][:, :])
                            filled1(m, "yT", d)

                    def last(b):
                        for u in range(NG):
                            pe.wait_ge(oh_ready, b * NG + (u + 1))
                            o = opened2(pe, b, "ohT", u)
                            for k in range(GT):
                                m = pe.transpose(o[0:E1, k * P:(k + 1) * P], oh_g[:, k, :], ident[:, :])
                            filled2(m, "ohT", u)
                            for e in range(E1):
                                o = opened2(pe, b, "mask", u, e)
                                for k in range(GT):
                                    m = pe.transpose(o[:, k * P:(k + 1) * P], oh_g[:, k, e:e + 1].broadcast_to([P, P]),
                                                     ident[:, :])
                                filled2(m, "mask", u, e)
                            o = opened2(pe, b, "sT", u)
                            for d in range(2):
                                for i in range(2):
                                    m = pe.matmul(o[:, :], outw[:, d, i, :],
                                                  yT_all[:, d, i, bass.ds(b, 1), u * GW:(u + 1) * GW].rearrange("p o t -> p (o t)"),
                                                  start=(d + i == 0), stop=(d + i == 2))
                            filled2(m, "sT", u)
                            done2(pe, b, "ohT", u)
                            for e in range(E1):
                                done2(pe, b, "mask", u, e)
                            pe.wait_ge(w_last, 96)
                            for i in range(HT):
                                o = opened2(pe, b, "h", u, i)
                                for e in range(E1):
                                    pe.matmul(o[:, :], e1w1[:, e, i * P:(i + 1) * P], xm[:, e, :], start=(e == 0), stop=False)
                                filled2(pe.matmul(o[:, :], e1b1[:, i * P:(i + 1) * P], ohT[:, :], start=False, stop=True),
                                        "h", u, i)
                            o = opened2(pe, b, "s", u)
                            done2(pe, b, "sT", u)
                            for k in range(GT):
                                m = pe.transpose(o[:, k * P:(k + 1) * P], sT[:, k * P:(k + 1) * P], ident[:, :])
                            filled2(m, "s", u)
                            o = opened2(pe, b, "ffn", u)
                            for i in range(HT):
                                done2(pe, b, "h", u, i)
                            for k in range(GT):
                                for i in range(HT):
                                    m = pe.matmul(o[:, k * P:(k + 1) * P], h1T[:, i, k * P:(k + 1) * P], e1wo[:, i, :],
                                                  start=(i == 0), stop=(i == HT - 1))
                            filled2(m, "ffn", u)

                    pe.wait_ge(w_mamba, 96)
                    with pe.Fori(0, NT) as c:
                        chunk(c)
                    for d in range(2):
                        done1(pe, NT - 1, "yT", d)
                    with pe.Fori(0, B) as b:
                        last(b)

                @block.scalar
                def _(act):
                    act.wait_ge(alog_ready, 1)
                    act.activation(expA[:, :, :], alog[:, :, :], ACT.Exp).then_inc(expA_ready, 1)
                    act.wait_ge(u_ready, 1)
                    act.activation(u_dt[:, :, :, :, :], u_dt[:, :, :, :, :], ACT.Exp).then_inc(u_made, 1)
                    act.wait_ge(ln_ready, 1)
                    act.activation(l_dt[:, :, :, :, :], w_dt[:, :, :, :, :], ACT.Ln).then_inc(u_made, 1)
                    act.wait_ge(a_ready, 1)
                    act.activation(dA_all[:, :, :, :, :], r_dt[:, :, :, :, :], ACT.Exp).then_inc(dA_ready, 1)
                    act.wait_ge(w_mamba, 96)

                    def chunk(c):
                        for d in range(2):
                            for i in range(3):
                                full1(act, c, "conv", d, i)
                                act.activation(cv[:, d, i, :, :], psum1("conv", d, i)[:, 0:B * CW].rearrange(
                                    "p (b t) -> p b t", b=B)[:, :, 0:P], ACT.Identity, bias=convb[:, d, i:i + 1],
                                    scale=convw[:, d, i, 0:1]).then_inc(tap0_ready, 1)
                        for d in range(2):
                            full1(act, c, "z", d)
                            act.wait_ge(yg_ready, 2 * c + START)
                            taken1(act.activation(zs[:, d, :, :].rearrange("p b i -> p (b i)"), psum1("z", d)[:, :], ACT.Silu),
                                   "z", d)
                        for d in range(2):
                            done1(act, c, "conv", d, 2)
                            done1(act, c, "conv", d, 1)
                            done1(act, c, "conv", d, 0)
                            act.activation(xs[:, d, :, :, :], cv[:, d, 0:2, :, :], ACT.Silu)
                            act.activation(BT[:, d, :, :], cv[0:MN, d, 2, :, :], ACT.Silu)
                            act.activation(CT[:, d, :, :], cv[MN:2 * MN, d, 2, :, :], ACT.Silu).then_inc(bc_ready, 1)
                        for d in range(2):
                            full1(act, c, "P", d)
                            act.activation(Pc[:, d, :, :].rearrange("p b h -> p (b h)"), psum1("P", d)[:, 0:8], ACT.Copy)
                            taken1(act.activation(Pend[:, d, :, :].rearrange("p b h -> p (b h)"), psum1("P", d)[0:MN, 8:16],
                                                  ACT.Copy), "P", d)
                        for d in range(2):
                            act.wait_ge(xD_ready, 2 * c + START)
                            for b in range(B):
                                full1(act, c, "tr", d, b)
                                act.activation(xtok[:, d, b, :], psum1("tr", d, b)[:, 0:DI], ACT.Copy)
                                taken1(act.activation(Btok[:, d, b, :], psum1("tr", d, b)[:, DI:DI + MN], ACT.Copy),
                                       "tr", d, b)
                        for d in range(2):
                            act.wait_ge(yg_ready, 2 * c + (d + 1) + START)
                            for b in range(B):
                                m = act.activation(ysq[:, d, b, :], yg[:, d, b, :], ACT.Square, accum_out=ss[:, d, b:b + 1])
                            m.then_inc(ss_ready, 1)
                            act.wait_ge(rs_ready, 2 * c + (d + 1))
                            for b in range(B):
                                m = act.activation(yn[:, d, b, :], yg[:, d, b, :], ACT.Copy, scale=rs[:, d, b:b + 1])
                            m.then_inc(yn_ready, 1)
                        for d in range(2):
                            full1(act, c, "yT", d)
                            tile = c if d == 0 else (NT - 1) - c
                            dst = yT_all[:, d, :, :, :].rearrange("p i b (n t) -> p (i b) n t", t=P)[:, :, bass.ds(tile, 1), :]
                            taken1(act.activation(dst.rearrange("p q o t -> p q (o t)"),
                                                  psum1("yT", d)[:, :].rearrange("p (q t) -> p q t", q=4), ACT.Copy), "yT", d)

                    with act.Fori(0, NT) as c:
                        chunk(c)

                    def last(b):
                        for u in range(NG):
                            full2(act, b, "ohT", u)
                            taken2(act.activation(ohT[:, :], psum2("ohT", u)[0:E1, :], ACT.Copy), "ohT", u)
                            full2(act, b, "sT", u)
                            taken2(act.activation(sT[:, :], psum2("sT", u)[:, :], ACT.Copy), "sT", u)
                            for i in range(HT):
                                full2(act, b, "h", u, i)
                                taken2(act.activation(h1T[:, i, :], psum2("h", u, i)[:, :], ACT.Gelu), "h", u, i)
                            act.wait_ge(g_ready, b * NG + (u + 1))
                            act.activation(th1[:, :, :], yh_g[:, :, :], ACT.Tanh, scale=0.5).then_inc(th1_ready, 1)

                    with act.Fori(0, B) as b:
                        last(b)

                @block.gpsimd
                def _(pool):
                    pool.wait_ge(setup_ready, 1)

                    def chunk(c):
                        done1(pool, c, "P", 0, before=1)
                        done1(pool, c, "P", 1, before=1)
                        done1(pool, c, "z", 0, before=1)
                        done1(pool, c, "z", 1, before=1)
                        full1(pool, c, "L", 1, 1, before=1)
                        for d, src in enumerate((xTf_all, xTr_all)):
                            pool.tensor_copy(xc[:, d, :, :], src[:, :, bass.ds(c * P, CW)])
                        for dst, src in ((dt_c, dt_all), (dA_c, dA_all), (dAz_c, dAz_all)):
                            m = pool.tensor_copy(dst[:, :, :, :].rearrange("p d b h -> p (d b) h"),
                                                 src[:, :, :, bass.ds(c, 1), :].rearrange("p d b o h -> p (d b) (o h)"))
                        m.then_inc(chunk_ready, 1)
                        pool.wait_ge(chunk_ready, c + 1)
                        for d in range(2):
                            for b in range(B):
                                done1(pool, c, "tr", d, b)
                            full1(pool, c, "S", d, before=1)
                            pool.tensor_tensor(heads(xdt[:, d, :, :]), heads(xtok[:, d, :, :]), per_head(dt_c[:, d, :, :]),
                                               ALU.mult).then_inc(xdt_ready, 1)
                            pool.wait_ge(xdt_ready, 2 * c + (d + 1))
                            for b in range(B):
                                done1(pool, c, "L", d, b)
                            end = Lm[:, d, :, :, P - 1].rearrange("p b h -> p (b h)").unsqueeze(2).broadcast_to([P, B * MH, HD])
                            pool.tensor_tensor(heads(xE[:, d, :, :]), heads(xdt[:, d, :, :]), end, ALU.mult
                                               ).then_inc(xE_ready, 1)
                            pool.tensor_tensor(heads(xD[:, d, :, :]), heads(xtok[:, d, :, :]), per_head(dskip2[:, d, :, :]),
                                               ALU.mult).then_inc(xD_ready, 1)
                        for d in range(2):
                            done1(pool, c, "P", d)
                            full1(pool, c, "y", d, B - 1)
                            pool.tensor_tensor(heads(S2[:, d, :, :]), heads(S[:, d, :, :]), per_head(Pend[:, d, :, :]), ALU.mult
                                               ).then_inc(S2_ready, 1)
                            for b in range(B):
                                done1(pool, c, "y", d, b)
                            pool.wait_ge(xD_ready, 2 * c + 2 + START)
                            pool.wait_ge(yn_ready, 2 * c + d + START)
                            pool.tensor_tensor(yg[:, d, :, :], yt[:, d, :, :], xD[:, d, :, :], ALU.add).then_inc(pool1, 1)
                            pool.wait_ge(pool1, 4 * c + (2 * d + 1) + START)
                            done1(pool, c, "z", d)
                            pool.tensor_tensor(yg[:, d, :, :], yg[:, d, :, :], zs[:, d, :, :], ALU.mult).then_inc(yg_ready, 1)
                            pool.wait_ge(setup_ready, 1)
                            pool.wait_ge(ss_ready, 2 * c + (d + 1))
                            pool.tensor_scalar(ms[:, d, :], ss[:, d, :], 1.0 / DI, 1e-5, ALU.mult, ALU.add).then_inc(pool1, 1)
                            pool.wait_ge(pool1, 4 * c + (2 * d + 2) + START)
                            pool.tensor_tensor(rs[:, d, :], ms[:, d, :], minus_half[:, 0:B], ALU.pow).then_inc(rs_ready, 1)

                    with pool.Fori(0, NT) as c:
                        chunk(c)

                    def last(b):
                        for u in range(NG):
                            full2(pool, b, "mask", 1 - u, E1 - 1, before=1 - u)
                            pool.tensor_copy(oh_g[:, :, :], oh_all[:, b, u * GT:(u + 1) * GT, :]).then_inc(oh_ready, 1)
                            pool.wait_ge(ve1_ready, b * NG + (u + 1))
                            pool.tensor_tensor(rstd1[:, :], ve1[:, :], minus_half[:, 0:GT], ALU.pow).then_inc(rstd1_ready, 1)

                    with pool.Fori(0, B) as b:
                        last(b)

                @block.vector
                def _(dve):
                    n = [0]

                    def step(ins, chain):
                        ins.then_inc(chain, 1)
                        n[0] += 1
                        return n[0]

                    def setup():
                        def then(ins):
                            dve.wait_ge(dve1, step(ins, dve1))

                        dve.memset(S[:, :, :, :], 0.0)
                        dve.wait_ge(w_small, 48)
                        dve.tensor_scalar(alog[:, :, :], alog[:, :, :], 88.7, None, ALU.min).then_inc(alog_ready, 1)
                        for d, src in enumerate((dtf_all[:, :, :, 0:MH], dtr_all[:, :, :, :])):
                            bias = dtb[:, d, :].unsqueeze(1).broadcast_to([P, B * NT, MH])
                            m = dve.tensor_tensor(z_dt[:, d, :, :, :].rearrange("p b n h -> p (b n) h"),
                                                  src.rearrange("p b n h -> p (b n) h"), bias, ALU.add)
                        for b in range(B):
                            dve.tensor_copy(dskip2[:, :, b, :], dskip[:, :, :])
                        then(m)
                        f = lambda t: t[:, :, :, :, :].rearrange("p d b n h -> p (d b n h)")
                        dve.scalar_tensor_tensor(out=f(u_dt), in0=f(z_dt), scalar=-1.0, in1=f(z_dt),
                                                 op0=ALU.mult, op1=ALU.min).then_inc(u_ready, 1)
                        dve.wait_ge(u_made, 1)
                        then(dve.tensor_scalar(f(w_dt), f(u_dt), 1.0, None, ALU.add))
                        then(dve.scalar_tensor_tensor(out=f(r_dt), in0=f(w_dt), scalar=-1.0, in1=f(u_dt),
                                                      op0=ALU.add, op1=ALU.subtract))
                        then(dve.reciprocal(f(dt_all), f(w_dt)))
                        then(dve.tensor_tensor(f(r_dt), f(r_dt), f(dt_all), ALU.mult))
                        dve.tensor_scalar(f(z_dt), f(z_dt), 0.0, None, ALU.max).then_inc(ln_ready, 1)
                        dve.wait_ge(ln_ready, 1)
                        then(dve.tensor_tensor(f(z_dt), f(z_dt), f(r_dt), ALU.subtract))
                        dve.wait_ge(u_made, 2)
                        then(dve.tensor_tensor(f(dt_all), f(z_dt), f(l_dt), ALU.add))
                        dve.wait_ge(expA_ready, 1)
                        for d in range(2):
                            m = dve.scalar_tensor_tensor(out=r_dt[:, d, :, :, :].rearrange("p b n h -> p (b n) h"),
                                                         in0=dt_all[:, d, :, :, :].rearrange("p b n h -> p (b n) h"), scalar=1.0 / HUGE,
                                                         in1=expA[:, d, :].unsqueeze(1).broadcast_to([P, B * NT, MH]),
                                                         op0=ALU.mult, op1=ALU.mult)
                        then(m)
                        dve.tensor_scalar(f(r_dt), f(r_dt), 120.0 / HUGE, -HUGE, ALU.min, ALU.mult).then_inc(a_ready, 1)
                        lg = dtf_all[:, :, :, MH:2 * MH].rearrange("p b n e -> p (b n) e")
                        lj = lg.unsqueeze(2).broadcast_to([P, B * NT, E1, E1])
                        le = lg.unsqueeze(3).broadcast_to([P, B * NT, E1, E1])
                        dve.tensor_tensor(rgt[:, :, :, :], lj, le, ALU.is_gt)
                        then(dve.tensor_tensor(req[:, :, :, :], lj, le, ALU.is_equal))
                        bf = before[:, 0:E1, 0:E1].unsqueeze(1).broadcast_to([P, B * NT, E1, E1])
                        then(dve.tensor_tensor(req[:, :, :, :], req[:, :, :, :], bf, ALU.mult))
                        then(dve.tensor_tensor(rgt[:, :, :, :], rgt[:, :, :, :], req[:, :, :, :], ALU.add))
                        then(dve.tensor_reduce(rrank[:, :, :], rgt[:, :, :, :], AX.X, ALU.add))
                        then(dve.tensor_scalar(oh_all[:, :, :, :].rearrange("p b n e -> p (b n) e"), rrank[:, :, :], 1.0, None,
                                               ALU.is_lt))
                        dve.wait_ge(w_mamba, 96)
                        for d in range(2):
                            for i in range(2):
                                dve.tensor_scalar(outw[:, d, i, :], outw[:, d, i, :], normw[:, d, i:i + 1], None, ALU.mult)
                        dve.wait_ge(dA_ready, 1)
                        then(dve.tensor_copy(f(dAz_all), f(dA_all)))
                        dve.memset(dAz_all[0:1, :, :, :, :], 0.0).then_inc(setup_ready, 1)

                    setup()
                    n[0] = 0
                    CHUNK_STEPS = 2 * 3 * 2 + 2 * 2

                    def chunk(c):
                        def after(count):
                            dve.wait_ge(dve2, c * CHUNK_STEPS + count)

                        for d in range(2):
                            for b in range(B):
                                full1(dve, c, "L", d, b)
                                if b == 0:
                                    full1(dve, c, "P", d, before=1)
                                    dve.wait_ge(xE_ready, 2 * c + START)
                                m = dve.tensor_tensor_scan(Lm[:, d, b, :, :].rearrange("s h t -> s (h t)"),
                                                           psum1("L", d, b)[:, :], ident4[:, :, :].rearrange("s h t -> s (h t)"),
                                                           0.0, ALU.mult, ALU.add)
                                taken1(m, "L", d, b)
                            done1(dve, c, "L", d, 0)
                            done1(dve, c, "L", d, 1)
                            dve.tensor_tensor(prow[0:1, d, :, :], dA_c[0:1, d, :, :], Lm[0:1, d, :, :, P - 1], ALU.mult
                                              ).then_inc(prow_ready, 1)
                        for tap in range(1, TAP):
                            for d in range(2):
                                for i in range(3):
                                    if tap == 1:
                                        dve.wait_ge(tap0_ready, 6 * c + (3 * d + i + 1))
                                    else:
                                        after(6 * (tap - 2) + 3 * d + i + 1)
                                    src = psum1("conv", d, i)[:, 0:B * CW].rearrange("p (b t) -> p b t", b=B)[:, :, tap:tap + P]
                                    m = dve.scalar_tensor_tensor(out=cv[:, d, i, :, :], in0=src, scalar=convw[:, d, i, tap:tap + 1],
                                                                 in1=cv[:, d, i, :, :], op0=ALU.mult, op1=ALU.add)
                                    if tap < TAP - 1:
                                        step(m, dve2)
                                    else:
                                        taken1(m, "conv", d, i)
                        for d in range(2):
                            full1(dve, c, "G", d)
                            for b in range(B):
                                g = psum1("G", d)[:, b * P:(b + 1) * P].unsqueeze(1).broadcast_to([P, MH, P])
                                m = dve.tensor_tensor(Mm[:, d, b, :, :], g, Lm[:, d, b, :, :], ALU.mult)
                            taken1(m, "G", d)
                        for d in range(2):
                            done1(dve, c, "P", d)
                            dve.wait_ge(pool1, 4 * c + START)
                            for b in range(B):
                                full1(dve, c, "y", d, b)
                                y = psum1("y", d, b)
                                after(step(dve.tensor_tensor(yt[:, d, b, :].rearrange("p (h i) -> p h i", i=HD),
                                                             y[:, DI:2 * DI].rearrange("p (h i) -> p h i", i=HD),
                                                             Pc[:, d, b, :].unsqueeze(2).broadcast_to([P, MH, HD]), ALU.mult), dve2))
                                taken1(dve.tensor_tensor(yt[:, d, b, :], y[:, 0:DI], yt[:, d, b, :], ALU.add), "y", d, b)
                            full1(dve, c, "S", d)
                            dve.wait_ge(S2_ready, 2 * c + (d + 1))
                            taken1(dve.tensor_tensor(S[:, d, :, :].rearrange("p b i -> p (b i)"), psum1("S", d)[0:MN, :],
                                                     S2[:, d, :, :].rearrange("p b i -> p (b i)"), ALU.add), "S", d)

                    with dve.Fori(0, NT) as c:
                        chunk(c)
                    assert n[0] == CHUNK_STEPS, n[0]
                    n[0] = 0
                    LAST_STEPS = NG * 7

                    def last(b):
                        def then(ins):
                            dve.wait_ge(dve3, b * LAST_STEPS + step(ins, dve3))

                        rows = lambda w: w[:, :].unsqueeze(1).broadcast_to([P, GT, D])
                        dve.wait_ge(w_last, 96)
                        for u in range(NG):
                            for e in range(E1):
                                full2(dve, b, "mask", u, e)
                                taken2(dve.tensor_tensor(xm[:, e, :], psum2("mask", u, e)[:, :],
                                                         xTf_all[:, b, TAP - 1 + u * GW:TAP - 1 + (u + 1) * GW], ALU.mult),
                                       "mask", u, e)
                            full2(dve, b, "ffn", u)
                            taken2(dve.tensor_tensor(y_g[:, :, :], psum2("ffn", u)[:, :].rearrange("t (k d) -> t k d", k=GT),
                                                     rows(bo_b), ALU.add), "ffn", u)
                            done2(dve, b, "ffn", u)
                            then(dve.tensor_tensor(y_g[:, :, :], y_g[:, :, :], xn2_all[:, b, u * GT:(u + 1) * GT, :], ALU.add))
                            for k in range(GT):
                                m = dve.bn_stats(stats1[:, k, :], y_g[:, k, :])
                            then(m)
                            mean_and_variance(dve, stats1, mean1, part1, ve1, 1e-12, then).then_inc(ve1_ready, 1)
                            dve.wait_ge(rstd1_ready, b * NG + (u + 1))
                            for k in range(GT):
                                m = dve.tensor_scalar(yh_g[:, k, :], y_g[:, k, :], mean1[:, k:k + 1], rstd1[:, k:k + 1],
                                                      ALU.subtract, ALU.mult)
                            then(m)
                            then(dve.tensor_tensor(yh_g[:, :, :], yh_g[:, :, :], rows(gamma_b), ALU.mult))
                            dve.tensor_tensor(yh_g[:, :, :], yh_g[:, :, :], rows(beta_b), ALU.add).then_inc(g_ready, 1)
                            dve.wait_ge(th1_ready, b * NG + (u + 1))
                            then(dve.scalar_tensor_tensor(out=sg1[:, :, :], in0=th1[:, :, :], scalar=1.0, in1=yh_g[:, :, :],
                                                          op0=ALU.add, op1=ALU.mult))
                            full2(dve, b, "s", u)
                            taken2(dve.tensor_tensor(sg1[:, :, :], psum2("s", u)[:, :].rearrange("t (k d) -> t k d", k=GT),
                                                     sg1[:, :, :], ALU.mult), "s", u)
                            done2(dve, b, "s", u)
                            dve.wait_ge(out_stored[u], 16 * b + 16)
                            dve.scalar_tensor_tensor(out=out_g[:, u, :, :], in0=sg1[:, :, :], scalar=0.5,
                                                     in1=x_all[:, b, u * GT:(u + 1) * GT, :], op0=ALU.mult, op1=ALU.add
                                                     ).then_inc(out_ready, 1)

                    with dve.Fori(0, B) as b:
                        last(b)
                    assert n[0] == LAST_STEPS, n[0]




def layouts(i):
    import numpy as np

    c = np.ascontiguousarray
    both = lambda n: (i["L1_attn_f_" + n], i["L1_attn_b_" + n])
    xbc = slice(DI, 2 * DI + 2 * MN)
    iw = both("in_w")
    dt = slice(2 * DI + 2 * MN, None)
    return {
        "x": i["L0_attn_x"], "w_qkv": i["L0_attn_w_qkv"], "w_gate": i["L0_attn_w_gate"],
        "w_out": c(i["L0_attn_w_out"].reshape(NP, P, D).transpose(1, 0, 2)),
        "wg": c(i["L0_ffn_Wg"].T), "bg": i["L0_ffn_bg"], "bias": i["L0_ffn_bias"],
        "w1": c(i["L0_ffn_W1"].transpose(0, 2, 1)), "ws1": c(i["L0_ffn_Ws1"].T),
        "w2": c(i["L0_ffn_W2"].reshape(E0, D, HT, P).transpose(0, 3, 2, 1)),
        "ws2": c(i["L0_ffn_Ws2"].reshape(D, HT, P).transpose(2, 1, 0)),
        "b1": c(i["L0_ffn_b1"].reshape(E0, HT, P).transpose(2, 0, 1)),
        "bs1": c(i["L0_ffn_bs1"].reshape(HT, P).T), "b2": i["L0_ffn_b2"], "bs2": i["L0_ffn_bs2"].reshape(1, D),
        "inw": c(np.stack([w[xbc].T for w in iw], 1)),
        "zw": c(np.stack([w[0:DI].T for w in iw], 1)),
        "dtw": c(np.concatenate([iw[0][dt].T, i["L1_ffn_W_router"], iw[1][dt].T], 1)),
        "convw": c(np.stack([w.reshape(3, P, TAP).transpose(1, 0, 2) for w in both("conv_w")], 1)),
        "convb": c(np.stack([w.reshape(3, P).T for w in both("conv_b")], 1)),
        "dt_bias": c(np.stack(both("dt_bias"))), "A_log": c(np.stack(both("A_log"))), "Dp": c(np.stack(both("Dp"))),
        "outw": c(np.stack([w.T.reshape(2, P, D).transpose(1, 0, 2) for w in both("out_w")], 1)),
        "normw": c(np.stack([w.reshape(2, P).T for w in both("norm_w")], 1)),
        "e1w1": c(i["L1_ffn_W1"].transpose(1, 0, 2)), "e1b1": i["L1_ffn_b1"],
        "e1wo": c(i["L1_ffn_Wo"].reshape(HT, P, D).transpose(1, 0, 2)),
        "bo": i["L1_ffn_bo"], "gamma": i["L1_ffn_ln_gamma"], "beta": i["L1_ffn_ln_beta"],
    }


def kernel(**inputs):
    import numpy as np
    import concourse.bacc as bacc
    from concourse.bass_utils import run_bass_kernel_spmd

    nc = bacc.Bacc("TRN2", target_bir_lowering=False, num_devices=1)
    arrays = layouts({n: np.asarray(v) for n, v in inputs.items()})
    a = {n: nc.dram_tensor(f"in_{n}", v.shape, mybir.dt.from_np(v.dtype), kind="ExternalInput").ap()
         for n, v in arrays.items()}
    out = nc.dram_tensor("out_x", (B, T, D), F32, kind="ExternalOutput").ap()
    build(nc, a, out)
    r = run_bass_kernel_spmd(nc, [{f"in_{n}": v for n, v in arrays.items()}], core_ids=[0])
    return r.results[0]["out_x"]
```

```python
from contextlib import ExitStack

import concourse.bass as bass
from concourse import mybir

F32 = mybir.dt.float32
ALU = mybir.AluOpType
ACT = mybir.ActivationFunctionType
AX = mybir.AxisListType

P = 128
B, T, D = 2, 1024, 128
NT = T // P
GT = 4
GW = GT * P
NG = NT // GT
H, HD = 16, 64
NP = H // 2
E0, HT = 8, 4
HA = HD + 1
E1 = 4
MH, MN = 4, 64
DI = MH * 64
ROOT_DI = DI ** -0.5
TAP = 4
CW = P + TAP - 1
NB = 8
HUGE = 2.0 ** 64
START = 1
DT_AT = 3
STATS_AT, NORM_AT, XT_AT, ROUTER_AT, TOP_AT = 1, 2, 4, 5, 6


class Jobs:

    def __init__(self, names, base):
        self.at = {name: i for i, name in enumerate(names)}
        assert len(self.at) == len(names)
        self.per = [len(range(k, len(names), NB)) for k in range(NB)]
        self.base = base

    def bank(self, name):
        return self.at[name] % NB

    def count(self, name, it, before=0):
        k = self.bank(name)
        return it * self.per[k] + (self.base[k] + self.at[name] // NB + 1 - before * self.per[k])

    def after(self, iterations):
        return [b + iterations * n for b, n in zip(self.base, self.per)]


def attention_jobs():
    names = []
    for u in range(NG):
        names += [("gate", u, k, i) for k in range(GT) for i in range(2)]
        names += [("x2f", u), ("x2r", u), ("wT", u)]
        for j in range(2 * NP):
            names += [("qk", u, j)]
            if j == DT_AT:
                names += [("dt", u)]
            if j % 2:
                names += [("v", u, j // 4, j // 2 % 2)]
        names += [("bias2", u)]
        for p in range(NP):
            if p == XT_AT:
                names += [("xT", u)]
            if p == ROUTER_AT:
                names += [("router", u)]
            names += [("kt", u, p), ("score", u, p, 0), ("score", u, p, 1), ("h", u, p, 0), ("h", u, p, 1),
                      ("kv", u, p, 0), ("kv", u, p, 1), ("h", u, p, 2), ("h", u, p, 3)]
            if p:
                names += [("oT", u, p - 1)]
            names += [("o", u, p, 0), ("o", u, p, 1), ("ffn", u, p)]
        names += [("h", u, E0, i) for i in range(HT)]
        names += [("oT", u, NP - 1), ("ffn", u, E0), ("attn", u)]
    return names


def mamba_jobs():
    names = [("ohT",), ("mask", 0), ("mask", 1), ("z", 0), ("z", 1)]
    names += [("conv", 0, i) for i in range(3)] + [("h", 0)] + [("conv", 1, i) for i in range(3)]
    names += [("L", 0, 0), ("L", 0, 1), ("L", 1, 0), ("h", 1), ("L", 1, 1), ("P",)]
    names += [("tr", d, b) for d in range(2) for b in range(B)]
    names += [("G",), ("yT", 0), ("yT", 1), ("ffn",)]
    for d in range(2):
        names += [("y", d, b) for b in range(B)]
        names += [("S", d)]
    return names


def last_jobs():
    return [(n, u) for u in range(NG) for n in ("sT", "s")]


def mean_and_variance(dve, stats, mean, part, var_eps, eps, then):
    even, odd = stats[:, :, 1], stats[:, :, 4]
    dve.tensor_tensor(part[:, 0, :], even, odd, ALU.subtract)
    dve.tensor_tensor(part[:, 1, :], stats[:, :, 2], stats[:, :, 5], ALU.add)
    then(dve.tensor_tensor(mean[:, :], even, odd, ALU.add))
    dve.tensor_tensor(part[:, 0, :], part[:, 0, :], part[:, 0, :], ALU.mult)
    dve.tensor_scalar(mean[:, :], mean[:, :], 0.5, None, ALU.mult)
    then(dve.tensor_scalar(part[:, 1, :], part[:, 1, :], 1.0 / D, eps, ALU.mult, ALU.add))
    return dve.scalar_tensor_tensor(out=var_eps[:, :], in0=part[:, 0, :], scalar=0.25, in1=part[:, 1, :],
                                    op0=ALU.mult, op1=ALU.add)


def build(nc, a, out):
    pairs_ready = NP * NG
    with ExitStack() as ctx:
        def sb(name, *shape, stack=ctx, dt=F32):
            return stack.enter_context(nc.sbuf_tensor(name, list(shape), dt))

        def sem(name):
            return ctx.enter_context(nc.semaphore(name))

        bank = [ctx.enter_context(nc.psum_tensor(f"bank{k}", [P, 512], F32)) for k in range(NB)]
        bank_full = [sem(f"bank_full{k}") for k in range(NB)]
        bank_done = [sem(f"bank_done{k}") for k in range(NB)]

        x_all = sb("x_all", P, 1 + B * NG, GT, D)
        xn2_all = sb("xn2_all", P, B, NT, D)
        xTf_all = sb("xTf_all", P, B, TAP - 1 + T + P)
        xTr_all = sb("xTr_all", P, B, TAP - 1 + T + P)
        dtf_all = sb("dtf_all", P, B, NT, 2 * MH)
        dtr_all = sb("dtr_all", P, B, NT, MH)
        ident = sb("ident", P, P)
        flip = sb("flip", P, P)
        causal = sb("causal", P, P)
        ones = sb("ones", P, P)
        before = sb("before", P, 8, 8)
        minus_half = sb("minus_half", P, 8)
        dtw = sb("dtw", P, 3 * MH)

        const_ready, credit = sem("const_ready"), sem("credit")
        w_x0 = sem("first_x_loaded")
        w_x, w_qkv, w_gate, w_router, w_ffn, w_b, w_out_s = (sem(n) for n in (
            "x_loaded", "qkv_loaded", "gate_loaded", "router_loaded", "ffn_loaded", "b_loaded", "wout_loaded"))
        dtw_loaded = sem("dtw_loaded")

        ahead = {n: sem(n) for n in ("og_ready", "x1_ready", "pool_copied", "xE_ready", "yn_ready", "yg_ready",
                                     "xD_ready", "pool1", "out_ready", "bc_ready")}
        og_ready, x1_ready, pool_copied, xE_ready, yn_ready, yg_ready, xD_ready, pool1, out_ready, bc_ready = ahead.values()
        out_stored = [sem(f"out_stored{u}") for u in range(NG)]

        L0 = Jobs(attention_jobs(), None)
        L0s = Jobs([("xT", 0), ("router", 0)], L0.per)
        L0.base = L0s.after(1)
        L0e = Jobs([("x2f", 0), ("x2r", 0), ("dt", 0)], L0.after(B))
        L1 = Jobs(mamba_jobs(), L0e.after(1))
        L1e = Jobs([("yT", d) for d in range(2)], L1.after(NT))
        L2 = Jobs(last_jobs(), L1e.after(1))

        def awaiting(jobs):
            def await_full(eng, it, *name, before=0):
                eng.wait_ge(bank_full[jobs.bank(name)], jobs.count(name, it, before))

            def await_done(eng, it, *name, before=0):
                eng.wait_ge(bank_done[jobs.bank(name)], jobs.count(name, it, before))

            def opened(eng, it, *name):
                k = jobs.bank(name)
                eng.wait_ge(bank_done[k], it * jobs.per[k] + (jobs.base[k] + jobs.at[name] // NB))
                return bank[k]

            def psum(*name):
                return bank[jobs.bank(name)]

            def filled(ins, *name):
                ins.then_inc(bank_full[jobs.bank(name)], 1)

            def taken(ins, *name):
                ins.then_inc(bank_done[jobs.bank(name)], 1)

            return await_full, await_done, opened, psum, filled, taken

        with nc.Block() as block:
            @block.gpsimd
            def _(pool):
                pool.memset(ident[:, :], 0.0).then_inc(const_ready, 1)
                pool.memset(flip[:, :], 0.0).then_inc(const_ready, 1)
                pool.memset(causal[:, :], 1.0).then_inc(const_ready, 1)
                pool.memset(before[:, :, :], 1.0).then_inc(const_ready, 1)
                pool.memset(ones[:, :], 1.0)
                pool.memset(minus_half[:, :], -0.5)
                pool.memset(xTf_all[:, :, 0:TAP - 1], 0.0)
                pool.memset(xTr_all[:, :, 0:TAP - 1], 0.0)
                pool.memset(xTf_all[:, :, TAP - 1 + T:], 0.0)
                pool.memset(xTr_all[:, :, TAP - 1 + T:], 0.0)
                pool.wait_ge(const_ready, 4)
                pool.affine_select(out=ident[:, :], in_=ident[:, :], compare_op=ALU.not_equal, fill=1.0,
                                   base=0, pattern=[[-1, P]], channel_multiplier=1).then_inc(const_ready, 1)
                pool.affine_select(out=flip[:, :], in_=flip[:, :], compare_op=ALU.not_equal, fill=1.0,
                                   base=1 - P, pattern=[[1, P]], channel_multiplier=1)
                pool.affine_select(out=causal[:, :], in_=causal[:, :], compare_op=ALU.is_ge, fill=0.0,
                                   base=0, pattern=[[1, P]], channel_multiplier=-1)
                pool.affine_select(out=before[:, :, :], in_=before[:, :, :], compare_op=ALU.is_gt, fill=0.0,
                                   base=0, pattern=[[1, 8], [-1, 8]], channel_multiplier=0)

            @block.sync
            def _(sp):
                for k in range(NB):
                    sp.sem_inc(bank_full[k], L0.per[k])
                    sp.sem_inc(bank_done[k], L0.per[k])
                for s in ahead.values():
                    sp.sem_inc(s, START)
                for u in range(NG):
                    sp.sem_inc(out_stored[u], 16)
                for b in range(B):
                    for u in range(NG):
                        sp.dma_start(x_all[:, b * NG + u + 1, :, :],
                                     a["x"][b, u * GW:(u + 1) * GW, :].rearrange("(k p) d -> p k d", p=P)
                                     ).then_inc(w_x if b + u else w_x0, 16)

        with ExitStack() as l0:
            def s0(name, *shape):
                return sb(name, *shape, stack=l0)

            wqkv = s0("wqkv", P, 3 * H * HD)
            wgate = s0("wgate", P, H * HD)
            wout = s0("wout", P, NP, D)
            w1 = s0("w1", P, E0 + 1, 512)
            w2 = s0("w2", P, E0 + 1, HT, D)
            b1 = s0("b1", P, E0 + 1, HT)
            b2 = s0("b2", E0 + 1, D)
            wg = s0("wg", P, E0)
            bg_b = s0("bg_b", P, E0)
            bias_b = s0("bias_b", P, E0)

            xn_g = s0("xn_g", P, GT, D)
            xT_g = s0("xT_g", P, NG, GW)
            stats = s0("stats", P, GT, 6)
            mean = s0("mean", P, GT)
            part = s0("part", P, 2, GT)
            vareps = s0("vareps", P, GT)
            rstd = s0("rstd", P, GT)
            logit = s0("logit", P, GT, E0)
            sexp = s0("sexp", P, GT, E0)
            score = s0("score", P, GT, E0)
            gt3 = s0("gt3", P, GT, E0, E0)
            eq3 = s0("eq3", P, GT, E0, E0)
            rank = s0("rank", P, GT, E0)
            w9 = s0("w9", P, NG, GT, E0 + 1)
            wT9 = s0("wT9", E0 + 1, GW)
            ebuf = s0("ebuf", P, 2, GW)
            qT = s0("qT", P, NP, GW)
            kT = s0("kT", P, NP, GW)
            v1 = s0("v1", P, GT, H, HA)
            gate = s0("gate", P, GT, H * HD)
            ktok = s0("ktok", P, GT, P)
            sm = s0("sm", P, 2, GT, P)
            kvc = s0("kvc", P, NP, 2, HA)
            kvw = s0("kvw", P, GT - 1, 2, HA)
            rden = s0("rden", P, GT, 2)
            o_g = s0("o_g", P, GT, P)
            og_g = s0("og_g", P, GT, P)
            oT = qT
            hT = s0("hT", P, HT, GW)
            facc = s0("facc", P, GT, D)
            th = xn_g
            sg = o_g
            x1_g = facc
            xn2_g = s0("xn2_g", P, GT, D)
            x2f_g = s0("x2f_g", P, GW)
            x2r_g = s0("x2r_g", P, GW)

            var_ready, rstd_ready, xn_ready = sem("var_ready"), sem("rstd_ready"), sem("xn_ready")
            var2_ready, rstd2_ready, xn2_ready = sem("var2_ready"), sem("rstd2_ready"), sem("xn2_ready")
            spare_zero = sem("spare_zero")
            sexp_ready, w9_ready = sem("sexp_ready"), sem("w9_ready")
            exp_ready, kv_ready = sem("exp_ready"), sem("kv_ready")
            th_ready = sem("th_ready")
            dve0 = sem("dve0")
            loop, first, final = awaiting(L0), awaiting(L0s), awaiting(L0e)
            await_full, await_done, opened, psum, filled, taken = loop
            MW = 64

            with nc.Block() as block:
                @block.sync
                def _(sp):
                    sp.dma_start(wg[:, :], a["wg"]).then_inc(w_router, 16)
                    sp.dma_start(dtw[:, :], a["dtw"]).then_inc(dtw_loaded, 16)
                    sp.dma_start(bg_b[:, :], a["bg"].partition_broadcast(P)).then_inc(w_router, 16)
                    sp.dma_start(bias_b[:, :], a["bias"].partition_broadcast(P)).then_inc(w_router, 16)
                    sp.dma_start(wgate[:, :], a["w_gate"]).then_inc(w_gate, 16)
                    for c in (slice(0, 1536), slice(1536, 3072)):
                        sp.dma_start(wqkv[:, c], a["w_qkv"][:, c]).then_inc(w_qkv, 16)
                    sp.dma_start(b1[:, 0:E0, :], a["b1"]).then_inc(w_b, 16)
                    sp.dma_start(b1[:, E0, :], a["bs1"]).then_inc(w_b, 16)
                    sp.dma_start(b2[0:E0, :], a["b2"]).then_inc(w_b, 16)
                    sp.dma_start(b2[E0:E0 + 1, :], a["bs2"]).then_inc(w_b, 16)
                    for e in range(E0 + 1):
                        sp.dma_start(w1[:, e, :], a["w1"][e] if e < E0 else a["ws1"]).then_inc(w_ffn, 16)
                        sp.dma_start(w2[:, e, :, :], a["w2"][e] if e < E0 else a["ws2"]).then_inc(w_ffn, 16)
                    sp.wait_ge(w_ffn, 16 * 2 * (E0 + 1))
                    sp.dma_start(wout[:, :, :], a["w_out"]).then_inc(w_out_s, 16)

                @block.tensor
                def _(pe):
                    def xT_job(jobs, it, u, nth):
                        _, _, opened, _, filled, _ = jobs
                        o = opened(pe, it, "xT", u)
                        pe.wait_ge(xn_ready, nth)
                        for k in range(GT):
                            m = pe.transpose(o[:, k * P:(k + 1) * P], xn_g[:, k, :], ident[:, :])
                        filled(m, "xT", u)

                    def router_job(jobs, it, u, slot):
                        _, await_done, opened, _, filled, _ = jobs
                        await_done(pe, it, "xT", u)
                        pe.wait_ge(w_router, 48)
                        o = opened(pe, it, "router", u)
                        for k in range(GT):
                            m = pe.matmul(o[:, k * E0:(k + 1) * E0], xT_g[:, slot, k * P:(k + 1) * P], wg[:, :],
                                          start=True, stop=True)
                        filled(m, "router", u)

                    def x2_jobs(jobs, it, u, nth=None):
                        _, _, opened, _, filled, _ = jobs
                        o = opened(pe, it, "x2f", u)
                        pe.wait_ge(xn2_ready, nth or it * NG + (u + 1))
                        for k in range(GT):
                            m = pe.transpose(o[:, k * P:(k + 1) * P], xn2_g[:, k, :], ident[:, :])
                        filled(m, "x2f", u)
                        o = opened(pe, it, "x2r", u)
                        for k in range(GT):
                            kr = GT - 1 - k
                            m = pe.transpose(o[:, kr * P:(kr + 1) * P], xn2_g[:, k, :], flip[:, :])
                        filled(m, "x2r", u)

                    def dt_job(jobs, it, u):
                        _, await_done, opened, _, filled, _ = jobs
                        o = opened(pe, it, "dt", u)
                        await_done(pe, it, "x2f", u)
                        await_done(pe, it, "x2r", u)
                        pe.wait_ge(dtw_loaded, 16)
                        for k in range(GT):
                            c = slice(k * P, (k + 1) * P)
                            pe.matmul(o[:, 8 * k:8 * k + 8], x2f_g[:, c], dtw[:, 0:8], start=True, stop=True)
                            m = pe.matmul(o[:, 32 + 4 * k:36 + 4 * k], x2r_g[:, c], dtw[:, 8:12],
                                          start=True, stop=True)
                        filled(m, "dt", u)

                    def layer(b):
                        def h_job(u, e, i):
                            pe.wait_ge(w_ffn, 32 * (E0 + 1))
                            o = opened(pe, b, "h", u, e, i)
                            filled(pe.matmul(o[:, :], w1[:, e, i * P:(i + 1) * P], xT_g[:, u, :],
                                             start=True, stop=True), "h", u, e, i)

                        def token_job(u, name, w, c0, k, i):
                            o = opened(pe, b, name, u, k, i)
                            filled(pe.matmul(o[:, :], xT_g[:, u, k * P:(k + 1) * P], w[:, c0:c0 + 512],
                                             start=True, stop=True), name, u, k, i)

                        def ffn_job(u, e):
                            o = opened(pe, b, "ffn", u, e)
                            for i in range(HT):
                                await_done(pe, b, "h", u, e, i)
                            for k in range(GT):
                                for i in range(HT):
                                    m = pe.matmul(o[:, k * P:(k + 1) * P], hT[:, i, k * P:(k + 1) * P],
                                                  w2[:, e, i, :], start=(i == 0), stop=(i == HT - 1))
                            filled(m, "ffn", u, e)

                        def oT_job(u, p):
                            o = opened(pe, b, "oT", u, p)
                            pe.wait_ge(og_ready, b * pairs_ready + (u * NP + p + 1) + START)
                            for k in range(GT):
                                m = pe.transpose(o[:, k * P:(k + 1) * P], og_g[:, k, :], ident[:, :])
                            filled(m, "oT", u, p)

                        for u in range(NG):
                            pe.wait_ge(w_gate, 16)
                            for k in range(GT):
                                for i in range(2):
                                    token_job(u, "gate", wgate, i * 512, k, i)
                            x2_jobs(loop, b, u)
                            o = opened(pe, b, "wT", u)
                            pe.wait_ge(w9_ready, b * NG + (u + 1))
                            for k in range(GT):
                                m = pe.transpose(o[0:E0 + 1, k * P:(k + 1) * P], w9[:, u, k, :], ident[:, :])
                            filled(m, "wT", u)
                            pe.wait_ge(w_qkv, 32)
                            for j in range(2 * NP):
                                o = opened(pe, b, "qk", u, j)
                                c = (j % 2) * H * HD + (j // 2) * P
                                filled(pe.matmul(o[:, :], wqkv[:, c:c + P], xT_g[:, u, :], start=True, stop=True),
                                       "qk", u, j)
                                if j == DT_AT:
                                    dt_job(loop, b, u)
                                if j % 2:
                                    k, i = j // 4, j // 2 % 2
                                    token_job(u, "v", wqkv, 2 * H * HD + i * 512, k, i)
                            o = opened(pe, b, "bias2", u)
                            await_done(pe, b, "wT", u)
                            pe.wait_ge(w_b, 64)
                            for k in range(GT):
                                m = pe.matmul(o[:, k * P:(k + 1) * P], wT9[:, k * P:(k + 1) * P], b2[:, :],
                                              start=True, stop=True)
                            filled(m, "bias2", u)
                            for p in range(NP):
                                if p == XT_AT:
                                    xT_job(loop, b, u, b * NG + (u + 2))
                                if p == ROUTER_AT:
                                    router_job(loop, b, u, 1 - u)
                                assert L0.at["kt", u, p] - L0.at["qk", u, 2 * p + 1] > NB
                                o = opened(pe, b, "kt", u, p)
                                for k in range(GT):
                                    m = pe.transpose(o[:, k * P:(k + 1) * P], kT[:, p, k * P:(k + 1) * P],
                                                     ident[:, :])
                                filled(m, "kt", u, p)
                                for hh in range(2):
                                    r = slice(MW * hh, MW * hh + HD)
                                    o = opened(pe, b, "score", u, p, hh)
                                    for k in range(GT):
                                        c = slice(k * P, (k + 1) * P)
                                        m = pe.matmul(o[:, c], kT[r, p, c], qT[r, p, c], start=True, stop=True)
                                    filled(m, "score", u, p, hh)
                                h_job(u, p, 0)
                                h_job(u, p, 1)
                                await_done(pe, b, "kt", u, p)
                                if p == 0:
                                    await_done(pe, b, "v", u, GT - 1, 1)
                                for i in range(2):
                                    o = opened(pe, b, "kv", u, p, i)
                                    for kk in range(2):
                                        k = 2 * i + kk
                                        m = pe.matmul(o[:, kk * 2 * HA:(kk + 1) * 2 * HA], ktok[:, k, :],
                                                      v1[:, k, 2 * p:2 * p + 2, :].rearrange("s h i -> s (h i)"),
                                                      start=True, stop=True)
                                    filled(m, "kv", u, p, i)
                                h_job(u, p, 2)
                                h_job(u, p, 3)
                                if p:
                                    oT_job(u, p - 1)
                                await_done(pe, b, "score", u, p, 0)
                                await_done(pe, b, "score", u, p, 1)
                                pe.wait_ge(kv_ready, b * pairs_ready + (u * NP + p + 1))
                                for i in range(2):
                                    o = opened(pe, b, "o", u, p, i)
                                    for kk in range(2):
                                        k = 2 * i + kk
                                        c = slice(k * P, (k + 1) * P)
                                        state = kvc[:, p, :, :] if k == 0 else kvw[:, k - 1, :, :]
                                        pe.matmul(o[:, kk * 2 * HA:(kk + 1) * 2 * HA], qT[:, p, c],
                                                  state.rearrange("j h i -> j (h i)"), start=True, stop=True)
                                        for hh in range(2):
                                            c0 = (2 * kk + hh) * HA
                                            m = pe.matmul(o[:, c0:c0 + HA], sm[:, hh, k, :], v1[:, k, 2 * p + hh, :],
                                                          start=False, stop=True, skip_group_check=True)
                                    filled(m, "o", u, p, i)
                                ffn_job(u, p)
                            for i in range(HT):
                                h_job(u, E0, i)
                            oT_job(u, NP - 1)
                            ffn_job(u, E0)
                            o = opened(pe, b, "attn", u)
                            await_done(pe, b, "oT", u, NP - 1)
                            pe.wait_ge(w_out_s, 16)
                            for k in range(GT):
                                for p in range(NP):
                                    m = pe.matmul(o[:, k * P:(k + 1) * P], oT[:, p, k * P:(k + 1) * P],
                                                  wout[:, p, :], start=(p == 0), stop=(p == NP - 1))
                            filled(m, "attn", u)

                    xT_job(first, 0, 0, 1)
                    router_job(first, 0, 0, 0)
                    with pe.Fori(0, B) as b:
                        layer(b)
                    x2_jobs(final, 0, 0, B * NG + 1)
                    dt_job(final, 0, 0)

                @block.scalar
                def _(act):
                    def xT_copy(jobs, it, u, slot):
                        await_full, _, _, psum, _, taken = jobs
                        await_full(act, it, "xT", u)
                        taken(act.activation(xT_g[:, slot, :], psum("xT", u)[:, :], ACT.Copy), "xT", u)

                    def router_exp(jobs, it, u):
                        _, await_done, _, _, _, _ = jobs
                        await_done(act, it, "router", u)
                        act.activation(sexp[:, :, :], logit[:, :, :], ACT.Exp, scale=-1.0).then_inc(sexp_ready, 1)

                    def x2_copies(jobs, it, u, copied):
                        await_full, _, _, psum, _, taken = jobs
                        act.wait_ge(pool_copied, copied + START)
                        await_full(act, it, "x2f", u)
                        taken(act.activation(x2f_g[:, :], psum("x2f", u)[:, :], ACT.Copy), "x2f", u)
                        await_full(act, it, "x2r", u)
                        taken(act.activation(x2r_g[:, :], psum("x2r", u)[:, :], ACT.Copy), "x2r", u)

                    def layer(b):
                        for u in range(NG):
                            act.wait_ge(og_ready, b * pairs_ready + u * NP + START)
                            for k in range(GT):
                                for i in range(2):
                                    await_full(act, b, "gate", u, k, i)
                                    taken(act.activation(gate[:, k, 512 * i:512 * i + 512],
                                                         psum("gate", u, k, i)[:, :], ACT.Sigmoid), "gate", u, k, i)
                            x2_copies(loop, b, u, b * NG + u)
                            await_full(act, b, "wT", u)
                            taken(act.activation(wT9[:, :], psum("wT", u)[0:E0 + 1, :], ACT.Copy), "wT", u)
                            for j in range(2 * NP):
                                await_full(act, b, "qk", u, j)
                                if j >= 2:
                                    await_done(act, b, "qk", u, j - 2)
                                else:
                                    await_done(act, b, "qk", (u + 1) % 2, 2 * NP - 2 + j, before=1 - u)
                                act.activation(ebuf[:, j % 2, :], psum("qk", u, j)[:, :], ACT.Exp
                                               ).then_inc(exp_ready, 1)
                                if j % 2:
                                    k, i = j // 4, j // 2 % 2
                                    await_full(act, b, "v", u, k, i)
                                    src = psum("v", u, k, i)[:, :].rearrange("t (h i) -> t h i", i=HD)
                                    taken(act.activation(v1[:, k, 8 * i:8 * i + 8, 0:HD], src, ACT.Copy),
                                          "v", u, k, i)
                            act.wait_ge(pool_copied, b * NG + (u + 1) + START)
                            await_full(act, b, "bias2", u)
                            taken(act.activation(facc[:, :, :], psum("bias2", u)[:, :].rearrange("t (k d) -> t k d", k=GT),
                                                 ACT.Copy), "bias2", u)

                            def gelu(e, i):
                                await_full(act, b, "h", u, e, i)
                                taken(act.activation(hT[:, i, :], psum("h", u, e, i)[:, :], ACT.Gelu,
                                                     bias=b1[:, e, i:i + 1]), "h", u, e, i)

                            def oT_copy(p):
                                await_full(act, b, "oT", u, p)
                                taken(act.activation(oT[:, p, :], psum("oT", u, p)[:, :], ACT.Copy), "oT", u, p)

                            act.wait_ge(w_b, 64)
                            for p in range(NP):
                                if p == XT_AT:
                                    xT_copy(loop, b, u, 1 - u)
                                await_full(act, b, "kt", u, p)
                                taken(act.activation(ktok[:, :, :], psum("kt", u, p)[:, :].rearrange("t (k d) -> t k d", k=GT),
                                                     ACT.Copy), "kt", u, p)
                                for i in range(HT):
                                    gelu(p, i)
                                if p:
                                    oT_copy(p - 1)
                                if p == ROUTER_AT:
                                    router_exp(loop, b, u)
                            for i in range(HT):
                                gelu(E0, i)
                            oT_copy(NP - 1)
                            await_done(act, b, "ffn", u, E0)
                            act.activation(th[:, :, :], facc[:, :, :], ACT.Tanh, scale=0.5).then_inc(th_ready, 1)

                    xT_copy(first, 0, 0, 0)
                    router_exp(first, 0, 0)
                    with act.Fori(0, B) as b:
                        layer(b)
                    x2_copies(final, 0, 0, B * NG)

                @block.gpsimd
                def _(pool):
                    def root(given, wanted, nth):
                        pool.wait_ge(given, nth)
                        pool.tensor_tensor(rstd[:, :], vareps[:, :], minus_half[:, 0:GT], ALU.pow).then_inc(wanted, 1)

                    def keep(jobs, it, u, nth, slot, b, ub):
                        _, await_done, _, _, _, _ = jobs
                        root(var2_ready, rstd2_ready, nth)
                        pool.tensor_copy(x_all[:, slot, :, :], x1_g[:, :, :])
                        pool.wait_ge(xn2_ready, nth)
                        pool.tensor_copy(xn2_all[:, b, ub * GT:(ub + 1) * GT, :], xn2_g[:, :, :])
                        await_done(pool, it, "x2f", u)
                        c0 = TAP - 1 + ub * GW
                        pool.tensor_copy(xTf_all[:, b, c0:c0 + GW], x2f_g[:, :])
                        await_done(pool, it, "x2r", u)
                        c0 = TAP - 1 + (NG - 1 - ub) * GW
                        pool.tensor_copy(xTr_all[:, b, c0:c0 + GW], x2r_g[:, :]).then_inc(pool_copied, 1)

                    def layer(b):
                        for u in range(NG):
                            keep(loop, b, u, b * NG + (u + 1), b * NG + u, b if u else b * -1 + 1, 1 - u)
                            for p in range(NP):
                                await_done(pool, b, "o", u, p, 0)
                                await_done(pool, b, "o", u, p, 1)
                                if p == 0:
                                    assert L0.at["o", u, 0, 0] - L0.at["gate", u, GT - 1, 1] > NB
                                    await_full(pool, b, "oT", 1 - u, NP - 1, before=1 - u)
                                else:
                                    await_full(pool, b, "oT", u, p - 1)
                                pool.tensor_tensor(og_g[:, :, :], o_g[:, :, :], gate[:, :, p * P:(p + 1) * P],
                                                   ALU.mult).then_inc(og_ready, 1)
                                if p == STATS_AT:
                                    root(var_ready, rstd_ready, b * NG + (u + 2))

                    pool.memset(o_g[:, :, :], 0.0)
                    pool.memset(x_all[:, 0, :, :], 0.0).then_inc(spare_zero, 1)
                    root(var_ready, rstd_ready, 1)
                    with pool.Fori(0, B) as b:
                        layer(b)
                    keep(final, 0, 0, B * NG + 1, B * NG, B - 1, NG - 1)

                PRO = 3 + 8
                STEPS = 1 + NG * (2 * 3 + 8 + 2 * NP + 4 * NP + 1)

                @block.vector
                def _(dve):
                    n = [0]

                    def step(ins):
                        ins.then_inc(dve0, 1)
                        n[0] += 1
                        return n[0]

                    def after(b, count):
                        dve.wait_ge(dve0, b * STEPS + count)

                    def moments(b, var, src):
                        for k in range(GT):
                            m = dve.bn_stats(stats[:, k, :], src(k))
                        after(b, step(m))
                        mean_and_variance(dve, stats, mean, part, vareps, 1e-5, lambda m: after(b, step(m))
                                          ).then_inc(var, 1)

                    def normalise(nth, root, made, src, dst):
                        dve.wait_ge(root, nth)
                        for k in range(GT):
                            m = dve.tensor_scalar(dst[:, k, :], src(k), mean[:, k:k + 1], rstd[:, k:k + 1],
                                                  ALU.subtract, ALU.mult)
                        m.then_inc(made, 1)

                    def logits(jobs, it, u, b):
                        await_full, _, _, psum, _, taken = jobs
                        await_full(dve, it, "router", u)
                        dve.wait_ge(w_router, 48)
                        lg = psum("router", u)[:, 0:GT * E0].rearrange("t (k e) -> t k e", k=GT)
                        after(b, step(dve.tensor_tensor(logit[:, :, :], lg, bg_b[:, :].unsqueeze(1).broadcast_to([P, GT, E0]),
                                                        ALU.add)))
                        taken(dve.tensor_tensor(logit[:, :, :], logit[:, :, :],
                                                bias_b[:, :].unsqueeze(1).broadcast_to([P, GT, E0]), ALU.add), "router", u)

                    def top_two(b, nth, slot):
                        then = lambda m: after(b, step(m))
                        dve.wait_ge(sexp_ready, nth)
                        then(dve.tensor_scalar(sexp[:, :, :], sexp[:, :, :], 1.0, None, ALU.add))
                        then(dve.reciprocal(score[:, :, :], sexp[:, :, :]))
                        sj = score[:, :, :].unsqueeze(2).broadcast_to([P, GT, E0, E0])
                        se = score[:, :, :].unsqueeze(3).broadcast_to([P, GT, E0, E0])
                        step(dve.tensor_tensor(gt3[:, :, :, :], sj, se, ALU.is_gt))
                        then(dve.tensor_tensor(eq3[:, :, :, :], sj, se, ALU.is_equal))
                        bf = before[:, :, :].rearrange("p e j -> p (e j)").unsqueeze(1).broadcast_to([P, GT, E0 * E0])
                        flat = eq3[:, :, :, :].rearrange("p k e j -> p k (e j)")
                        then(dve.tensor_tensor(flat, flat, bf, ALU.mult))
                        then(dve.tensor_tensor(gt3[:, :, :, :], gt3[:, :, :, :], eq3[:, :, :, :], ALU.add))
                        then(dve.tensor_reduce(rank[:, :, :], gt3[:, :, :, :], AX.X, ALU.add))
                        dve.scalar_tensor_tensor(out=w9[:, slot, :, 0:E0], in0=rank[:, :, :], scalar=2.0,
                                                 in1=score[:, :, :], op0=ALU.is_lt, op1=ALU.mult).then_inc(w9_ready, 1)

                    def result(b, nth, slot):
                        dve.wait_ge(pool_copied, nth - 1 + START)
                        dve.scalar_tensor_tensor(out=x1_g[:, :, :], in0=sg[:, :, :], scalar=0.5,
                                                 in1=x_all[:, slot, :, :], op0=ALU.mult, op1=ALU.add).then_inc(x1_ready, 1)
                        dve.wait_ge(x1_ready, nth + START)
                        moments(b, var2_ready, lambda k: x1_g[:, k, :])
                        normalise(nth, rstd2_ready, xn2_ready, lambda k: x1_g[:, k, :], xn2_g)

                    def dt_copies(jobs, it, u, b, ub):
                        await_full, _, _, psum, _, taken = jobs
                        await_full(dve, it, "dt", u)
                        dt, ur = psum("dt", u), NG - 1 - ub
                        dve.tensor_copy(dtf_all[:, b, ub * GT:(ub + 1) * GT, :], dt[:, 0:32].rearrange("t (k c) -> t k c", k=GT))
                        taken(dve.tensor_copy(dtr_all[:, b, ur * GT:(ur + 1) * GT, :],
                                              dt[:, 32:48].rearrange("t (k c) -> t k c", k=GT)), "dt", u)

                    def layer(b):
                        then = lambda m: after(b, step(m))
                        kvc_zero = step(dve.memset(kvc[:, :, :, :], 0.0))
                        for u in range(NG):
                            result(b, b * NG + (u + 1), b * NG + u)
                            for j in range(2 * NP):
                                dve.wait_ge(exp_ready, b * NG * 2 * NP + (u * 2 * NP + j + 1))
                                then(dve.tensor_scalar(ebuf[:, j % 2, :], ebuf[:, j % 2, :], 1.0, None, ALU.min))
                                dst = (qT, kT)[j % 2]
                                taken(dve.scalar_tensor_tensor(out=dst[:, j // 2, :], in0=psum("qk", u, j)[:, :],
                                                               scalar=1.0, in1=ebuf[:, j % 2, :],
                                                               op0=ALU.add, op1=ALU.max), "qk", u, j)
                                if j == DT_AT:
                                    dt_copies(loop, b, u, b if u else b * -1 + 1, 1 - u)

                            def ffn_add(e):
                                if e == 0:
                                    await_done(dve, b, "bias2", u)
                                    dve.wait_ge(w9_ready, b * NG + (u + 1))
                                else:
                                    await_done(dve, b, "ffn", u, e - 1)
                                await_full(dve, b, "ffn", u, e)
                                for k in range(GT):
                                    m = dve.scalar_tensor_tensor(out=facc[:, k, :], in0=psum("ffn", u, e)[:, k * P:(k + 1) * P],
                                                                 scalar=w9[:, u, k, e:e + 1], in1=facc[:, k, :],
                                                                 op0=ALU.mult, op1=ALU.add)
                                taken(m, "ffn", u, e)

                            def add_state(p, k, dst, src):
                                i, kk = k // 2, k % 2
                                for hh in range(2):
                                    r = slice(MW * hh, MW * hh + HD)
                                    c0 = (2 * kk + hh) * HA
                                    m = dve.tensor_tensor(dst[r, hh, :], psum("kv", u, p, i)[r, c0:c0 + HA], src[r, hh, :],
                                                          ALU.add)
                                return m

                            if u == 0:
                                after(b, kvc_zero)
                            for p in range(NP):
                                if p == ROUTER_AT:
                                    logits(loop, b, u, b)
                                for hh in range(2):
                                    await_full(dve, b, "score", u, p, hh)
                                    taken(dve.tensor_tensor(sm[:, hh, :, :],
                                                            psum("score", u, p, hh)[:, :].rearrange("s (k t) -> s k t", k=GT),
                                                            causal[:, :].unsqueeze(1).broadcast_to([P, GT, P]), ALU.mult),
                                          "score", u, p, hh)
                                await_full(dve, b, "kv", u, p, 0)
                                carry = kvc[:, p, :, :]
                                s = step(add_state(p, 0, kvw[:, 0, :, :], carry))
                                after(b, s)
                                m = add_state(p, 1, kvw[:, 1, :, :], kvw[:, 0, :, :])
                                taken(m, "kv", u, p, 0)
                                await_done(dve, b, "kv", u, p, 0)
                                await_full(dve, b, "kv", u, p, 1)
                                add_state(p, 2, kvw[:, 2, :, :], kvw[:, 1, :, :]).then_inc(kv_ready, 1)
                                for i in range(2):
                                    await_full(dve, b, "o", u, p, i)
                                    den = psum("o", u, p, i)[:, 0:4 * HA].rearrange("t (c i) -> t c i", i=HA)[:, :, HD]
                                    s = step(dve.tensor_scalar(rden[:, 2 * i:2 * i + 2, :].rearrange("t k h -> t (k h)"), den,
                                                               1e-6, None, ALU.add))
                                after(b, s)
                                then(dve.reciprocal(rden[:, :, :], rden[:, :, :]))
                                dve.wait_ge(og_ready, b * pairs_ready + (u * NP + p) + START)
                                for i in range(2):
                                    src = psum("o", u, p, i)[:, 0:4 * HA].rearrange("t (c i) -> t c i", i=HA)[:, :, 0:HD]
                                    m = dve.tensor_tensor(
                                        o_g[:, 2 * i:2 * i + 2, :].rearrange("t k (h i) -> t (k h) i", h=2), src,
                                        rden[:, 2 * i:2 * i + 2, :].rearrange("t k h -> t (k h)").unsqueeze(2).broadcast_to([P, 4, HD]),
                                        ALU.mult)
                                    taken(m, "o", u, p, i)
                                await_done(dve, b, "o", u, p, 0)
                                await_done(dve, b, "o", u, p, 1)
                                dve.wait_ge(kv_ready, b * pairs_ready + (u * NP + p + 1))
                                s = add_state(p, 3, kvc[:, p, :, :], kvw[:, 2, :, :])
                                taken(s, "kv", u, p, 1)
                                ffn_add(p)
                                slot = b * NG + (u + 2) if u == 0 else b * -NG + (NG + 1)
                                if p == STATS_AT:
                                    moments(b, var_ready, lambda k: x_all[:, slot, k, :])
                                if p == NORM_AT:
                                    normalise(b * NG + (u + 2), rstd_ready, xn_ready, lambda k: x_all[:, slot, k, :], xn_g)
                                if p == TOP_AT:
                                    top_two(b, b * NG + (u + 2), 1 - u)
                            ffn_add(E0)
                            await_done(dve, b, "ffn", u, E0)
                            dve.wait_ge(th_ready, b * NG + (u + 1))
                            dve.wait_ge(og_ready, b * pairs_ready + (u + 1) * NP + START)
                            then(dve.scalar_tensor_tensor(out=sg[:, :, :], in0=th[:, :, :], scalar=1.0, in1=facc[:, :, :],
                                                          op0=ALU.add, op1=ALU.mult))
                            await_full(dve, b, "attn", u)
                            taken(dve.tensor_tensor(sg[:, :, :], psum("attn", u)[:, :].rearrange("t (k d) -> t k d", k=GT),
                                                    sg[:, :, :], ALU.mult), "attn", u)
                            await_done(dve, b, "attn", u)

                    dve.memset(kvw[:, :, :, :], 0.0)
                    dve.memset(v1[:, :, :, HD:HA], 1.0)
                    dve.memset(w9[:, :, :, E0:E0 + 1], 1.0)
                    dve.wait_ge(w_x0, 16)
                    moments(0, var_ready, lambda k: x_all[:, 1, k, :])
                    normalise(1, rstd_ready, xn_ready, lambda k: x_all[:, 1, k, :], xn_g)
                    logits(first, 0, 0, 0)
                    top_two(0, 1, 0)
                    assert n[0] == PRO, n[0]
                    dve.wait_ge(w_x, 16 * (B * NG - 1))
                    dve.wait_ge(spare_zero, 1)
                    with dve.Fori(0, B) as b:
                        layer(b)
                    assert n[0] == PRO + STEPS, n[0]
                    n[0] = PRO
                    result(B, B * NG + 1, B * NG)
                    dt_copies(final, 0, 0, B - 1, NG - 1)

        with ExitStack() as l1:
            def s1(name, *shape):
                return sb(name, *shape, stack=l1)

            ident4 = s1("ident4", P, MH, P)
            inw = s1("inw", P, 2, 3 * P)
            zw = s1("zw", P, 2, DI)
            convw = s1("convw", P, 2, 3, TAP)
            convb = s1("convb", P, 2, 3)
            dtb = s1("dtb", P, 2, MH)
            alog = s1("alog", P, 2, MH)
            dskip = s1("dskip", P, 2, MH)
            outw = s1("outw", P, 2, 2, D)
            normw = s1("normw", P, 2, 2)
            e1w1 = s1("e1w1", P, E1, 512)
            e1b1 = s1("e1b1", E1, 512)
            e1wo = s1("e1wo", P, HT, D)
            bo_b = s1("bo_b", P, D)
            gamma_b = s1("gamma_b", P, D)
            beta_b = s1("beta_b", P, D)

            yT_all = s1("yT_all", P, 2, 2, B, T + P)
            g_all = s1("g_all", P, B, NT, D)
            z_dt = s1("z_dt", P, 2, B, NT, MH)
            u_dt = s1("u_dt", P, 2, B, NT, MH)
            w_dt = s1("w_dt", P, 2, B, NT, MH)
            r_dt = s1("r_dt", P, 2, B, NT, MH)
            dt_flat = s1("dt_flat", P, 2, B, NT, MH)
            l_dt = s1("l_dt", P, 2, B, NT, MH)
            dt_all = s1("dt_all", P, 2, B, NT + 1, MH)
            dA_all = s1("dA_all", P, 2, B, NT + 1, MH)
            dAz_all = s1("dAz_all", P, 2, B, NT + 1, MH)
            expA = s1("expA", P, 2, MH)
            dskip2 = s1("dskip2", P, 2, B, MH)
            oh_all = s1("oh_all", P, B, NT + 1, E1)
            rgt = s1("rgt", P, B * NT, E1, E1)
            req = s1("req", P, B * NT, E1, E1)
            rrank = s1("rrank", P, B * NT, E1)

            xc = s1("xc", P, 2, B, CW)
            dt_c = s1("dt_c", P, 2, B, MH)
            dA_c = s1("dA_c", P, 2, B, MH)
            dAz_c = s1("dAz_c", P, 2, B, MH)
            cv = s1("cv", P, 2, 3, B, P)
            xs = s1("xs", P, 2, 2, B, P)
            BT = s1("BT", MN, 2, B, P)
            CT = s1("CT", MN, 2, B, P)
            zs = s1("zs", P, 2, B, DI)
            xtok = s1("xtok", P, 2, B, DI)
            Btok = s1("Btok", P, 2, B, MN)
            Lm = s1("Lm", P, 2, B, MH, P)
            Mm = s1("Mm", P, 2, B, MH, P)
            xdt = s1("xdt", P, 2, B, DI)
            xE = s1("xE", P, 2, B, DI)
            xD = s1("xD", P, 2, B, DI)
            Pc = s1("Pc", P, 2, B, MH)
            prow = s1("prow", 1, 2, B, MH)
            Pend = s1("Pend", MN, 2, B, MH)
            S = s1("S", MN, 2, B, DI)
            S2 = s1("S2", MN, 2, B, DI)
            yt = s1("yt", P, 2, B, DI)
            yg = s1("yg", P, 2, B, DI)
            ysq = s1("ysq", P, 2, B, DI)
            yn = s1("yn", P, 2, B, DI)
            ss = s1("ss", P, 2, B)
            ms = s1("ms", P, 2, B)
            rs = s1("rs", P, 2, B)
            eps_b = s1("eps_b", P, B)

            oh_c = s1("oh_c", P, B, E1)
            ohT = s1("ohT", E1, B * P)
            xm = s1("xm", P, E1, B * P)
            h1T = s1("h1T", P, HT, B * P)
            y_c = s1("y_c", P, B, D)
            yh_c = s1("yh_c", P, B, D)
            th1 = s1("th1", P, B, D)
            stats1 = s1("stats1", P, B, 6)
            mean1 = s1("mean1", P, B)
            part1 = s1("part1", P, 2, B)
            ve1 = s1("ve1", P, B)
            rstd1 = s1("rstd1", P, B)
            out_g = Mm[:, :, 0, :, :]
            sT = Mm[:, 0, 1, :, :].rearrange("p k t -> p (k t)")
            sg1 = Mm[:, 1, 1, :, :]

            (w_mamba, w_small, w_last, u_ready, u_made, ln_ready, a_ready, dA_ready, dve1, dve2, dve3) = (sem(n) for n in (
                "mamba_w_loaded", "small_w_loaded", "last_w_loaded", "u_ready", "u_made", "ln_ready", "a_ready", "dA_ready",
                "dve1", "dve2", "dve3"))
            (alog_ready, expA_ready, setup_ready, chunk_ready, xc_ready, yg_zero, xdt_ready, prow_ready, S2_ready,
             ss_ready, rs_ready, Mm_ready) = (sem(n) for n in (
                "alog_ready", "expA_ready", "setup_ready", "chunk_ready", "xc_ready", "yg_zero", "xdt_ready",
                "prow_ready", "S2_ready", "ss_ready", "rs_ready", "Mm_ready"))
            ident4_ready = sem("ident4_ready")
            (oh_all_ready, ve1_ready, rstd1_ready, g_ready, th1_ready) = (sem(n) for n in (
                "oh_all_ready", "ve1_ready", "rstd1_ready", "g_ready", "th1_ready"))

            full1, done1, opened1, psum1, filled1, taken1 = awaiting(L1)
            full1e, done1e, opened1e, psum1e, filled1e, taken1e = awaiting(L1e)
            full2, done2, opened2, psum2, filled2, taken2 = awaiting(L2)
            heads = lambda ap: ap.rearrange("p b (h i) -> p (b h) i", i=HD)
            per_head = lambda ap: ap.rearrange("p b h -> p (b h)").unsqueeze(2).broadcast_to([ap.shape[0], B * MH, HD])

            with nc.Block() as block:
                @block.sync
                def _(sp):
                    for dst, src in ((inw[:, :, :], "inw"), (convw[:, :, :, :], "convw"), (convb[:, :, :], "convb"),
                                     (zw[:, :, :], "zw"), (outw[:, :, :, :], "outw"), (normw[:, :, :], "normw")):
                        sp.dma_start(dst, a[src]).then_inc(w_mamba, 16)
                    for dst, src in ((dtb, "dt_bias"), (alog, "A_log"), (dskip, "Dp")):
                        sp.dma_start(dst[:, :, :], a[src].partition_broadcast(P)).then_inc(w_small, 16)
                    for dst, src in ((e1w1[:, :, :], "e1w1"), (e1b1[:, :], "e1b1"), (e1wo[:, :, :], "e1wo")):
                        sp.dma_start(dst, a[src]).then_inc(w_last, 16)
                    for dst, src in ((bo_b, "bo"), (gamma_b, "gamma"), (beta_b, "beta")):
                        sp.dma_start(dst[:, :], a[src].partition_broadcast(P)).then_inc(w_last, 16)
                    with sp.Fori(0, B) as b:
                        for u in range(NG):
                            sp.wait_ge(out_ready, b * NG + (u + 1) + START)
                            sp.dma_start(out[bass.ds(b, 1), u * GW:(u + 1) * GW, :].rearrange("o (k p) d -> p (o k) d", p=P),
                                         out_g[:, u, :, :]).then_inc(out_stored[u], 16)
                    for u in range(NG):
                        sp.wait_ge(out_stored[u], 16 * B + 16)

                @block.tensor
                def _(pe):
                    def turn_y(d, o):
                        for i in range(2):
                            for b in range(B):
                                m = pe.transpose(o[:, (i * B + b) * P:(i * B + b + 1) * P], yn[:, d, b, i * P:(i + 1) * P],
                                                 (ident, flip)[d][:, :])
                        return m

                    def h_job(c, j):
                        o = opened1(pe, c, "h", j)
                        for ii in range(2):
                            cols, w = slice(ii * B * P, (ii + 1) * B * P), slice((2 * j + ii) * P, (2 * j + ii + 1) * P)
                            for e in range(E1):
                                pe.matmul(o[:, cols], e1w1[:, e, w], xm[:, e, :], start=(e == 0), stop=False)
                            m = pe.matmul(o[:, cols], e1b1[:, w], ohT[:, :], start=False, stop=True)
                        filled1(m, "h", j)

                    def conv_jobs(c, d):
                        for i in range(3):
                            o = opened1(pe, c, "conv", d, i)
                            filled1(pe.matmul(o[:, 0:B * CW], inw[:, d, i * P:(i + 1) * P],
                                              xc[:, d, :, :].rearrange("p b t -> p (b t)"), start=True, stop=True),
                                    "conv", d, i)

                    def chunk(c):
                        pe.wait_ge(xc_ready, c + 1)
                        o = opened1(pe, c, "ohT")
                        for b in range(B):
                            m = pe.transpose(o[0:E1, b * P:(b + 1) * P], oh_c[:, b, :], ident[:, :])
                        filled1(m, "ohT")
                        for j in range(2):
                            o = opened1(pe, c, "mask", j)
                            for ee in range(2):
                                for b in range(B):
                                    q = ee * B + b
                                    m = pe.transpose(o[:, q * P:(q + 1) * P],
                                                     oh_c[:, b, 2 * j + ee:2 * j + ee + 1].broadcast_to([P, P]), ident[:, :])
                            filled1(m, "mask", j)
                        for d in range(2):
                            o = opened1(pe, c, "z", d)
                            for b in range(B):
                                m = pe.matmul(o[:, b * DI:(b + 1) * DI], xc[:, d, b, TAP - 1:CW], zw[:, d, :],
                                              start=True, stop=True)
                            filled1(m, "z", d)
                        conv_jobs(c, 0)
                        pe.wait_ge(w_last, 96)
                        done1(pe, c, "ohT")
                        done1(pe, c, "mask", 0)
                        done1(pe, c, "mask", 1)
                        h_job(c, 0)
                        conv_jobs(c, 1)
                        pe.wait_ge(chunk_ready, c + 1)
                        for d in range(2):
                            for b in range(B):
                                o = opened1(pe, c, "L", d, b)
                                for h in range(MH):
                                    m = pe.transpose(o[:, h * P:(h + 1) * P],
                                                     dAz_c[:, d, b, h:h + 1].broadcast_to([P, P]), ident[:, :])
                                filled1(m, "L", d, b)
                                if (d, b) == (1, 0):
                                    h_job(c, 1)
                        o = opened1(pe, c, "P")
                        for d in range(2):
                            pe.wait_ge(prow_ready, 2 * c + (d + 1))
                            for b in range(B):
                                for h in range(MH):
                                    q = (d * B + b) * MH + h
                                    pe.matmul(o[:, q:q + 1], Lm[0:1, d, b, h, :], dA_c[0:1, d, b, h:h + 1],
                                              start=True, stop=True)
                        filled1(pe.matmul(o[0:MN, 16:32], ones[0:1, 0:MN], prow[0:1, :, :, :].rearrange("p d b h -> p (d b h)"),
                                          start=True, stop=True), "P")
                        for d in range(2):
                            pe.wait_ge(bc_ready, 2 * c + (d + 1) + START)
                            for b in range(B):
                                o = opened1(pe, c, "tr", d, b)
                                for i in range(2):
                                    pe.transpose(o[:, i * P:(i + 1) * P], xs[:, d, i, b, :], ident[:, :])
                                filled1(pe.transpose(o[:, DI:DI + MN], BT[:, d, b, :], ident[0:MN, 0:MN]), "tr", d, b)
                        o = opened1(pe, c, "G")
                        for d in range(2):
                            for b in range(B):
                                m = pe.matmul(o[:, (2 * d + b) * P:(2 * d + b + 1) * P], BT[:, d, b, :], CT[:, d, b, :],
                                              start=True, stop=True)
                        filled1(m, "G")
                        for d in range(2):
                            o = opened1(pe, c, "yT", d)
                            pe.wait_ge(yn_ready, 2 * c + (d + 1) + START)
                            filled1(turn_y(d, o), "yT", d)
                        o = opened1(pe, c, "ffn")
                        done1(pe, c, "h", 0)
                        done1(pe, c, "h", 1)
                        for b in range(B):
                            for i in range(HT):
                                m = pe.matmul(o[:, b * D:(b + 1) * D], h1T[:, i, b * P:(b + 1) * P], e1wo[:, i, :],
                                              start=(i == 0), stop=(i == HT - 1))
                        filled1(m, "ffn")
                        for d in range(2):
                            pe.wait_ge(xdt_ready, 2 * c + (d + 1))
                            if d == 0:
                                pe.wait_ge(Mm_ready, c + 1)
                            else:
                                done1(pe, c, "G")
                            done1(pe, c, "S", d, before=1)
                            for b in range(B):
                                o = opened1(pe, c, "y", d, b)
                                for h in range(MH):
                                    pe.matmul(o[:, h * HD:(h + 1) * HD], Mm[:, d, b, h, :], xdt[:, d, b, h * HD:(h + 1) * HD],
                                              start=True, stop=True)
                                filled1(pe.matmul(o[:, DI:2 * DI], CT[:, d, b, :], S[:, d, b, :], start=True, stop=True),
                                        "y", d, b)
                            o = opened1(pe, c, "S", d)
                            pe.wait_ge(xE_ready, 2 * c + (d + 1) + START)
                            for b in range(B):
                                done1(pe, c, "tr", d, b)
                                m = pe.matmul(o[0:MN, b * DI:(b + 1) * DI], Btok[:, d, b, :], xE[:, d, b, :],
                                              start=True, stop=True)
                            filled1(m, "S", d)

                    def last(b):
                        for u in range(NG):
                            o = opened2(pe, b, "sT", u)
                            for d in range(2):
                                c0 = u * GW + (P if d == 0 else 0)
                                for i in range(2):
                                    m = pe.matmul(o[:, :], outw[:, d, i, :],
                                                  yT_all[:, d, i, bass.ds(b, 1), c0:c0 + GW].rearrange("p o t -> p (o t)"),
                                                  start=(d + i == 0), stop=(d + i == 2))
                            filled2(m, "sT", u)
                            o = opened2(pe, b, "s", u)
                            done2(pe, b, "sT", u)
                            for k in range(GT):
                                m = pe.transpose(o[:, k * P:(k + 1) * P], sT[:, k * P:(k + 1) * P], ident[:, :])
                            filled2(m, "s", u)

                    pe.wait_ge(w_mamba, 96)
                    with pe.Fori(0, NT) as c:
                        chunk(c)
                    for d in range(2):
                        o = opened1e(pe, 0, "yT", d)
                        pe.wait_ge(yn_ready, 2 * NT + (d + 1) + START)
                        filled1e(turn_y(d, o), "yT", d)
                    for d in range(2):
                        done1e(pe, 0, "yT", d)
                    pe.wait_ge(setup_ready, 1)
                    with pe.Fori(0, B) as b:
                        last(b)

                @block.scalar
                def _(act):
                    act.wait_ge(alog_ready, 1)
                    act.activation(expA[:, :, :], alog[:, :, :], ACT.Exp).then_inc(expA_ready, 1)
                    act.wait_ge(u_ready, 1)
                    act.activation(u_dt[:, :, :, :, :], u_dt[:, :, :, :, :], ACT.Exp).then_inc(u_made, 1)
                    act.wait_ge(ln_ready, 1)
                    act.activation(l_dt[:, :, :, :, :], w_dt[:, :, :, :, :], ACT.Ln).then_inc(u_made, 1)
                    act.wait_ge(a_ready, 1)
                    act.activation(dA_all[:, :, :, 0:NT, :].rearrange("p d b n h -> p (d b) (n h)"),
                                   r_dt[:, :, :, :, :].rearrange("p d b n h -> p (d b) (n h)"), ACT.Exp).then_inc(dA_ready, 1)
                    act.wait_ge(w_mamba, 96)

                    def squares(c):
                        act.wait_ge(yg_ready, 2 * c + START)
                        for d in range(2):
                            for b in range(B):
                                m = act.activation(ysq[:, d, b, :], yg[:, d, b, :], ACT.Square, scale=ROOT_DI,
                                                   accum_out=ss[:, d, b:b + 1])
                            m.then_inc(ss_ready, 1)

                    def normed(c):
                        for d in range(2):
                            act.wait_ge(rs_ready, 2 * c + (d + 1))
                            for b in range(B):
                                m = act.activation(yn[:, d, b, :], yg[:, d, b, :], ACT.Copy, scale=rs[:, d, b:b + 1])
                            m.then_inc(yn_ready, 1)

                    def chunk(c):
                        def gelu(j):
                            full1(act, c, "h", j)
                            taken1(act.activation(h1T[:, 2 * j:2 * j + 2, :].rearrange("p i t -> p (i t)"), psum1("h", j)[:, :],
                                                  ACT.Gelu), "h", j)

                        full1(act, c, "ohT")
                        taken1(act.activation(ohT[:, :], psum1("ohT")[0:E1, 0:B * P], ACT.Copy), "ohT")
                        squares(c)
                        for d in range(2):
                            full1(act, c, "z", d)
                            taken1(act.activation(zs[:, d, :, :].rearrange("p b i -> p (b i)"), psum1("z", d)[:, :], ACT.Silu),
                                   "z", d)
                        for d in range(2):
                            done1(act, c, "conv", d, 2)
                            done1(act, c, "conv", d, 1)
                            done1(act, c, "conv", d, 0)
                            act.activation(xs[:, d, :, :, :], cv[:, d, 0:2, :, :], ACT.Silu)
                            act.activation(BT[:, d, :, :], cv[0:MN, d, 2, :, :], ACT.Silu)
                            act.activation(CT[:, d, :, :], cv[MN:2 * MN, d, 2, :, :], ACT.Silu).then_inc(bc_ready, 1)
                            if d == 0:
                                gelu(0)
                        normed(c)

                        gelu(1)
                        full1(act, c, "P")
                        act.activation(Pc[:, :, :, :].rearrange("p d b h -> p (d b h)"), psum1("P")[:, 0:16], ACT.Copy)
                        taken1(act.activation(Pend[:, :, :, :].rearrange("p d b h -> p (d b h)"), psum1("P")[0:MN, 16:32],
                                              ACT.Copy), "P")
                        for d in range(2):
                            act.wait_ge(xD_ready, 2 * c + START)
                            for b in range(B):
                                full1(act, c, "tr", d, b)
                                act.activation(xtok[:, d, b, :], psum1("tr", d, b)[:, 0:DI], ACT.Copy)
                                taken1(act.activation(Btok[:, d, b, :], psum1("tr", d, b)[:, DI:DI + MN], ACT.Copy),
                                       "tr", d, b)
                        for d in range(2):
                            full1(act, c, "yT", d)
                            taken1(put_y(d, c if d == 0 else NT - c, psum1("yT", d)), "yT", d)
                        act.wait_ge(g_ready, c + 1)
                        act.activation(th1[:, :, :], yh_c[:, :, :], ACT.Tanh, scale=0.5).then_inc(th1_ready, 1)

                    def put_y(d, slot, o):
                        dst = yT_all[:, d, :, :, :].rearrange("p i b (n t) -> p (i b) n t", t=P)[:, :, bass.ds(slot, 1), :]
                        return act.activation(dst.rearrange("p q o t -> p q (o t)"),
                                              o[:, :].rearrange("p (q t) -> p q t", q=4), ACT.Copy)

                    act.wait_ge(yg_zero, 1)
                    with act.Fori(0, NT) as c:
                        chunk(c)
                    squares(NT)
                    normed(NT)
                    for d in range(2):
                        full1e(act, 0, "yT", d)
                        taken1e(put_y(d, NT if d == 0 else 0, psum1e("yT", d)), "yT", d)

                    def last(b):
                        for u in range(NG):
                            full2(act, b, "sT", u)
                            taken2(act.activation(sT[:, :], psum2("sT", u)[:, :], ACT.Copy), "sT", u)

                    with act.Fori(0, B) as b:
                        last(b)

                @block.gpsimd
                def _(pool):
                    def load_x(c):
                        for d, src in enumerate((xTf_all, xTr_all)):
                            pool.tensor_copy(xc[:, d, :, :], src[:, :, bass.ds(c * P, CW)])
                        pool.tensor_copy(oh_c[:, :, :], oh_all[:, :, bass.ds(c, 1), :].rearrange("p b o e -> p b (o e)")
                                         ).then_inc(xc_ready, 1)

                    def load_dt(c):
                        for dst, src in ((dt_c, dt_all), (dA_c, dA_all), (dAz_c, dAz_all)):
                            m = pool.tensor_copy(dst[:, :, :, :].rearrange("p d b h -> p (d b) h"),
                                                 src[:, :, :, bass.ds(c, 1), :].rearrange("p d b o h -> p (d b) (o h)"))
                        m.then_inc(chunk_ready, 1)

                    for h in range(MH):
                        m = pool.tensor_copy(ident4[:, h, :], ident[:, :])
                    m.then_inc(ident4_ready, 1)
                    for t in (dt_all, dA_all, dAz_all):
                        pool.memset(t[:, :, :, NT, :], 0.0)
                    pool.memset(oh_all[:, :, NT, :], 0.0)
                    pool.memset(eps_b[:, :], 1e-5)
                    pool.memset(yg[:, :, :, :], 0.0).then_inc(yg_zero, 1)
                    pool.wait_ge(oh_all_ready, 1)
                    load_x(0)
                    pool.wait_ge(setup_ready, 1)
                    load_dt(0)

                    def roots(c):
                        for d in range(2):
                            pool.wait_ge(ss_ready, 2 * c + (d + 1))
                            pool.tensor_tensor(ms[:, d, :], ss[:, d, :], eps_b[:, :], ALU.add).then_inc(pool1, 1)
                            pool.wait_ge(pool1, 4 * c + (d + 1) + START)
                            pool.tensor_tensor(rs[:, d, :], ms[:, d, :], minus_half[:, 0:B], ALU.pow).then_inc(rs_ready, 1)

                    def chunk(c):
                        roots(c)
                        pool.wait_ge(chunk_ready, c + 1)
                        for d in range(2):
                            for b in range(B):
                                done1(pool, c, "tr", d, b)
                            full1(pool, c, "S", d, before=1)
                            pool.tensor_tensor(heads(xdt[:, d, :, :]), heads(xtok[:, d, :, :]), per_head(dt_c[:, d, :, :]),
                                               ALU.mult).then_inc(xdt_ready, 1)
                            pool.wait_ge(xdt_ready, 2 * c + (d + 1))
                            for b in range(B):
                                done1(pool, c, "L", d, b)
                            end = Lm[:, d, :, :, P - 1].rearrange("p b h -> p (b h)").unsqueeze(2).broadcast_to([P, B * MH, HD])
                            pool.tensor_tensor(heads(xE[:, d, :, :]), heads(xdt[:, d, :, :]), end, ALU.mult
                                               ).then_inc(xE_ready, 1)
                            pool.tensor_tensor(heads(xD[:, d, :, :]), heads(xtok[:, d, :, :]), per_head(dskip2[:, d, :, :]),
                                               ALU.mult).then_inc(xD_ready, 1)
                        done1(pool, c, "z", 0)
                        done1(pool, c, "z", 1)
                        done1(pool, c, "mask", 0)
                        done1(pool, c, "mask", 1)
                        done1(pool, c, "ohT")
                        load_x(c + 1)
                        done1(pool, c, "P")
                        full1(pool, c, "L", 1, 1)
                        load_dt(c + 1)
                        pool.wait_ge(ve1_ready, c + 1)
                        pool.tensor_tensor(rstd1[:, :], ve1[:, :], minus_half[:, 0:B], ALU.pow).then_inc(rstd1_ready, 1)
                        for d in range(2):
                            full1(pool, c, "y", d, B - 1)
                            pool.tensor_tensor(heads(S2[:, d, :, :]), heads(S[:, d, :, :]), per_head(Pend[:, d, :, :]), ALU.mult
                                               ).then_inc(S2_ready, 1)
                        for d in range(2):
                            for b in range(B):
                                done1(pool, c, "y", d, b)
                            pool.wait_ge(xD_ready, 2 * c + 2 + START)
                            pool.wait_ge(yn_ready, 2 * c + (d + 1) + START)
                            pool.tensor_tensor(yg[:, d, :, :], yt[:, d, :, :], xD[:, d, :, :], ALU.add).then_inc(pool1, 1)
                            pool.wait_ge(pool1, 4 * c + (d + 3) + START)
                            done1(pool, c, "z", d)
                            pool.tensor_tensor(yg[:, d, :, :], yg[:, d, :, :], zs[:, d, :, :], ALU.mult).then_inc(yg_ready, 1)

                    with pool.Fori(0, NT) as c:
                        chunk(c)
                    roots(NT)

                @block.vector
                def _(dve):
                    n = [0]

                    def step(ins, chain):
                        ins.then_inc(chain, 1)
                        n[0] += 1
                        return n[0]

                    def setup():
                        def then(ins):
                            dve.wait_ge(dve1, step(ins, dve1))

                        dve.memset(S[:, :, :, :], 0.0)
                        lg = dtf_all[:, :, :, MH:2 * MH].rearrange("p b n e -> p (b n) e")
                        lj = lg.unsqueeze(2).broadcast_to([P, B * NT, E1, E1])
                        le = lg.unsqueeze(3).broadcast_to([P, B * NT, E1, E1])
                        dve.tensor_tensor(rgt[:, :, :, :], lj, le, ALU.is_gt)
                        then(dve.tensor_tensor(req[:, :, :, :], lj, le, ALU.is_equal))
                        bf = before[:, 0:E1, 0:E1].unsqueeze(1).broadcast_to([P, B * NT, E1, E1])
                        then(dve.tensor_tensor(req[:, :, :, :], req[:, :, :, :], bf, ALU.mult))
                        then(dve.tensor_tensor(rgt[:, :, :, :], rgt[:, :, :, :], req[:, :, :, :], ALU.add))
                        then(dve.tensor_reduce(rrank[:, :, :], rgt[:, :, :, :], AX.X, ALU.add))
                        for b in range(B):
                            m = dve.tensor_scalar(oh_all[:, b, 0:NT, :], rrank[:, b * NT:(b + 1) * NT, :], 1.0, None, ALU.is_lt)
                        m.then_inc(oh_all_ready, 1)
                        dve.wait_ge(w_small, 48)
                        dve.tensor_scalar(alog[:, :, :], alog[:, :, :], 88.7, None, ALU.min).then_inc(alog_ready, 1)
                        for d, src in enumerate((dtf_all[:, :, :, 0:MH], dtr_all[:, :, :, :])):
                            bias = dtb[:, d, :].unsqueeze(1).broadcast_to([P, B * NT, MH])
                            m = dve.tensor_tensor(z_dt[:, d, :, :, :].rearrange("p b n h -> p (b n) h"),
                                                  src.rearrange("p b n h -> p (b n) h"), bias, ALU.add)
                        for b in range(B):
                            dve.tensor_copy(dskip2[:, :, b, :], dskip[:, :, :])
                        then(m)
                        f = lambda t: t[:, :, :, 0:NT, :].rearrange("p d b n h -> p (d b) (n h)")
                        dve.scalar_tensor_tensor(out=f(u_dt), in0=f(z_dt), scalar=-1.0, in1=f(z_dt),
                                                 op0=ALU.mult, op1=ALU.min).then_inc(u_ready, 1)
                        dve.wait_ge(u_made, 1)
                        then(dve.tensor_scalar(f(w_dt), f(u_dt), 1.0, None, ALU.add))
                        then(dve.scalar_tensor_tensor(out=f(r_dt), in0=f(w_dt), scalar=-1.0, in1=f(u_dt),
                                                      op0=ALU.add, op1=ALU.subtract))
                        then(dve.reciprocal(f(dt_flat), f(w_dt)))
                        then(dve.tensor_tensor(f(r_dt), f(r_dt), f(dt_flat), ALU.mult))
                        dve.tensor_scalar(f(z_dt), f(z_dt), 0.0, None, ALU.max).then_inc(ln_ready, 1)
                        dve.wait_ge(ln_ready, 1)
                        then(dve.tensor_tensor(f(z_dt), f(z_dt), f(r_dt), ALU.subtract))
                        dve.wait_ge(u_made, 2)
                        dve.tensor_tensor(f(dt_all), f(z_dt), f(l_dt), ALU.add)
                        then(dve.tensor_tensor(f(dt_flat), f(z_dt), f(l_dt), ALU.add))
                        dve.wait_ge(expA_ready, 1)
                        for d in range(2):
                            m = dve.scalar_tensor_tensor(out=r_dt[:, d, :, :, :].rearrange("p b n h -> p (b n) h"),
                                                         in0=dt_flat[:, d, :, :, :].rearrange("p b n h -> p (b n) h"), scalar=1.0 / HUGE,
                                                         in1=expA[:, d, :].unsqueeze(1).broadcast_to([P, B * NT, MH]),
                                                         op0=ALU.mult, op1=ALU.mult)
                        then(m)
                        dve.tensor_scalar(f(r_dt), f(r_dt), 120.0 / HUGE, -HUGE, ALU.min, ALU.mult).then_inc(a_ready, 1)
                        dve.wait_ge(w_mamba, 96)
                        for d in range(2):
                            for i in range(2):
                                dve.tensor_scalar(outw[:, d, i, :], outw[:, d, i, :], normw[:, d, i:i + 1], None, ALU.mult)
                        dve.wait_ge(dA_ready, 1)
                        then(dve.tensor_copy(f(dAz_all), f(dA_all)))
                        dve.memset(dAz_all[0:1, :, :, 0:NT, :], 0.0).then_inc(setup_ready, 1)

                    setup()
                    dve.wait_ge(ident4_ready, 1)
                    n[0] = 0
                    CHUNK_STEPS = 3 * 3 * 2 + 2 * 2 + 6

                    def chunk(c):
                        def after(count):
                            dve.wait_ge(dve2, c * CHUNK_STEPS + count)

                        xf = xc[:, 0, :, TAP - 1:CW]
                        for j in range(2):
                            full1(dve, c, "mask", j)
                            for ee in range(2):
                                m = dve.tensor_tensor(xm[:, 2 * j + ee, :].rearrange("p (b t) -> p b t", b=B),
                                                      psum1("mask", j)[:, ee * B * P:(ee + 1) * B * P].rearrange(
                                                          "p (b t) -> p b t", b=B), xf, ALU.mult)
                            taken1(m, "mask", j)
                        dve.wait_ge(bc_ready, 2 * c + START)
                        for d in range(2):
                            for tap in range(TAP):
                                for i in range(3):
                                    if tap:
                                        after(9 * d + 3 * (tap - 1) + i + 1)
                                    else:
                                        full1(dve, c, "conv", d, i)
                                    src = psum1("conv", d, i)[:, 0:B * CW].rearrange("p (b t) -> p b t", b=B)[:, :, tap:tap + P]
                                    w = convw[:, d, i, tap:tap + 1]
                                    if tap == 0:
                                        step(dve.tensor_scalar(cv[:, d, i, :, :], src, w, convb[:, d, i:i + 1],
                                                               ALU.mult, ALU.add), dve2)
                                        continue
                                    m = dve.scalar_tensor_tensor(out=cv[:, d, i, :, :], in0=src, scalar=w,
                                                                 in1=cv[:, d, i, :, :], op0=ALU.mult, op1=ALU.add)
                                    if tap < TAP - 1:
                                        step(m, dve2)
                                    else:
                                        taken1(m, "conv", d, i)
                        for d in range(2):
                            for b in range(B):
                                full1(dve, c, "L", d, b)
                                if b == 0:
                                    full1(dve, c, "P", before=1)
                                    dve.wait_ge(xE_ready, 2 * c + START)
                                m = dve.tensor_tensor_scan(Lm[:, d, b, :, :].rearrange("s h t -> s (h t)"),
                                                           psum1("L", d, b)[:, :], ident4[:, :, :].rearrange("s h t -> s (h t)"),
                                                           0.0, ALU.mult, ALU.add)
                                taken1(m, "L", d, b)
                            done1(dve, c, "L", d, 0)
                            done1(dve, c, "L", d, 1)
                            dve.tensor_tensor(prow[0:1, d, :, :], dA_c[0:1, d, :, :], Lm[0:1, d, :, :, P - 1], ALU.mult
                                              ).then_inc(prow_ready, 1)
                        full1(dve, c, "G")
                        for d in range(2):
                            for b in range(B):
                                q = (2 * d + b) * P
                                g = psum1("G")[:, q:q + P].unsqueeze(1).broadcast_to([P, MH, P])
                                m = dve.tensor_tensor(Mm[:, d, b, :, :], g, Lm[:, d, b, :, :], ALU.mult)
                            if d == 0:
                                m.then_inc(Mm_ready, 1)
                            else:
                                taken1(m, "G")
                        rows = lambda w: w[:, :].unsqueeze(1).broadcast_to([P, B, D])
                        full1(dve, c, "ffn")
                        dve.wait_ge(w_last, 96)
                        taken1(dve.tensor_tensor(y_c[:, :, :], psum1("ffn")[:, 0:B * D].rearrange("t (b d) -> t b d", b=B),
                                                 rows(bo_b), ALU.add), "ffn")
                        def outputs(d):
                            done1(dve, c, "P")
                            dve.wait_ge(pool1, 4 * c + START)
                            for b in range(B):
                                full1(dve, c, "y", d, b)
                                y = psum1("y", d, b)
                                after(step(dve.tensor_tensor(yt[:, d, b, :].rearrange("p (h i) -> p h i", i=HD),
                                                             y[:, DI:2 * DI].rearrange("p (h i) -> p h i", i=HD),
                                                             Pc[:, d, b, :].unsqueeze(2).broadcast_to([P, MH, HD]), ALU.mult), dve2))
                                taken1(dve.tensor_tensor(yt[:, d, b, :], y[:, 0:DI], yt[:, d, b, :], ALU.add), "y", d, b)
                            full1(dve, c, "S", d)
                            dve.wait_ge(S2_ready, 2 * c + (d + 1))
                            taken1(dve.tensor_tensor(S[:, d, :, :].rearrange("p b i -> p (b i)"), psum1("S", d)[0:MN, :],
                                                     S2[:, d, :, :].rearrange("p b i -> p (b i)"), ALU.add), "S", d)

                        done1(dve, c, "ffn")
                        then = lambda m: after(step(m, dve2))
                        then(dve.tensor_tensor(y_c[:, :, :], y_c[:, :, :],
                                               xn2_all[:, :, bass.ds(c, 1), :].rearrange("p b o d -> p b (o d)"), ALU.add))
                        for b in range(B):
                            m = dve.bn_stats(stats1[:, b, :], y_c[:, b, :])
                        then(m)
                        mean_and_variance(dve, stats1, mean1, part1, ve1, 1e-12, then).then_inc(ve1_ready, 1)
                        outputs(0)
                        dve.wait_ge(rstd1_ready, c + 1)
                        for b in range(B):
                            m = dve.tensor_scalar(yh_c[:, b, :], y_c[:, b, :], mean1[:, b:b + 1], rstd1[:, b:b + 1],
                                                  ALU.subtract, ALU.mult)
                        then(m)
                        then(dve.tensor_tensor(yh_c[:, :, :], yh_c[:, :, :], rows(gamma_b), ALU.mult))
                        dve.tensor_tensor(yh_c[:, :, :], yh_c[:, :, :], rows(beta_b), ALU.add).then_inc(g_ready, 1)
                        outputs(1)
                        dve.wait_ge(th1_ready, c + 1)
                        dve.scalar_tensor_tensor(out=g_all[:, :, bass.ds(c, 1), :].rearrange("p b o d -> p b (o d)"),
                                                 in0=th1[:, :, :], scalar=1.0, in1=yh_c[:, :, :], op0=ALU.add, op1=ALU.mult)

                    with dve.Fori(0, NT) as c:
                        chunk(c)
                    assert n[0] == CHUNK_STEPS, n[0]
                    n[0] = 0

                    def last(b):
                        for u in range(NG):
                            full2(dve, b, "s", u)
                            dve.wait_ge(out_ready, b * NG + u + START)
                            taken2(dve.tensor_tensor(sg1[:, :, :], psum2("s", u)[:, :].rearrange("t (k d) -> t k d", k=GT),
                                                     g_all[:, b, u * GT:(u + 1) * GT, :], ALU.mult), "s", u)
                            done2(dve, b, "s", u)
                            dve.wait_ge(out_stored[u], 16 * b + 16)
                            dve.scalar_tensor_tensor(out=out_g[:, u, :, :], in0=sg1[:, :, :], scalar=0.5,
                                                     in1=x_all[:, b * NG + (u + 1), :, :], op0=ALU.mult, op1=ALU.add
                                                     ).then_inc(out_ready, 1)

                    with dve.Fori(0, B) as b:
                        last(b)




def layouts(i):
    import numpy as np

    c = np.ascontiguousarray
    both = lambda n: (i["L1_attn_f_" + n], i["L1_attn_b_" + n])
    xbc = slice(DI, 2 * DI + 2 * MN)
    iw = both("in_w")
    dt = slice(2 * DI + 2 * MN, None)
    return {
        "x": i["L0_attn_x"], "w_qkv": i["L0_attn_w_qkv"], "w_gate": i["L0_attn_w_gate"],
        "w_out": c(i["L0_attn_w_out"].reshape(NP, P, D).transpose(1, 0, 2)),
        "wg": c(i["L0_ffn_Wg"].T), "bg": i["L0_ffn_bg"], "bias": i["L0_ffn_bias"],
        "w1": c(i["L0_ffn_W1"].transpose(0, 2, 1)), "ws1": c(i["L0_ffn_Ws1"].T),
        "w2": c(i["L0_ffn_W2"].reshape(E0, D, HT, P).transpose(0, 3, 2, 1)),
        "ws2": c(i["L0_ffn_Ws2"].reshape(D, HT, P).transpose(2, 1, 0)),
        "b1": c(i["L0_ffn_b1"].reshape(E0, HT, P).transpose(2, 0, 1)),
        "bs1": c(i["L0_ffn_bs1"].reshape(HT, P).T), "b2": i["L0_ffn_b2"], "bs2": i["L0_ffn_bs2"].reshape(1, D),
        "inw": c(np.stack([w[xbc].T for w in iw], 1)),
        "zw": c(np.stack([w[0:DI].T for w in iw], 1)),
        "dtw": c(np.concatenate([iw[0][dt].T, i["L1_ffn_W_router"], iw[1][dt].T], 1)),
        "convw": c(np.stack([w.reshape(3, P, TAP).transpose(1, 0, 2) for w in both("conv_w")], 1)),
        "convb": c(np.stack([w.reshape(3, P).T for w in both("conv_b")], 1)),
        "dt_bias": c(np.stack(both("dt_bias"))), "A_log": c(np.stack(both("A_log"))), "Dp": c(np.stack(both("Dp"))),
        "outw": c(np.stack([w.T.reshape(2, P, D).transpose(1, 0, 2) for w in both("out_w")], 1)),
        "normw": c(np.stack([w.reshape(2, P).T for w in both("norm_w")], 1)),
        "e1w1": c(i["L1_ffn_W1"].transpose(1, 0, 2)), "e1b1": i["L1_ffn_b1"],
        "e1wo": c(i["L1_ffn_Wo"].reshape(HT, P, D).transpose(1, 0, 2)),
        "bo": i["L1_ffn_bo"], "gamma": i["L1_ffn_ln_gamma"], "beta": i["L1_ffn_ln_beta"],
    }


def kernel(**inputs):
    import numpy as np
    import concourse.bacc as bacc
    from concourse.bass_utils import run_bass_kernel_spmd

    nc = bacc.Bacc("TRN2", target_bir_lowering=False, num_devices=1)
    arrays = layouts({n: np.asarray(v) for n, v in inputs.items()})
    a = {n: nc.dram_tensor(f"in_{n}", v.shape, mybir.dt.from_np(v.dtype), kind="ExternalInput").ap()
         for n, v in arrays.items()}
    out = nc.dram_tensor("out_x", (B, T, D), F32, kind="ExternalOutput").ap()
    build(nc, a, out)
    r = run_bass_kernel_spmd(nc, [{f"in_{n}": v for n, v in arrays.items()}], core_ids=[0])
    return r.results[0]["out_x"]
```

```python
from contextlib import ExitStack

import concourse.bass as bass
from concourse import mybir

F32 = mybir.dt.float32
BF16 = mybir.dt.bfloat16
ALU = mybir.AluOpType
ACT = mybir.ActivationFunctionType
AX = mybir.AxisListType

P = 128
B, T, D = 2, 1024, 128
NT = T // P
GT = 4
GW = GT * P
NG = NT // GT
H, HD = 16, 64
NP = H // 2
E0, HT = 8, 4
HA = HD + 1
E1 = 4
MH, MN = 4, 64
DI = MH * 64
MEAN_ROOT = DI ** -0.5
TAP = 4
CW = P + TAP - 1
NB = 8
PARTS, PW = 3, 32
HUGE = 2.0 ** 64
START = 1
SKIP = None
DT_AT = 3
STATS_AT, NORM_AT, XT_AT, ROUTER_AT, TOP_AT = 1, 2, 4, 5, 6


class Jobs:

    def __init__(self, names, base):
        self.at, self.per = {}, [0] * NB
        for i, name in enumerate(names):
            if name is not SKIP:
                assert name not in self.at
                self.at[name] = i % NB, self.per[i % NB]
                self.per[i % NB] += 1
        self.names = names
        self.base = base

    def bank(self, name):
        return self.at[name][0]

    def count(self, name, it, before=0):
        k, n = self.at[name]
        return it * self.per[k] + (self.base[k] + n + 1 - before * self.per[k])

    def reopened(self, name, by):
        return self.names.index(by) - self.names.index(name) > NB

    def after(self, iterations):
        return [b + iterations * n for b, n in zip(self.base, self.per)]


def attention_jobs():
    names = []
    for u in range(NG):
        names += [("gate", u, k, i) for k in range(GT) for i in range(2)]
        names += [("x2f", u), ("x2r", u), ("wT", u)]
        for j in range(2 * NP):
            names += [("qk", u, j)]
            if j == DT_AT:
                names += [("dt", u)]
            if j % 2:
                names += [("v", u, j // 4, j // 2 % 2)]
        names += [("bias2", u)]
        for p in range(NP):
            if p == XT_AT:
                names += [("xT", u)]
            if p == ROUTER_AT:
                names += [("router", u)]
            names += [("kt", u, p), ("score", u, p, 0), ("score", u, p, 1), ("h", u, p, 0), ("h", u, p, 1),
                      ("kv", u, p, 0), ("kv", u, p, 1), ("h", u, p, 2), ("h", u, p, 3)]
            if p:
                names += [("oT", u, p - 1)]
            names += [("o", u, p, 0), ("o", u, p, 1), ("ffn", u, p)]
        names += [("h", u, E0, i) for i in range(HT)]
        names += [("oT", u, NP - 1), ("ffn", u, E0), ("attn", u)]
    return names


def mamba_jobs():
    names = [("ohT",), ("z", 0), ("z", 1), ("mask", 0), ("mask", 1)]
    names += [("conv", 0, i) for i in range(3)] + [("h", 0)] + [("conv", 1, i) for i in range(3)]
    names += [("L", 0, 0), ("L", 0, 1), ("L", 1, 0), ("h", 1), ("L", 1, 1)]
    names += [("tr", 0, 0), ("tr", 0, 1), ("G",), ("tr", 1, 0), ("tr", 1, 1)]
    names += [("yT", 0), ("yT", 1), ("ffn",)]
    for d in range(2):
        names += [("y", d, b) for b in range(B)]
        names += [("S", d)]
    return names + [SKIP]


EARLY = 4
LAST = [(b, tiles) for b in range(B) for tiles in ((1, 2, 3), (4, 5, 6))] + [(b, (0, NT - 1)) for b in range(B)]


def mean_and_variance(dve, stats, mean, part, var_eps, eps, then):
    even, odd = stats[:, :, 1], stats[:, :, 4]
    dve.tensor_tensor(part[:, 0, :], even, odd, ALU.subtract)
    dve.tensor_tensor(part[:, 1, :], stats[:, :, 2], stats[:, :, 5], ALU.add)
    then(dve.tensor_tensor(mean[:, :], even, odd, ALU.add))
    dve.tensor_tensor(part[:, 0, :], part[:, 0, :], part[:, 0, :], ALU.mult)
    dve.tensor_scalar(mean[:, :], mean[:, :], 0.5, None, ALU.mult)
    then(dve.tensor_scalar(part[:, 1, :], part[:, 1, :], 1.0 / D, eps, ALU.mult, ALU.add))
    return dve.scalar_tensor_tensor(out=var_eps[:, :], in0=part[:, 0, :], scalar=0.25, in1=part[:, 1, :],
                                    op0=ALU.mult, op1=ALU.add)


def build(nc, a, out):
    pairs_ready = NP * NG
    with ExitStack() as ctx:
        def sb(name, *shape, stack=ctx, dt=F32):
            return stack.enter_context(nc.sbuf_tensor(name, list(shape), dt))

        def sem(name):
            return ctx.enter_context(nc.semaphore(name))

        bank = [ctx.enter_context(nc.psum_tensor(f"bank{k}", [P, 512], F32)) for k in range(NB)]
        bank_full = [sem(f"bank_full{k}") for k in range(NB)]
        bank_done = [sem(f"bank_done{k}") for k in range(NB)]

        x_all = sb("x_all", P, 1 + B * NG, GT, D)
        xn2_all = sb("xn2_all", P, B, NT, D)
        xTf_all = sb("xTf_all", P, B, TAP - 1 + T + P)
        xTr_all = sb("xTr_all", P, B, TAP - 1 + T + P)
        dtf_all = sb("dtf_all", P, B, NT, 2 * MH)
        dtr_all = sb("dtr_all", P, B, NT, MH)
        ident = sb("ident", P, P)
        flip = sb("flip", P, P)
        causal = sb("causal", P, P)
        ones = sb("ones", P, P)
        before = sb("before", P, 8, 8)
        minus_half = sb("minus_half", P, 8)
        dtb = sb("dtb", P, 2, MH)
        alog = sb("alog", P, 2, MH)
        dskip = sb("dskip", P, 2, MH)
        sel = sb("sel", PARTS * PW, E1, P, dt=BF16)
        dtw = sb("dtw", P, 3 * MH)

        const_ready = sem("const_ready")
        first_x_loaded = sem("first_x_loaded")
        x_loaded, qkv_loaded, gate_loaded, router_loaded, ffn_loaded, biases_loaded, wout_loaded = (sem(n) for n in (
            "x_loaded", "qkv_loaded", "gate_loaded", "router_loaded", "ffn_loaded", "b_loaded", "wout_loaded"))
        dtw_loaded, heads_loaded = sem("dtw_loaded"), sem("heads_loaded")

        ahead = {n: sem(n) for n in ("og_ready", "x1_ready", "pool_copied", "xE_ready", "yn_ready", "yg_ready",
                                     "xD_ready", "pool_steps", "bc_ready")}
        og_ready, x1_ready, pool_copied, xE_ready, yn_ready, yg_ready, xD_ready, pool_steps, bc_ready = ahead.values()
        out_ready, out_stored = sem("out_ready"), sem("out_stored")

        L0 = Jobs(attention_jobs(), None)
        L0s = Jobs([("xT", 0), ("router", 0)], L0.per)
        L0.base = L0s.after(1)
        L0e = Jobs([("x2f", 0), ("x2r", 0), ("dt", 0)], L0.after(B))
        L1s = Jobs([("sums",)], L0e.after(1))
        L1 = Jobs(mamba_jobs(), L1s.after(1))
        last = [("s", n) for n in range(len(LAST))]
        L2 = Jobs(last[:EARLY] + [("yT", 0), ("yT", 1)] + last[EARLY:], L1.after(NT))

        def awaiting(jobs):
            def await_full(eng, it, *name, before=0):
                eng.wait_ge(bank_full[jobs.bank(name)], jobs.count(name, it, before))

            def await_done(eng, it, *name, before=0):
                eng.wait_ge(bank_done[jobs.bank(name)], jobs.count(name, it, before))

            def opened(eng, it, *name):
                k = jobs.bank(name)
                eng.wait_ge(bank_done[k], jobs.count(name, it) - 1)
                return bank[k]

            def psum(*name):
                return bank[jobs.bank(name)]

            def filled(ins, *name):
                ins.then_inc(bank_full[jobs.bank(name)], 1)

            def taken(ins, *name):
                ins.then_inc(bank_done[jobs.bank(name)], 1)

            return await_full, await_done, opened, psum, filled, taken

        with nc.Block() as block:
            @block.gpsimd
            def _(pool):
                pool.memset(ident[:, :], 0.0).then_inc(const_ready, 1)
                pool.memset(minus_half[:, :], -0.5)
                pool.wait_ge(const_ready, 1)
                pool.affine_select(out=ident[:, :], in_=ident[:, :], compare_op=ALU.not_equal, fill=1.0,
                                   base=0, pattern=[[-1, P]], channel_multiplier=1)

            @block.tensor
            def _(pe):
                for k in range(NB):
                    pe.sem_inc(bank_full[k], L0.per[k])

            @block.scalar
            def _(act):
                for k in range(NB):
                    act.sem_inc(bank_done[k], L0.per[k])

            @block.vector
            def _(dve):
                for s in ahead.values():
                    dve.sem_inc(s, START)

            @block.sync
            def _(sp):
                for b in range(B):
                    for u in range(NG):
                        sp.dma_start(x_all[:, b * NG + u + 1, :, :],
                                     a["x"][b, u * GW:(u + 1) * GW, :].rearrange("(k p) d -> p k d", p=P)
                                     ).then_inc(x_loaded if b + u else first_x_loaded, 16)

        with ExitStack() as l0:
            def s0(name, *shape):
                return sb(name, *shape, stack=l0)

            wqkv = s0("wqkv", P, 3 * H * HD)
            wgate = s0("wgate", P, H * HD)
            wout = s0("wout", P, NP, D)
            w1 = s0("w1", P, E0 + 1, 512)
            w2 = s0("w2", P, E0 + 1, HT, D)
            b1 = s0("b1", P, E0 + 1, HT)
            b2 = s0("b2", E0 + 1, D)
            wg = s0("wg", P, E0)
            bg_b = s0("bg_b", P, E0)
            bias_b = s0("bias_b", P, E0)

            xn_g = s0("xn_g", P, GT, D)
            xT_g = s0("xT_g", P, NG, GW)
            stats = s0("stats", P, GT, 6)
            mean = s0("mean", P, GT)
            part = s0("part", P, 2, GT)
            vareps = s0("vareps", P, GT)
            rstd = s0("rstd", P, GT)
            logit = s0("logit", P, GT, E0)
            sexp = logit
            score = s0("score", P, GT, E0)
            gt3 = s0("gt3", P, GT, E0, E0)
            eq3 = s0("eq3", P, GT, E0, E0)
            rank = s0("rank", P, GT, E0)
            w9 = s0("w9", P, NG, GT, E0 + 1)
            wT9 = s0("wT9", E0 + 1, GW)
            ebuf = s0("ebuf", P, 2, GW)
            qT = s0("qT", P, NP, GW)
            kT = s0("kT", P, NP, GW)
            v1 = s0("v1", P, GT, H, HA)
            gate = s0("gate", P, GT, H * HD)
            ktok = s0("ktok", P, GT, P)
            sm = s0("sm", P, 2, GT, P)
            kvc = s0("kvc", P, NP, 2, HA)
            kvw = s0("kvw", P, GT - 1, 2, HA)
            rden = s0("rden", P, GT, 2)
            o_g = s0("o_g", P, GT, P)
            og_g = s0("og_g", P, GT, P)
            oT = qT
            hT = s0("hT", P, HT, GW)
            facc = s0("facc", P, GT, D)
            th = xn_g
            sg = o_g
            x1_g = facc
            xn2_g = s0("xn2_g", P, GT, D)
            x2f_g = s0("x2f_g", P, GW)
            x2r_g = s0("x2r_g", P, GW)

            var_ready, rstd_ready, xn_ready = sem("var_ready"), sem("rstd_ready"), sem("xn_ready")
            var2_ready, rstd2_ready, xn2_ready = sem("var2_ready"), sem("rstd2_ready"), sem("xn2_ready")
            spare_zero, const_filled, masks_ready, flip_ready, sel_ready = (sem(n) for n in (
                "spare_zero", "const_filled", "masks_ready", "flip_ready", "sel_ready"))
            sexp_ready, w9_ready = sem("sexp_ready"), sem("w9_ready")
            exp_ready, kv_ready = sem("exp_ready"), sem("kv_ready")
            th_ready = sem("th_ready")
            dve_steps0 = sem("dve_steps0")
            loop, first, final = awaiting(L0), awaiting(L0s), awaiting(L0e)
            await_full, await_done, opened, psum, filled, taken = loop
            MW = 64

            with nc.Block() as block:
                @block.sync
                def _(sp):
                    sp.dma_start(wg[:, :], a["wg"]).then_inc(router_loaded, 16)
                    sp.dma_start(bg_b[:, :], a["bg"].partition_broadcast(P)).then_inc(router_loaded, 16)
                    sp.dma_start(bias_b[:, :], a["bias"].partition_broadcast(P)).then_inc(router_loaded, 16)
                    sp.dma_start(wgate[:, :], a["w_gate"]).then_inc(gate_loaded, 16)
                    for c in (slice(0, 1536), slice(1536, 3072)):
                        sp.dma_start(wqkv[:, c], a["w_qkv"][:, c]).then_inc(qkv_loaded, 16)
                    sp.dma_start(b1[:, 0:E0, :], a["b1"]).then_inc(biases_loaded, 16)
                    sp.dma_start(b1[:, E0, :], a["bs1"]).then_inc(biases_loaded, 16)
                    sp.dma_start(b2[0:E0, :], a["b2"]).then_inc(biases_loaded, 16)
                    sp.dma_start(b2[E0:E0 + 1, :], a["bs2"]).then_inc(biases_loaded, 16)
                    sp.dma_start(dtw[:, :], a["dtw"]).then_inc(dtw_loaded, 16)
                    for e in range(E0 + 1):
                        sp.dma_start(w1[:, e, :], a["w1"][e] if e < E0 else a["ws1"]).then_inc(ffn_loaded, 16)
                        sp.dma_start(w2[:, e, :, :], a["w2"][e] if e < E0 else a["ws2"]).then_inc(ffn_loaded, 16)
                    sp.wait_ge(ffn_loaded, 16 * 2 * (E0 + 1))
                    sp.dma_start(wout[:, :, :], a["w_out"]).then_inc(wout_loaded, 16)
                    for dst, src in ((dtb, "dt_bias"), (alog, "A_log"), (dskip, "Dp")):
                        sp.dma_start(dst[:, :, :], a[src].partition_broadcast(P)).then_inc(heads_loaded, 16)

                @block.tensor
                def _(pe):
                    def xT_job(jobs, it, u, nth):
                        _, _, opened, _, filled, _ = jobs
                        o = opened(pe, it, "xT", u)
                        pe.wait_ge(xn_ready, nth)
                        for k in range(GT):
                            m = pe.transpose(o[:, k * P:(k + 1) * P], xn_g[:, k, :], ident[:, :])
                        filled(m, "xT", u)

                    def router_job(jobs, it, u, slot):
                        _, await_done, opened, _, filled, _ = jobs
                        await_done(pe, it, "xT", u)
                        pe.wait_ge(router_loaded, 48)
                        o = opened(pe, it, "router", u)
                        for k in range(GT):
                            m = pe.matmul(o[:, k * E0:(k + 1) * E0], xT_g[:, slot, k * P:(k + 1) * P], wg[:, :],
                                          start=True, stop=True)
                        filled(m, "router", u)

                    def x2_jobs(jobs, it, u, nth=None):
                        _, _, opened, _, filled, _ = jobs
                        o = opened(pe, it, "x2f", u)
                        pe.wait_ge(xn2_ready, nth or it * NG + (u + 1))
                        for k in range(GT):
                            m = pe.transpose(o[:, k * P:(k + 1) * P], xn2_g[:, k, :], ident[:, :])
                        filled(m, "x2f", u)
                        o = opened(pe, it, "x2r", u)
                        for k in range(GT):
                            kr = GT - 1 - k
                            m = pe.transpose(o[:, kr * P:(kr + 1) * P], xn2_g[:, k, :], flip[:, :])
                        filled(m, "x2r", u)

                    def dt_job(jobs, it, u):
                        _, await_done, opened, _, filled, _ = jobs
                        o = opened(pe, it, "dt", u)
                        await_done(pe, it, "x2f", u)
                        await_done(pe, it, "x2r", u)
                        pe.wait_ge(dtw_loaded, 16)
                        for k in range(GT):
                            c = slice(k * P, (k + 1) * P)
                            pe.matmul(o[:, 8 * k:8 * k + 8], x2f_g[:, c], dtw[:, 0:8], start=True, stop=True)
                            m = pe.matmul(o[:, 32 + 4 * k:36 + 4 * k], x2r_g[:, c], dtw[:, 8:12],
                                          start=True, stop=True)
                        filled(m, "dt", u)

                    def layer(b):
                        def h_job(u, e, i):
                            pe.wait_ge(ffn_loaded, 32 * (E0 + 1))
                            o = opened(pe, b, "h", u, e, i)
                            filled(pe.matmul(o[:, :], w1[:, e, i * P:(i + 1) * P], xT_g[:, u, :],
                                             start=True, stop=True), "h", u, e, i)

                        def token_job(u, name, w, c0, k, i):
                            o = opened(pe, b, name, u, k, i)
                            filled(pe.matmul(o[:, :], xT_g[:, u, k * P:(k + 1) * P], w[:, c0:c0 + 512],
                                             start=True, stop=True), name, u, k, i)

                        def ffn_job(u, e):
                            o = opened(pe, b, "ffn", u, e)
                            for i in range(HT):
                                await_done(pe, b, "h", u, e, i)
                            for k in range(GT):
                                for i in range(HT):
                                    m = pe.matmul(o[:, k * P:(k + 1) * P], hT[:, i, k * P:(k + 1) * P],
                                                  w2[:, e, i, :], start=(i == 0), stop=(i == HT - 1))
                            filled(m, "ffn", u, e)

                        def oT_job(u, p):
                            o = opened(pe, b, "oT", u, p)
                            pe.wait_ge(og_ready, b * pairs_ready + (u * NP + p + 1) + START)
                            for k in range(GT):
                                m = pe.transpose(o[:, k * P:(k + 1) * P], og_g[:, k, :], ident[:, :])
                            filled(m, "oT", u, p)

                        for u in range(NG):
                            pe.wait_ge(gate_loaded, 16)
                            for k in range(GT):
                                for i in range(2):
                                    token_job(u, "gate", wgate, i * 512, k, i)
                            x2_jobs(loop, b, u)
                            o = opened(pe, b, "wT", u)
                            pe.wait_ge(w9_ready, b * NG + (u + 1))
                            for k in range(GT):
                                m = pe.transpose(o[0:E0 + 1, k * P:(k + 1) * P], w9[:, u, k, :], ident[:, :])
                            filled(m, "wT", u)
                            pe.wait_ge(qkv_loaded, 32)
                            for j in range(2 * NP):
                                o = opened(pe, b, "qk", u, j)
                                c = (j % 2) * H * HD + (j // 2) * P
                                filled(pe.matmul(o[:, :], wqkv[:, c:c + P], xT_g[:, u, :], start=True, stop=True),
                                       "qk", u, j)
                                if j == DT_AT:
                                    dt_job(loop, b, u)
                                if j % 2:
                                    k, i = j // 4, j // 2 % 2
                                    token_job(u, "v", wqkv, 2 * H * HD + i * 512, k, i)
                            o = opened(pe, b, "bias2", u)
                            await_done(pe, b, "wT", u)
                            pe.wait_ge(biases_loaded, 64)
                            for k in range(GT):
                                m = pe.matmul(o[:, k * P:(k + 1) * P], wT9[:, k * P:(k + 1) * P], b2[:, :],
                                              start=True, stop=True)
                            filled(m, "bias2", u)
                            for p in range(NP):
                                if p == XT_AT:
                                    xT_job(loop, b, u, b * NG + (u + 2))
                                if p == ROUTER_AT:
                                    router_job(loop, b, u, 1 - u)
                                assert L0.reopened(("qk", u, 2 * p + 1), ("kt", u, p))
                                o = opened(pe, b, "kt", u, p)
                                for k in range(GT):
                                    m = pe.transpose(o[:, k * P:(k + 1) * P], kT[:, p, k * P:(k + 1) * P],
                                                     ident[:, :])
                                filled(m, "kt", u, p)
                                for hh in range(2):
                                    r = slice(MW * hh, MW * hh + HD)
                                    o = opened(pe, b, "score", u, p, hh)
                                    for k in range(GT):
                                        c = slice(k * P, (k + 1) * P)
                                        m = pe.matmul(o[:, c], kT[r, p, c], qT[r, p, c], start=True, stop=True)
                                    filled(m, "score", u, p, hh)
                                h_job(u, p, 0)
                                h_job(u, p, 1)
                                await_done(pe, b, "kt", u, p)
                                if p == 0:
                                    await_done(pe, b, "v", u, GT - 1, 1)
                                for i in range(2):
                                    o = opened(pe, b, "kv", u, p, i)
                                    for kk in range(2):
                                        k = 2 * i + kk
                                        m = pe.matmul(o[:, kk * 2 * HA:(kk + 1) * 2 * HA], ktok[:, k, :],
                                                      v1[:, k, 2 * p:2 * p + 2, :].rearrange("s h i -> s (h i)"),
                                                      start=True, stop=True)
                                    filled(m, "kv", u, p, i)
                                h_job(u, p, 2)
                                h_job(u, p, 3)
                                if p:
                                    oT_job(u, p - 1)
                                await_done(pe, b, "score", u, p, 0)
                                await_done(pe, b, "score", u, p, 1)
                                pe.wait_ge(kv_ready, b * pairs_ready + (u * NP + p + 1))
                                for i in range(2):
                                    o = opened(pe, b, "o", u, p, i)
                                    for kk in range(2):
                                        k = 2 * i + kk
                                        c = slice(k * P, (k + 1) * P)
                                        state = kvc[:, p, :, :] if k == 0 else kvw[:, k - 1, :, :]
                                        pe.matmul(o[:, kk * 2 * HA:(kk + 1) * 2 * HA], qT[:, p, c],
                                                  state.rearrange("j h i -> j (h i)"), start=True, stop=True)
                                        for hh in range(2):
                                            c0 = (2 * kk + hh) * HA
                                            m = pe.matmul(o[:, c0:c0 + HA], sm[:, hh, k, :], v1[:, k, 2 * p + hh, :],
                                                          start=False, stop=True, skip_group_check=True)
                                    filled(m, "o", u, p, i)
                                ffn_job(u, p)
                            for i in range(HT):
                                h_job(u, E0, i)
                            oT_job(u, NP - 1)
                            ffn_job(u, E0)
                            o = opened(pe, b, "attn", u)
                            await_done(pe, b, "oT", u, NP - 1)
                            pe.wait_ge(wout_loaded, 16)
                            for k in range(GT):
                                for p in range(NP):
                                    m = pe.matmul(o[:, k * P:(k + 1) * P], oT[:, p, k * P:(k + 1) * P],
                                                  wout[:, p, :], start=(p == 0), stop=(p == NP - 1))
                            filled(m, "attn", u)

                    xT_job(first, 0, 0, 1)
                    router_job(first, 0, 0, 0)
                    pe.wait_ge(flip_ready, 1)
                    with pe.Fori(0, B) as b:
                        layer(b)
                    x2_jobs(final, 0, 0, B * NG + 1)
                    dt_job(final, 0, 0)

                @block.scalar
                def _(act):
                    def xT_copy(jobs, it, u, slot):
                        await_full, _, _, psum, _, taken = jobs
                        await_full(act, it, "xT", u)
                        taken(act.activation(xT_g[:, slot, :], psum("xT", u)[:, :], ACT.Copy), "xT", u)

                    def router_exp(jobs, it, u):
                        _, await_done, _, _, _, _ = jobs
                        await_done(act, it, "router", u)
                        act.activation(sexp[:, :, :], logit[:, :, :], ACT.Exp, scale=-1.0).then_inc(sexp_ready, 1)

                    def x2_copies(jobs, it, u, copied):
                        await_full, _, _, psum, _, taken = jobs
                        act.wait_ge(pool_copied, copied + START)
                        await_full(act, it, "x2f", u)
                        taken(act.activation(x2f_g[:, :], psum("x2f", u)[:, :], ACT.Copy), "x2f", u)
                        await_full(act, it, "x2r", u)
                        taken(act.activation(x2r_g[:, :], psum("x2r", u)[:, :], ACT.Copy), "x2r", u)

                    def layer(b):
                        for u in range(NG):
                            act.wait_ge(og_ready, b * pairs_ready + u * NP + START)
                            for k in range(GT):
                                for i in range(2):
                                    await_full(act, b, "gate", u, k, i)
                                    taken(act.activation(gate[:, k, 512 * i:512 * i + 512],
                                                         psum("gate", u, k, i)[:, :], ACT.Sigmoid), "gate", u, k, i)
                            x2_copies(loop, b, u, b * NG + u)
                            await_full(act, b, "wT", u)
                            taken(act.activation(wT9[:, :], psum("wT", u)[0:E0 + 1, :], ACT.Copy), "wT", u)
                            for j in range(2 * NP):
                                await_full(act, b, "qk", u, j)
                                if j >= 2:
                                    await_done(act, b, "qk", u, j - 2)
                                else:
                                    await_done(act, b, "qk", (u + 1) % 2, 2 * NP - 2 + j, before=1 - u)
                                act.activation(ebuf[:, j % 2, :], psum("qk", u, j)[:, :], ACT.Exp
                                               ).then_inc(exp_ready, 1)
                                if j % 2:
                                    k, i = j // 4, j // 2 % 2
                                    await_full(act, b, "v", u, k, i)
                                    src = psum("v", u, k, i)[:, :].rearrange("t (h i) -> t h i", i=HD)
                                    taken(act.activation(v1[:, k, 8 * i:8 * i + 8, 0:HD], src, ACT.Copy),
                                          "v", u, k, i)
                            act.wait_ge(pool_copied, b * NG + (u + 1) + START)
                            await_full(act, b, "bias2", u)
                            taken(act.activation(facc[:, :, :], psum("bias2", u)[:, :].rearrange("t (k d) -> t k d", k=GT),
                                                 ACT.Copy), "bias2", u)

                            def gelu(e, i):
                                await_full(act, b, "h", u, e, i)
                                taken(act.activation(hT[:, i, :], psum("h", u, e, i)[:, :], ACT.Gelu,
                                                     bias=b1[:, e, i:i + 1]), "h", u, e, i)

                            def oT_copy(p):
                                await_full(act, b, "oT", u, p)
                                taken(act.activation(oT[:, p, :], psum("oT", u, p)[:, :], ACT.Copy), "oT", u, p)

                            act.wait_ge(biases_loaded, 64)
                            for p in range(NP):
                                if p == XT_AT:
                                    xT_copy(loop, b, u, 1 - u)
                                await_full(act, b, "kt", u, p)
                                taken(act.activation(ktok[:, :, :], psum("kt", u, p)[:, :].rearrange("t (k d) -> t k d", k=GT),
                                                     ACT.Copy), "kt", u, p)
                                for i in range(HT):
                                    gelu(p, i)
                                if p:
                                    oT_copy(p - 1)
                                if p == ROUTER_AT:
                                    router_exp(loop, b, u)
                            for i in range(HT):
                                gelu(E0, i)
                            oT_copy(NP - 1)
                            await_done(act, b, "ffn", u, E0)
                            act.activation(th[:, :, :], facc[:, :, :], ACT.Tanh, scale=0.5).then_inc(th_ready, 1)

                    xT_copy(first, 0, 0, 0)
                    router_exp(first, 0, 0)
                    with act.Fori(0, B) as b:
                        layer(b)
                    x2_copies(final, 0, 0, B * NG)

                @block.gpsimd
                def _(pool):
                    def root(given, wanted, nth):
                        pool.wait_ge(given, nth)
                        pool.tensor_tensor(rstd[:, :], vareps[:, :], minus_half[:, 0:GT], ALU.pow).then_inc(wanted, 1)

                    def keep(jobs, it, u, nth, slot, b, ub):
                        _, await_done, _, _, _, _ = jobs
                        root(var2_ready, rstd2_ready, nth)
                        pool.tensor_copy(x_all[:, slot, :, :], x1_g[:, :, :])
                        await_done(pool, it, "x2f", u)
                        c0 = TAP - 1 + ub * GW
                        pool.tensor_copy(xTf_all[:, b, c0:c0 + GW], x2f_g[:, :])
                        await_done(pool, it, "x2r", u)
                        c0 = TAP - 1 + (NG - 1 - ub) * GW
                        pool.tensor_copy(xTr_all[:, b, c0:c0 + GW], x2r_g[:, :])
                        pool.wait_ge(xn2_ready, nth)
                        pool.tensor_copy(xn2_all[:, b, ub * GT:(ub + 1) * GT, :], xn2_g[:, :, :]).then_inc(pool_copied, 1)

                    def layer(b):
                        for u in range(NG):
                            keep(loop, b, u, b * NG + (u + 1), b * NG + u, b if u else b * -1 + 1, 1 - u)
                            for p in range(NP):
                                await_done(pool, b, "o", u, p, 0)
                                await_done(pool, b, "o", u, p, 1)
                                if p == 0:
                                    assert L0.reopened(("gate", u, GT - 1, 1), ("o", u, 0, 0))
                                    await_full(pool, b, "oT", 1 - u, NP - 1, before=1 - u)
                                else:
                                    await_full(pool, b, "oT", u, p - 1)
                                pool.tensor_tensor(og_g[:, :, :], o_g[:, :, :], gate[:, :, p * P:(p + 1) * P],
                                                   ALU.mult).then_inc(og_ready, 1)
                                if p == STATS_AT:
                                    root(var_ready, rstd_ready, b * NG + (u + 2))

                    pool.memset(o_g[:, :, :], 0.0)
                    pool.memset(x_all[:, 0, :, :], 0.0).then_inc(spare_zero, 1)
                    sel_src = xn2_all[0:PARTS * PW, 0, 0:E1, :]
                    for t, value in ((flip[:, :], 0.0), (causal[:, :], 1.0), (before[:, :, :], 1.0), (sel_src, 0.0)):
                        pool.memset(t, value).then_inc(const_filled, 1)
                    root(var_ready, rstd_ready, 1)
                    pool.wait_ge(const_filled, 4)
                    pool.affine_select(out=before[:, :, :], in_=before[:, :, :], compare_op=ALU.is_gt, fill=0.0,
                                       base=0, pattern=[[1, 8], [-1, 8]], channel_multiplier=0).then_inc(masks_ready, 1)
                    pool.affine_select(out=causal[:, :], in_=causal[:, :], compare_op=ALU.is_ge, fill=0.0,
                                       base=0, pattern=[[1, P]], channel_multiplier=-1).then_inc(masks_ready, 1)
                    pool.affine_select(out=flip[:, :], in_=flip[:, :], compare_op=ALU.not_equal, fill=1.0,
                                       base=1 - P, pattern=[[1, P]], channel_multiplier=1).then_inc(flip_ready, 1)
                    pool.affine_select(out=sel_src, in_=sel_src, compare_op=ALU.not_equal, fill=1.0,
                                       base=0, pattern=[[-1, E1], [0, P]], channel_multiplier=1).then_inc(sel_ready, 1)
                    pool.memset(ones[:, :], 1.0)
                    for t in (xTf_all, xTr_all):
                        pool.memset(t[:, :, 0:TAP - 1], 0.0)
                        pool.memset(t[:, :, TAP - 1 + T:], 0.0)
                    pool.wait_ge(sel_ready, 1)
                    pool.tensor_copy(sel[:, :, :], sel_src).then_inc(sel_ready, 1)
                    pool.wait_ge(sel_ready, 2)
                    with pool.Fori(0, B) as b:
                        layer(b)
                    keep(final, 0, 0, B * NG + 1, B * NG, B - 1, NG - 1)

                PRO = 3 + 8
                STEPS = 1 + NG * (2 * 3 + 8 + 2 * NP + 4 * NP + 1)

                @block.vector
                def _(dve):
                    n = [0]

                    def step(ins):
                        ins.then_inc(dve_steps0, 1)
                        n[0] += 1
                        return n[0]

                    def after(b, count):
                        dve.wait_ge(dve_steps0, b * STEPS + count)

                    def moments(b, var, src):
                        for k in range(GT):
                            m = dve.bn_stats(stats[:, k, :], src(k))
                        after(b, step(m))
                        mean_and_variance(dve, stats, mean, part, vareps, 1e-5, lambda m: after(b, step(m))
                                          ).then_inc(var, 1)

                    def normalise(nth, root, made, src, dst):
                        dve.wait_ge(root, nth)
                        for k in range(GT):
                            m = dve.tensor_scalar(dst[:, k, :], src(k), mean[:, k:k + 1], rstd[:, k:k + 1],
                                                  ALU.subtract, ALU.mult)
                        m.then_inc(made, 1)

                    def logits(jobs, it, u, b):
                        await_full, _, _, psum, _, taken = jobs
                        await_full(dve, it, "router", u)
                        dve.wait_ge(router_loaded, 48)
                        lg = psum("router", u)[:, 0:GT * E0].rearrange("t (k e) -> t k e", k=GT)
                        after(b, step(dve.tensor_tensor(logit[:, :, :], lg, bg_b[:, :].unsqueeze(1).broadcast_to([P, GT, E0]),
                                                        ALU.add)))
                        taken(dve.tensor_tensor(logit[:, :, :], logit[:, :, :],
                                                bias_b[:, :].unsqueeze(1).broadcast_to([P, GT, E0]), ALU.add), "router", u)

                    def top_two(b, nth, slot):
                        then = lambda m: after(b, step(m))
                        dve.wait_ge(sexp_ready, nth)
                        then(dve.tensor_scalar(sexp[:, :, :], sexp[:, :, :], 1.0, None, ALU.add))
                        then(dve.reciprocal(score[:, :, :], sexp[:, :, :]))
                        sj = score[:, :, :].unsqueeze(2).broadcast_to([P, GT, E0, E0])
                        se = score[:, :, :].unsqueeze(3).broadcast_to([P, GT, E0, E0])
                        step(dve.tensor_tensor(gt3[:, :, :, :], sj, se, ALU.is_gt))
                        then(dve.tensor_tensor(eq3[:, :, :, :], sj, se, ALU.is_equal))
                        bf = before[:, :, :].rearrange("p e j -> p (e j)").unsqueeze(1).broadcast_to([P, GT, E0 * E0])
                        flat = eq3[:, :, :, :].rearrange("p k e j -> p k (e j)")
                        then(dve.tensor_tensor(flat, flat, bf, ALU.mult))
                        then(dve.tensor_tensor(gt3[:, :, :, :], gt3[:, :, :, :], eq3[:, :, :, :], ALU.add))
                        then(dve.tensor_reduce(rank[:, :, :], gt3[:, :, :, :], AX.X, ALU.add))
                        dve.scalar_tensor_tensor(out=w9[:, slot, :, 0:E0], in0=rank[:, :, :], scalar=2.0,
                                                 in1=score[:, :, :], op0=ALU.is_lt, op1=ALU.mult).then_inc(w9_ready, 1)

                    def result(b, nth, slot):
                        dve.wait_ge(pool_copied, nth - 1 + START)
                        dve.scalar_tensor_tensor(out=x1_g[:, :, :], in0=sg[:, :, :], scalar=0.5,
                                                 in1=x_all[:, slot, :, :], op0=ALU.mult, op1=ALU.add).then_inc(x1_ready, 1)
                        dve.wait_ge(x1_ready, nth + START)
                        moments(b, var2_ready, lambda k: x1_g[:, k, :])
                        normalise(nth, rstd2_ready, xn2_ready, lambda k: x1_g[:, k, :], xn2_g)

                    def dt_copies(jobs, it, u, b, ub):
                        await_full, _, _, psum, _, taken = jobs
                        await_full(dve, it, "dt", u)
                        dt, ur = psum("dt", u), NG - 1 - ub
                        dve.tensor_copy(dtf_all[:, b, ub * GT:(ub + 1) * GT, :], dt[:, 0:32].rearrange("t (k c) -> t k c", k=GT))
                        taken(dve.tensor_copy(dtr_all[:, b, ur * GT:(ur + 1) * GT, :],
                                              dt[:, 32:48].rearrange("t (k c) -> t k c", k=GT)), "dt", u)

                    def layer(b):
                        then = lambda m: after(b, step(m))
                        other = b * -1 + 1
                        kvc_zero = step(dve.memset(kvc[:, :, :, :], 0.0))
                        for u in range(NG):
                            result(b, b * NG + (u + 1), b * NG + u)
                            for j in range(2 * NP):
                                dve.wait_ge(exp_ready, b * NG * 2 * NP + (u * 2 * NP + j + 1))
                                then(dve.tensor_scalar(ebuf[:, j % 2, :], ebuf[:, j % 2, :], 1.0, None, ALU.min))
                                dst = (qT, kT)[j % 2]
                                taken(dve.scalar_tensor_tensor(out=dst[:, j // 2, :], in0=psum("qk", u, j)[:, :],
                                                               scalar=1.0, in1=ebuf[:, j % 2, :],
                                                               op0=ALU.add, op1=ALU.max), "qk", u, j)
                                if j == DT_AT:
                                    dt_copies(loop, b, u, b if u else other, 1 - u)

                            def ffn_add(e):
                                if e == 0:
                                    await_done(dve, b, "bias2", u)
                                    dve.wait_ge(w9_ready, b * NG + (u + 1))
                                else:
                                    await_done(dve, b, "ffn", u, e - 1)
                                await_full(dve, b, "ffn", u, e)
                                for k in range(GT):
                                    m = dve.scalar_tensor_tensor(out=facc[:, k, :], in0=psum("ffn", u, e)[:, k * P:(k + 1) * P],
                                                                 scalar=w9[:, u, k, e:e + 1], in1=facc[:, k, :],
                                                                 op0=ALU.mult, op1=ALU.add)
                                taken(m, "ffn", u, e)

                            def add_state(p, k, dst, src):
                                i, kk = k // 2, k % 2
                                for hh in range(2):
                                    r = slice(MW * hh, MW * hh + HD)
                                    c0 = (2 * kk + hh) * HA
                                    m = dve.tensor_tensor(dst[r, hh, :], psum("kv", u, p, i)[r, c0:c0 + HA], src[r, hh, :],
                                                          ALU.add)
                                return m

                            if u == 0:
                                after(b, kvc_zero)
                            for p in range(NP):
                                if p == ROUTER_AT:
                                    logits(loop, b, u, b)
                                for hh in range(2):
                                    await_full(dve, b, "score", u, p, hh)
                                    taken(dve.tensor_tensor(sm[:, hh, :, :],
                                                            psum("score", u, p, hh)[:, :].rearrange("s (k t) -> s k t", k=GT),
                                                            causal[:, :].unsqueeze(1).broadcast_to([P, GT, P]), ALU.mult),
                                          "score", u, p, hh)
                                await_full(dve, b, "kv", u, p, 0)
                                carry = kvc[:, p, :, :]
                                s = step(add_state(p, 0, kvw[:, 0, :, :], carry))
                                after(b, s)
                                m = add_state(p, 1, kvw[:, 1, :, :], kvw[:, 0, :, :])
                                taken(m, "kv", u, p, 0)
                                await_done(dve, b, "kv", u, p, 0)
                                await_full(dve, b, "kv", u, p, 1)
                                add_state(p, 2, kvw[:, 2, :, :], kvw[:, 1, :, :]).then_inc(kv_ready, 1)
                                for i in range(2):
                                    await_full(dve, b, "o", u, p, i)
                                    den = psum("o", u, p, i)[:, 0:4 * HA].rearrange("t (c i) -> t c i", i=HA)[:, :, HD]
                                    s = step(dve.tensor_scalar(rden[:, 2 * i:2 * i + 2, :].rearrange("t k h -> t (k h)"), den,
                                                               1e-6, None, ALU.add))
                                after(b, s)
                                then(dve.reciprocal(rden[:, :, :], rden[:, :, :]))
                                dve.wait_ge(og_ready, b * pairs_ready + (u * NP + p) + START)
                                for i in range(2):
                                    src = psum("o", u, p, i)[:, 0:4 * HA].rearrange("t (c i) -> t c i", i=HA)[:, :, 0:HD]
                                    m = dve.tensor_tensor(
                                        o_g[:, 2 * i:2 * i + 2, :].rearrange("t k (h i) -> t (k h) i", h=2), src,
                                        rden[:, 2 * i:2 * i + 2, :].rearrange("t k h -> t (k h)").unsqueeze(2).broadcast_to([P, 4, HD]),
                                        ALU.mult)
                                    taken(m, "o", u, p, i)
                                await_done(dve, b, "o", u, p, 0)
                                await_done(dve, b, "o", u, p, 1)
                                dve.wait_ge(kv_ready, b * pairs_ready + (u * NP + p + 1))
                                s = add_state(p, 3, kvc[:, p, :, :], kvw[:, 2, :, :])
                                taken(s, "kv", u, p, 1)
                                ffn_add(p)
                                slot = b * NG + (u + 2) if u == 0 else other * NG + 1
                                if p == STATS_AT:
                                    moments(b, var_ready, lambda k: x_all[:, slot, k, :])
                                if p == NORM_AT:
                                    normalise(b * NG + (u + 2), rstd_ready, xn_ready, lambda k: x_all[:, slot, k, :], xn_g)
                                if p == TOP_AT:
                                    top_two(b, b * NG + (u + 2), 1 - u)
                            ffn_add(E0)
                            await_done(dve, b, "ffn", u, E0)
                            dve.wait_ge(th_ready, b * NG + (u + 1))
                            dve.wait_ge(og_ready, b * pairs_ready + (u + 1) * NP + START)
                            then(dve.scalar_tensor_tensor(out=sg[:, :, :], in0=th[:, :, :], scalar=1.0, in1=facc[:, :, :],
                                                          op0=ALU.add, op1=ALU.mult))
                            await_full(dve, b, "attn", u)
                            taken(dve.tensor_tensor(sg[:, :, :], psum("attn", u)[:, :].rearrange("t (k d) -> t k d", k=GT),
                                                    sg[:, :, :], ALU.mult), "attn", u)
                            await_done(dve, b, "attn", u)

                    dve.memset(kvw[:, :, :, :], 0.0)
                    dve.memset(v1[:, :, :, HD:HA], 1.0)
                    dve.memset(w9[:, :, :, E0:E0 + 1], 1.0)
                    dve.wait_ge(first_x_loaded, 16)
                    moments(0, var_ready, lambda k: x_all[:, 1, k, :])
                    normalise(1, rstd_ready, xn_ready, lambda k: x_all[:, 1, k, :], xn_g)
                    logits(first, 0, 0, 0)
                    dve.wait_ge(masks_ready, 2)
                    top_two(0, 1, 0)
                    assert n[0] == PRO, n[0]
                    dve.wait_ge(x_loaded, 16 * (B * NG - 1))
                    dve.wait_ge(spare_zero, 1)
                    with dve.Fori(0, B) as b:
                        layer(b)
                    assert n[0] == PRO + STEPS, n[0]
                    n[0] = PRO
                    result(B, B * NG + 1, B * NG)
                    dt_copies(final, 0, 0, B - 1, NG - 1)

        with ExitStack() as l1:
            def s1(name, *shape, dt=F32):
                return sb(name, *shape, stack=l1, dt=dt)

            ident4 = s1("ident4", P, MH, P)
            inw = s1("inw", P, 2, 3 * P)
            zw = s1("zw", P, 2, DI)
            convw = s1("convw", P, 2, 3, TAP)
            convb = s1("convb", P, 2, 3)
            outw = s1("outw", P, 2, 2, D)
            normw = s1("normw", P, 2, 2)
            e1w1 = s1("e1w1", P, E1, 512)
            b1_src = s1("b1_src", PARTS * PW, 512)
            b1_parts = s1("b1_parts", PARTS * PW, 512, dt=BF16)
            b1_part = s1("b1_part", PARTS * PW, 512, dt=BF16)
            e1wo = s1("e1wo", P, HT, D)
            bo_b = s1("bo_b", P, D)
            gamma_b = s1("gamma_b", P, D)
            beta_b = s1("beta_b", P, D)

            yT_all = s1("yT_all", P, 2, 2, B, T + P)
            g_all = s1("g_all", P, B, NT, D)
            z_dt = s1("z_dt", P, 2, B, NT, MH)
            u_dt = s1("u_dt", P, 2, B, NT, MH)
            w_dt = s1("w_dt", P, 2, B, NT, MH)
            r_dt = s1("r_dt", P, 2, B, NT, MH)
            dt_flat = s1("dt_flat", P, 2, B, NT, MH)
            l_dt = s1("l_dt", P, 2, B, NT, MH)
            dt_all = s1("dt_all", P, 2, B, NT + 1, MH)
            dA_all = s1("dA_all", P, 2, B, NT, MH)
            dAz_all = s1("dAz_all", P, 2, B, NT + 1, MH)
            Pc_all = s1("Pc_all", P, 2, B, NT + 1, MH)
            Pend_all = s1("Pend_all", P, 2, B, NT + 1, MH)
            expA = s1("expA", P, 2, MH)
            dskip2 = s1("dskip2", P, 2, B, MH)
            oh_all = s1("oh_all", P, B, NT + 1, E1)
            rgt = s1("rgt", P, B * NT, E1, E1)
            req = s1("req", P, B * NT, E1, E1)
            rrank = s1("rrank", P, B * NT, E1)

            xc = s1("xc", P, 2, B, CW)
            dt_c = s1("dt_c", P, 2, B, MH)
            Pc = s1("Pc", P, 2, B, MH)
            Pend = s1("Pend", P, 2, B, MH)
            dAz_c = s1("dAz_c", P, 2, B, MH)
            cv = s1("cv", P, 2, 3, B, P)
            xs = s1("xs", P, 2, 2, B, P)
            BT = s1("BT", MN, 2, B, P)
            CT = s1("CT", MN, 2, B, P)
            zs = s1("zs", P, 2, B, DI)
            xtok = s1("xtok", P, 2, B, DI)
            Btok = s1("Btok", P, 2, B, MN)
            Lm = s1("Lm", P, 2, B, MH, P)
            Mm = s1("Mm", P, 2, B, MH, P)
            xdt = s1("xdt", P, 2, B, DI)
            xE = s1("xE", P, 2, B, DI)
            xD = s1("xD", P, 2, B, DI)
            S = s1("S", MN, 2, B, DI)
            S2 = s1("S2", MN, 2, B, DI)
            yt = s1("yt", P, 2, B, DI)
            yg = s1("yg", P, 2, B, DI)
            ysq = s1("ysq", P, 2, B, DI)
            yn = s1("yn", P, 2, B, DI)
            ss = s1("ss", P, 2, B)
            ms = s1("ms", P, 2, B)
            rs = s1("rs", P, 2, B)
            eps_b = s1("eps_b", P, B)
            table = s1("table", P, 1)

            oh_c = s1("oh_c", P, B, PARTS, PW)
            ohT = s1("ohT", PARTS * PW, B * P, dt=BF16)
            xm = s1("xm", P, E1, B * P)
            h1T = s1("h1T", P, HT, B * P)
            y_c = s1("y_c", P, B, D)
            yh_c = s1("yh_c", P, B, D)
            th1 = s1("th1", P, B, D)
            stats1 = s1("stats1", P, B, 6)
            mean1 = s1("mean1", P, B)
            part1 = s1("part1", P, 2, B)
            ve1 = s1("ve1", P, B)
            rstd1 = s1("rstd1", P, B)
            out_all = Mm[:, :, :, :, :].rearrange("p d b h t -> p d (b h) t")

            (mamba_loaded, experts_loaded, u_ready, u_made, ln_ready, a_ready, dA_ready, dve_steps1, dve_steps2) = (sem(n) for n in (
                "mamba_loaded", "experts_loaded", "u_ready", "u_made", "ln_ready", "a_ready", "dA_ready",
                "dve_steps1", "dve_steps2"))
            (alog_ready, expA_ready, outw_ready, chunk_ready, xc_ready, yg_zero, xdt_ready, S2_ready,
             ss_ready, rs_ready, Mm_ready) = (sem(n) for n in (
                "alog_ready", "expA_ready", "outw_ready", "chunk_ready", "xc_ready", "yg_zero", "xdt_ready",
                "S2_ready", "ss_ready", "rs_ready", "Mm_ready"))
            ident4_ready, decays_ready = sem("ident4_ready"), sem("decays_ready")
            (oh_all_ready, ve1_ready, rstd1_ready, g_ready, th1_ready) = (sem(n) for n in (
                "oh_all_ready", "ve1_ready", "rstd1_ready", "g_ready", "th1_ready"))

            fulls, dones, openeds, psums, filleds, takens = awaiting(L1s)
            full1, done1, opened1, psum1, filled1, taken1 = awaiting(L1)
            full2, done2, opened2, psum2, filled2, taken2 = awaiting(L2)
            NDT = 2 * B * NT * MH
            heads = lambda ap: ap.rearrange("p b (h i) -> p (b h) i", i=HD)
            per_head = lambda ap: ap.rearrange("p b h -> p (b h)").unsqueeze(2).broadcast_to([ap.shape[0], B * MH, HD])

            b1_loaded, parts_zero, parts_ready, oh_zero, S_zero = (sem(n) for n in (
                "b1_loaded", "parts_zero", "parts_ready", "oh_zero", "S_zero"))
            with nc.Block() as block:
                @block.sync
                def _(sp):
                    for q in range(PARTS):
                        sp.dma_start(b1_src[q * PW:q * PW + E1, :], a["e1b1"]).then_inc(b1_loaded, 16)
                    for dst, src in ((inw[:, :, :], "inw"), (convw[:, :, :, :], "convw"), (convb[:, :, :], "convb"),
                                     (zw[:, :, :], "zw"), (outw[:, :, :, :], "outw"), (normw[:, :, :], "normw")):
                        sp.dma_start(dst, a[src]).then_inc(mamba_loaded, 16)
                    for dst, src in ((e1w1[:, :, :], "e1w1"), (e1wo[:, :, :], "e1wo")):
                        sp.dma_start(dst, a[src]).then_inc(experts_loaded, 16)
                    for dst, src in ((bo_b, "bo"), (gamma_b, "gamma"), (beta_b, "beta")):
                        sp.dma_start(dst[:, :], a[src].partition_broadcast(P)).then_inc(experts_loaded, 16)
                    for n, (b, tiles) in enumerate(LAST):
                        sp.wait_ge(out_ready, n + 1)
                        t0, step = tiles[0], tiles[1] - tiles[0]
                        for t, k in ([(t0, len(tiles))] if step == 1 else [(t, 1) for t in tiles]):
                            sp.dma_start(out[b, t * P:(t + k) * P, :].rearrange("(k p) d -> p k d", p=P),
                                         out_all[:, b, t:t + k, :]).then_inc(out_stored, 16)
                    sp.wait_ge(out_stored, 16 * sum(1 if tiles[1] - tiles[0] == 1 else 2 for _, tiles in LAST))

                @block.tensor
                def _(pe):
                    def turn_y(d, o):
                        for i in range(2):
                            for b in range(B):
                                m = pe.transpose(o[:, (i * B + b) * P:(i * B + b + 1) * P], yn[:, d, b, i * P:(i + 1) * P],
                                                 (ident, flip)[d][:, :])
                        return m

                    def h_job(c, j):
                        o = opened1(pe, c, "h", j)
                        for ii in range(2):
                            cols, w = slice(ii * B * P, (ii + 1) * B * P), slice((2 * j + ii) * P, (2 * j + ii + 1) * P)
                            for e in range(E1):
                                pe.matmul(o[:, cols], e1w1[:, e, w], xm[:, e, :], start=(e == 0), stop=False)
                            m = pe.matmul(o[:, cols], b1_parts[:, w], ohT[:, :], start=False, stop=True)
                        filled1(m, "h", j)

                    def conv_jobs(c, d):
                        for i in range(3):
                            o = opened1(pe, c, "conv", d, i)
                            filled1(pe.matmul(o[:, 0:B * CW], inw[:, d, i * P:(i + 1) * P],
                                              xc[:, d, :, :].rearrange("p b t -> p (b t)"), start=True, stop=True),
                                    "conv", d, i)

                    def chunk(c):
                        def turn_x(d):
                            pe.wait_ge(bc_ready, 2 * c + (d + 1) + START)
                            for b in range(B):
                                o = opened1(pe, c, "tr", d, b)
                                for i in range(2):
                                    pe.transpose(o[:, i * P:(i + 1) * P], xs[:, d, i, b, :], ident[:, :])
                                filled1(pe.transpose(o[:, DI:DI + MN], BT[:, d, b, :], ident[0:MN, 0:MN]), "tr", d, b)

                        pe.wait_ge(xc_ready, c + 1)
                        o = opened1(pe, c, "ohT")
                        for b in range(B):
                            m = pe.transpose(o[0:PARTS * PW, b * P:(b + 1) * P], oh_c[:, b, :, :].rearrange("p q e -> p (q e)"),
                                             ident[:, :])
                        filled1(m, "ohT")
                        for d in range(2):
                            o = opened1(pe, c, "z", d)
                            for b in range(B):
                                m = pe.matmul(o[:, b * DI:(b + 1) * DI], xc[:, d, b, TAP - 1:CW], zw[:, d, :],
                                              start=True, stop=True)
                            filled1(m, "z", d)
                        done1(pe, c, "ohT")
                        for j in range(2):
                            o = opened1(pe, c, "mask", j)
                            for ee in range(2):
                                m = pe.matmul(o[:, ee * B * P:(ee + 1) * B * P], sel[:, 2 * j + ee, :], ohT[:, :],
                                              start=True, stop=True)
                            filled1(m, "mask", j)
                        conv_jobs(c, 0)
                        pe.wait_ge(experts_loaded, 80)
                        pe.wait_ge(parts_ready, PARTS)
                        done1(pe, c, "mask", 0)
                        done1(pe, c, "mask", 1)
                        h_job(c, 0)
                        conv_jobs(c, 1)
                        pe.wait_ge(chunk_ready, c + 1)
                        for d in range(2):
                            for b in range(B):
                                o = opened1(pe, c, "L", d, b)
                                for h in range(MH):
                                    m = pe.transpose(o[:, h * P:(h + 1) * P],
                                                     dAz_c[:, d, b, h:h + 1].broadcast_to([P, P]), ident[:, :])
                                filled1(m, "L", d, b)
                                if (d, b) == (1, 0):
                                    h_job(c, 1)
                        turn_x(0)
                        pe.wait_ge(bc_ready, 2 * c + 2 + START)
                        o = opened1(pe, c, "G")
                        for d in range(2):
                            for b in range(B):
                                m = pe.matmul(o[:, (2 * d + b) * P:(2 * d + b + 1) * P], BT[:, d, b, :], CT[:, d, b, :],
                                              start=True, stop=True)
                        filled1(m, "G")
                        turn_x(1)
                        for d in range(2):
                            o = opened1(pe, c, "yT", d)
                            pe.wait_ge(yn_ready, 2 * c + (d + 1) + START)
                            filled1(turn_y(d, o), "yT", d)
                        o = opened1(pe, c, "ffn")
                        done1(pe, c, "h", 0)
                        done1(pe, c, "h", 1)
                        for b in range(B):
                            for i in range(HT):
                                m = pe.matmul(o[:, b * D:(b + 1) * D], h1T[:, i, b * P:(b + 1) * P], e1wo[:, i, :],
                                              start=(i == 0), stop=(i == HT - 1))
                        filled1(m, "ffn")
                        for d in range(2):
                            pe.wait_ge(xdt_ready, 2 * c + (d + 1))
                            if d == 0:
                                pe.wait_ge(Mm_ready, c + 1)
                            else:
                                done1(pe, c, "G")
                            done1(pe, c, "S", d, before=1)
                            for b in range(B):
                                o = opened1(pe, c, "y", d, b)
                                for h in range(MH):
                                    pe.matmul(o[:, h * HD:(h + 1) * HD], Mm[:, d, b, h, :], xdt[:, d, b, h * HD:(h + 1) * HD],
                                              start=True, stop=True)
                                filled1(pe.matmul(o[:, DI:2 * DI], CT[:, d, b, :], S[:, d, b, :], start=True, stop=True),
                                        "y", d, b)
                            o = opened1(pe, c, "S", d)
                            pe.wait_ge(xE_ready, 2 * c + (d + 1) + START)
                            for b in range(B):
                                done1(pe, c, "tr", d, b)
                                m = pe.matmul(o[0:MN, b * DI:(b + 1) * DI], Btok[:, d, b, :], xE[:, d, b, :],
                                              start=True, stop=True)
                            filled1(m, "S", d)

                    def last(n):
                        b, tiles = LAST[n]
                        o = opened2(pe, 0, "s", n)
                        for k, t in enumerate(tiles):
                            for d in range(2):
                                c0 = (t + (1 if d == 0 else 0)) * P
                                for i in range(2):
                                    m = pe.matmul(o[:, k * P:(k + 1) * P], yT_all[:, d, i, b, c0:c0 + P], outw[:, d, i, :],
                                                  start=(d + i == 0), stop=(d + i == 2))
                        filled2(m, "s", n)

                    pe.wait_ge(a_ready, 1)
                    o = openeds(pe, 0, "sums")
                    a_all = r_dt[:, :, :, :, :].rearrange("p d b n h -> p (d b n h)")
                    pe.matmul(o[:, 0:NDT], causal[:, :], a_all, start=True, stop=True)
                    filleds(pe.matmul(o[:, NDT:2 * NDT], ones[:, :], a_all, start=True, stop=True), "sums")
                    pe.wait_ge(mamba_loaded, 96)
                    with pe.Fori(0, NT) as c:
                        chunk(c)
                    done1(pe, NT - 1, "yT", 1)
                    pe.wait_ge(outw_ready, 1)
                    for n in range(EARLY):
                        last(n)
                    for d in range(2):
                        o = opened2(pe, 0, "yT", d)
                        pe.wait_ge(yn_ready, 2 * NT + (d + 1) + START)
                        filled2(turn_y(d, o), "yT", d)
                    for d in range(2):
                        done2(pe, 0, "yT", d)
                    for n in range(EARLY, len(LAST)):
                        last(n)

                @block.scalar
                def _(act):
                    act.wait_ge(alog_ready, 1)
                    act.activation(expA[:, :, :], alog[:, :, :], ACT.Exp).then_inc(expA_ready, 1)
                    act.wait_ge(u_ready, 1)
                    act.activation(u_dt[:, :, :, :, :], u_dt[:, :, :, :, :], ACT.Exp).then_inc(u_made, 1)
                    act.wait_ge(ln_ready, 1)
                    act.activation(l_dt[:, :, :, :, :], w_dt[:, :, :, :, :], ACT.Ln).then_inc(u_made, 1)
                    act.wait_ge(a_ready, 1)
                    act.activation(dA_all[:, :, :, :, :].rearrange("p d b n h -> p (d b) (n h)"),
                                   r_dt[:, :, :, :, :].rearrange("p d b n h -> p (d b) (n h)"), ACT.Exp).then_inc(dA_ready, 1)
                    fulls(act, 0, "sums")
                    for k, dst in enumerate((Pc_all, Pend_all)):
                        m = act.activation(dst[:, :, :, 0:NT, :].rearrange("p d b n h -> p (d b) (n h)"),
                                           psums("sums")[:, k * NDT:(k + 1) * NDT].rearrange("p (q n) -> p q n", q=2 * B), ACT.Exp)
                    takens(m, "sums")
                    act.wait_ge(mamba_loaded, 96)

                    def silu_table():
                        act.activation(table[:, :], minus_half[:, 0:1], ACT.Silu)

                    def squares(c):
                        act.wait_ge(yg_ready, 2 * c + START)
                        for d in range(2):
                            for b in range(B):
                                m = act.activation(ysq[:, d, b, :], yg[:, d, b, :], ACT.Square, scale=MEAN_ROOT,
                                                   accum_out=ss[:, d, b:b + 1])
                            m.then_inc(ss_ready, 1)

                    def normed(c):
                        for d in range(2):
                            act.wait_ge(rs_ready, 2 * c + (d + 1))
                            for b in range(B):
                                m = act.activation(yn[:, d, b, :], yg[:, d, b, :], ACT.Copy, scale=rs[:, d, b:b + 1])
                            m.then_inc(yn_ready, 1)

                    def chunk(c):
                        def gelu(j):
                            full1(act, c, "h", j)
                            taken1(act.activation(h1T[:, 2 * j:2 * j + 2, :].rearrange("p i t -> p (i t)"), psum1("h", j)[:, :],
                                                  ACT.Gelu), "h", j)

                        silu_table()
                        full1(act, c, "ohT")
                        taken1(act.activation(ohT[:, :], psum1("ohT")[0:PARTS * PW, 0:B * P], ACT.Copy), "ohT")
                        squares(c)
                        for d in range(2):
                            full1(act, c, "z", d)
                            taken1(act.activation(zs[:, d, :, :].rearrange("p b i -> p (b i)"), psum1("z", d)[:, :], ACT.Silu),
                                   "z", d)
                        normed(c)
                        for d in range(2):
                            for i in range(3):
                                done1(act, c, "conv", d, i)
                            act.activation(xs[:, d, :, :, :], cv[:, d, 0:2, :, :], ACT.Silu)
                            act.activation(BT[:, d, :, :], cv[0:MN, d, 2, :, :], ACT.Silu)
                            act.activation(CT[:, d, :, :], cv[MN:2 * MN, d, 2, :, :], ACT.Silu).then_inc(bc_ready, 1)
                            gelu(d)
                            if d == 0:
                                silu_table()
                        for d in range(2):
                            act.wait_ge(xD_ready, 2 * c + START)
                            for b in range(B):
                                full1(act, c, "tr", d, b)
                                act.activation(xtok[:, d, b, :], psum1("tr", d, b)[:, 0:DI], ACT.Copy)
                                taken1(act.activation(Btok[:, d, b, :], psum1("tr", d, b)[:, DI:DI + MN], ACT.Copy),
                                       "tr", d, b)
                        for d in range(2):
                            full1(act, c, "yT", d)
                            taken1(put_y(d, c if d == 0 else NT - c, psum1("yT", d)), "yT", d)
                        act.wait_ge(g_ready, c + 1)
                        act.activation(th1[:, :, :], yh_c[:, :, :], ACT.Tanh, scale=0.5).then_inc(th1_ready, 1)

                    def put_y(d, slot, o):
                        dst = yT_all[:, d, :, :, :].rearrange("p i b (n t) -> p (i b) n t", t=P)[:, :, bass.ds(slot, 1), :]
                        return act.activation(dst.rearrange("p q o t -> p q (o t)"),
                                              o[:, :].rearrange("p (q t) -> p q t", q=4), ACT.Copy)

                    act.wait_ge(yg_zero, 1)
                    with act.Fori(0, NT) as c:
                        chunk(c)
                    squares(NT)
                    normed(NT)
                    for d in range(2):
                        full2(act, 0, "yT", d)
                        taken2(put_y(d, NT if d == 0 else 0, psum2("yT", d)), "yT", d)

                @block.gpsimd
                def _(pool):
                    def load_x(c):
                        for d, src in enumerate((xTf_all, xTr_all)):
                            pool.tensor_copy(xc[:, d, :, :], src[:, :, bass.ds(c * P, CW)])

                    def load_oh(c):
                        for q in range(PARTS):
                            m = pool.tensor_copy(oh_c[:, :, q, 0:E1], oh_all[:, :, bass.ds(c, 1), :].rearrange("p b o e -> p b (o e)"))
                        m.then_inc(xc_ready, 1)

                    def load_dt(c):
                        for dst, src in ((dt_c, dt_all), (Pc, Pc_all), (Pend, Pend_all), (dAz_c, dAz_all)):
                            m = pool.tensor_copy(dst[:, :, :, :].rearrange("p d b h -> p (d b) h"),
                                                 src[:, :, :, bass.ds(c, 1), :].rearrange("p d b o h -> p (d b) (o h)"))
                        m.then_inc(chunk_ready, 1)

                    for t in (dt_all, Pc_all, Pend_all, dAz_all):
                        pool.memset(t[:, :, :, NT, :], 0.0)
                    pool.memset(oh_all[:, :, NT, :], 0.0)
                    pool.memset(eps_b[:, :], 1e-5)
                    pool.memset(yg[:, :, :, :], 0.0).then_inc(yg_zero, 1)
                    pool.memset(oh_c[:, :, :, :], 0.0).then_inc(oh_zero, 1)
                    pool.memset(S[:, :, :, :], 0.0).then_inc(S_zero, 1)
                    load_x(0)
                    pool.wait_ge(oh_zero, 1)
                    pool.wait_ge(oh_all_ready, 1)
                    load_oh(0)
                    for h in range(MH):
                        m = pool.tensor_copy(ident4[:, h, :], ident[:, :])
                    m.then_inc(ident4_ready, 1)
                    pool.wait_ge(S_zero, 1)
                    pool.wait_ge(decays_ready, 1)
                    dones(pool, 0, "sums")
                    load_dt(0)

                    def roots(c):
                        for d in range(2):
                            pool.wait_ge(ss_ready, 2 * c + (d + 1))
                            pool.tensor_tensor(ms[:, d, :], ss[:, d, :], eps_b[:, :], ALU.add).then_inc(pool_steps, 1)
                            pool.wait_ge(pool_steps, 4 * c + (d + 1) + START)
                            pool.tensor_tensor(rs[:, d, :], ms[:, d, :], minus_half[:, 0:B], ALU.pow).then_inc(rs_ready, 1)

                    def chunk(c):
                        roots(c)
                        pool.wait_ge(chunk_ready, c + 1)
                        for d in range(2):
                            done1(pool, c, "S", d, before=1)
                            pool.tensor_tensor(heads(S2[:, d, :, :]), heads(S[:, d, :, :]), per_head(Pend[0:MN, d, :, :]),
                                               ALU.mult).then_inc(S2_ready, 1)
                        for d in range(2):
                            for b in range(B):
                                done1(pool, c, "tr", d, b)
                            full1(pool, c, "S", d, before=1)
                            pool.tensor_tensor(heads(xdt[:, d, :, :]), heads(xtok[:, d, :, :]), per_head(dt_c[:, d, :, :]),
                                               ALU.mult).then_inc(xdt_ready, 1)
                            pool.wait_ge(xdt_ready, 2 * c + (d + 1))
                            for b in range(B):
                                done1(pool, c, "L", d, b)
                            end = Lm[:, d, :, :, P - 1].rearrange("p b h -> p (b h)").unsqueeze(2).broadcast_to([P, B * MH, HD])
                            pool.tensor_tensor(heads(xE[:, d, :, :]), heads(xdt[:, d, :, :]), end, ALU.mult
                                               ).then_inc(xE_ready, 1)
                        pool.wait_ge(ve1_ready, c + 1)
                        pool.tensor_tensor(rstd1[:, :], ve1[:, :], minus_half[:, 0:B], ALU.pow).then_inc(rstd1_ready, 1)
                        for d in range(2):
                            pool.tensor_tensor(heads(xD[:, d, :, :]), heads(xtok[:, d, :, :]), per_head(dskip2[:, d, :, :]),
                                               ALU.mult).then_inc(xD_ready, 1)
                        done1(pool, c, "z", 0)
                        done1(pool, c, "z", 1)
                        done1(pool, c, "ohT")
                        load_x(c + 1)
                        load_oh(c + 1)
                        for d in range(2):
                            for b in range(B):
                                done1(pool, c, "y", d, b)
                            pool.wait_ge(xD_ready, 2 * c + 2 + START)
                            pool.wait_ge(yn_ready, 2 * c + (d + 1) + START)
                            pool.tensor_tensor(yg[:, d, :, :], yt[:, d, :, :], xD[:, d, :, :], ALU.add).then_inc(pool_steps, 1)
                            pool.wait_ge(pool_steps, 4 * c + (d + 3) + START)
                            done1(pool, c, "z", d)
                            pool.tensor_tensor(yg[:, d, :, :], yg[:, d, :, :], zs[:, d, :, :], ALU.mult).then_inc(yg_ready, 1)

                        full1(pool, c, "L", 1, 1)
                        load_dt(c + 1)

                    with pool.Fori(0, NT) as c:
                        chunk(c)
                    roots(NT)

                @block.vector
                def _(dve):
                    n = [0]

                    def step(ins, chain):
                        ins.then_inc(chain, 1)
                        n[0] += 1
                        return n[0]

                    def setup():
                        def then(ins):
                            dve.wait_ge(dve_steps1, step(ins, dve_steps1))

                        dve.wait_ge(heads_loaded, 48)
                        dve.tensor_scalar(alog[:, :, :], alog[:, :, :], 88.7, None, ALU.min).then_inc(alog_ready, 1)
                        for d, src in enumerate((dtf_all[:, :, :, 0:MH], dtr_all[:, :, :, :])):
                            bias = dtb[:, d, :].unsqueeze(1).broadcast_to([P, B * NT, MH])
                            m = dve.tensor_tensor(z_dt[:, d, :, :, :].rearrange("p b n h -> p (b n) h"),
                                                  src.rearrange("p b n h -> p (b n) h"), bias, ALU.add)
                        for b in range(B):
                            dve.tensor_copy(dskip2[:, :, b, :], dskip[:, :, :])
                        then(m)
                        f = lambda t: t[:, :, :, 0:NT, :].rearrange("p d b n h -> p (d b) (n h)")
                        dve.scalar_tensor_tensor(out=f(u_dt), in0=f(z_dt), scalar=-1.0, in1=f(z_dt),
                                                 op0=ALU.mult, op1=ALU.min).then_inc(u_ready, 1)
                        lg = dtf_all[:, :, :, MH:2 * MH].rearrange("p b n e -> p (b n) e")
                        lj = lg.unsqueeze(2).broadcast_to([P, B * NT, E1, E1])
                        le = lg.unsqueeze(3).broadcast_to([P, B * NT, E1, E1])
                        dve.tensor_tensor(rgt[:, :, :, :], lj, le, ALU.is_gt)
                        then(dve.tensor_tensor(req[:, :, :, :], lj, le, ALU.is_equal))
                        bf = before[:, 0:E1, 0:E1].unsqueeze(1).broadcast_to([P, B * NT, E1, E1])
                        then(dve.tensor_tensor(req[:, :, :, :], req[:, :, :, :], bf, ALU.mult))
                        then(dve.tensor_tensor(rgt[:, :, :, :], rgt[:, :, :, :], req[:, :, :, :], ALU.add))
                        then(dve.tensor_reduce(rrank[:, :, :], rgt[:, :, :, :], AX.X, ALU.add))
                        for b in range(B):
                            m = dve.tensor_scalar(oh_all[:, b, 0:NT, :], rrank[:, b * NT:(b + 1) * NT, :], 1.0, None, ALU.is_lt)
                        m.then_inc(oh_all_ready, 1)
                        dve.wait_ge(u_made, 1)
                        then(dve.tensor_scalar(f(w_dt), f(u_dt), 1.0, None, ALU.add))
                        then(dve.scalar_tensor_tensor(out=f(r_dt), in0=f(w_dt), scalar=-1.0, in1=f(u_dt),
                                                      op0=ALU.add, op1=ALU.subtract))
                        then(dve.reciprocal(f(dt_flat), f(w_dt)))
                        then(dve.tensor_tensor(f(r_dt), f(r_dt), f(dt_flat), ALU.mult))
                        dve.tensor_scalar(f(z_dt), f(z_dt), 0.0, None, ALU.max).then_inc(ln_ready, 1)
                        dve.wait_ge(ln_ready, 1)
                        then(dve.tensor_tensor(f(z_dt), f(z_dt), f(r_dt), ALU.subtract))
                        dve.wait_ge(u_made, 2)
                        dve.tensor_tensor(f(dt_all), f(z_dt), f(l_dt), ALU.add)
                        then(dve.tensor_tensor(f(dt_flat), f(z_dt), f(l_dt), ALU.add))
                        dve.wait_ge(expA_ready, 1)
                        for d in range(2):
                            m = dve.scalar_tensor_tensor(out=r_dt[:, d, :, :, :].rearrange("p b n h -> p (b n) h"),
                                                         in0=dt_flat[:, d, :, :, :].rearrange("p b n h -> p (b n) h"), scalar=1.0 / HUGE,
                                                         in1=expA[:, d, :].unsqueeze(1).broadcast_to([P, B * NT, MH]),
                                                         op0=ALU.mult, op1=ALU.mult)
                        then(m)
                        dve.tensor_scalar(f(r_dt), f(r_dt), 120.0 / HUGE, -HUGE, ALU.min, ALU.mult).then_inc(a_ready, 1)
                        dve.memset(b1_parts[:, :], 0.0).then_inc(parts_zero, 1)
                        dve.wait_ge(dA_ready, 1)
                        then(dve.tensor_copy(f(dAz_all), f(dA_all)))
                        dve.memset(dAz_all[0:1, :, :, 0:NT, :], 0.0).then_inc(decays_ready, 1)
                        dve.wait_ge(b1_loaded, 16 * PARTS)
                        dve.wait_ge(parts_zero, 1)
                        rows = [slice(q * PW, q * PW + E1) for q in range(PARTS)]
                        dve.tensor_copy(b1_parts[rows[0], :], b1_src[rows[0], :]).then_inc(parts_ready, 1)
                        for q in (1, 2, 2):
                            r = rows[q]
                            then(dve.tensor_copy(b1_part[r, :], b1_src[r, :]))
                            then(dve.tensor_tensor(b1_src[r, :], b1_src[r, :], b1_part[r, :], ALU.subtract))
                        for r in rows[1:]:
                            dve.tensor_copy(b1_parts[r, :], b1_src[r, :]).then_inc(parts_ready, 1)
                        dve.wait_ge(mamba_loaded, 96)
                        for d in range(2):
                            for i in range(2):
                                m = dve.tensor_scalar(outw[:, d, i, :], outw[:, d, i, :], normw[:, d, i:i + 1], None, ALU.mult)
                        m.then_inc(outw_ready, 1)

                    setup()
                    dve.wait_ge(ident4_ready, 1)
                    n[0] = 0
                    CHUNK_STEPS = 3 * 3 * 2 + 2 * 2 + 6

                    def chunk(c):
                        def after(count):
                            dve.wait_ge(dve_steps2, c * CHUNK_STEPS + count)

                        xf = xc[:, 0, :, TAP - 1:CW]
                        for j in range(2):
                            full1(dve, c, "mask", j)
                            for ee in range(2):
                                m = dve.tensor_tensor(xm[:, 2 * j + ee, :].rearrange("p (b t) -> p b t", b=B),
                                                      psum1("mask", j)[:, ee * B * P:(ee + 1) * B * P].rearrange(
                                                          "p (b t) -> p b t", b=B), xf, ALU.mult)
                            taken1(m, "mask", j)
                        dve.wait_ge(bc_ready, 2 * c + START)
                        for d in range(2):
                            for tap in range(TAP):
                                for i in range(3):
                                    if tap:
                                        after(9 * d + 3 * (tap - 1) + i + 1)
                                    else:
                                        full1(dve, c, "conv", d, i)
                                    src = psum1("conv", d, i)[:, 0:B * CW].rearrange("p (b t) -> p b t", b=B)[:, :, tap:tap + P]
                                    w = convw[:, d, i, tap:tap + 1]
                                    if tap == 0:
                                        step(dve.tensor_scalar(cv[:, d, i, :, :], src, w, convb[:, d, i:i + 1],
                                                               ALU.mult, ALU.add), dve_steps2)
                                        continue
                                    m = dve.scalar_tensor_tensor(out=cv[:, d, i, :, :], in0=src, scalar=w,
                                                                 in1=cv[:, d, i, :, :], op0=ALU.mult, op1=ALU.add)
                                    if tap < TAP - 1:
                                        step(m, dve_steps2)
                                    else:
                                        taken1(m, "conv", d, i)
                        for d in range(2):
                            for b in range(B):
                                full1(dve, c, "L", d, b)
                                if b == 0:
                                    dve.wait_ge(xE_ready, 2 * c + START)
                                m = dve.tensor_tensor_scan(Lm[:, d, b, :, :].rearrange("s h t -> s (h t)"),
                                                           psum1("L", d, b)[:, :], ident4[:, :, :].rearrange("s h t -> s (h t)"),
                                                           0.0, ALU.mult, ALU.add)
                                taken1(m, "L", d, b)
                        for d in range(2):
                            for b in range(B):
                                done1(dve, c, "L", d, b)
                        full1(dve, c, "G")
                        for d in range(2):
                            for b in range(B):
                                q = (2 * d + b) * P
                                g = psum1("G")[:, q:q + P].unsqueeze(1).broadcast_to([P, MH, P])
                                m = dve.tensor_tensor(Mm[:, d, b, :, :], g, Lm[:, d, b, :, :], ALU.mult)
                            if d == 0:
                                m.then_inc(Mm_ready, 1)
                            else:
                                taken1(m, "G")
                        rows = lambda w: w[:, :].unsqueeze(1).broadcast_to([P, B, D])
                        full1(dve, c, "ffn")
                        dve.wait_ge(experts_loaded, 80)
                        taken1(dve.tensor_tensor(y_c[:, :, :], psum1("ffn")[:, 0:B * D].rearrange("t (b d) -> t b d", b=B),
                                                 rows(bo_b), ALU.add), "ffn")

                        def outputs(d):
                            dve.wait_ge(chunk_ready, c + 1)
                            dve.wait_ge(pool_steps, 4 * c + START)
                            for b in range(B):
                                full1(dve, c, "y", d, b)
                                y = psum1("y", d, b)
                                after(step(dve.tensor_tensor(yt[:, d, b, :].rearrange("p (h i) -> p h i", i=HD),
                                                             y[:, DI:2 * DI].rearrange("p (h i) -> p h i", i=HD),
                                                             Pc[:, d, b, :].unsqueeze(2).broadcast_to([P, MH, HD]), ALU.mult), dve_steps2))
                                taken1(dve.tensor_tensor(yt[:, d, b, :], y[:, 0:DI], yt[:, d, b, :], ALU.add), "y", d, b)
                            full1(dve, c, "S", d)
                            dve.wait_ge(S2_ready, 2 * c + (d + 1))
                            taken1(dve.tensor_tensor(S[:, d, :, :].rearrange("p b i -> p (b i)"), psum1("S", d)[0:MN, :],
                                                     S2[:, d, :, :].rearrange("p b i -> p (b i)"), ALU.add), "S", d)

                        done1(dve, c, "ffn")
                        then = lambda m: after(step(m, dve_steps2))
                        then(dve.tensor_tensor(y_c[:, :, :], y_c[:, :, :],
                                               xn2_all[:, :, bass.ds(c, 1), :].rearrange("p b o d -> p b (o d)"), ALU.add))
                        for b in range(B):
                            m = dve.bn_stats(stats1[:, b, :], y_c[:, b, :])
                        then(m)
                        mean_and_variance(dve, stats1, mean1, part1, ve1, 1e-12, then).then_inc(ve1_ready, 1)
                        outputs(0)
                        dve.wait_ge(rstd1_ready, c + 1)
                        for b in range(B):
                            m = dve.tensor_scalar(yh_c[:, b, :], y_c[:, b, :], mean1[:, b:b + 1], rstd1[:, b:b + 1],
                                                  ALU.subtract, ALU.mult)
                        then(m)
                        then(dve.tensor_tensor(yh_c[:, :, :], yh_c[:, :, :], rows(gamma_b), ALU.mult))
                        dve.tensor_tensor(yh_c[:, :, :], yh_c[:, :, :], rows(beta_b), ALU.add).then_inc(g_ready, 1)
                        outputs(1)
                        dve.wait_ge(th1_ready, c + 1)
                        dve.scalar_tensor_tensor(out=g_all[:, :, bass.ds(c, 1), :].rearrange("p b o d -> p b (o d)"),
                                                 in0=th1[:, :, :], scalar=1.0, in1=yh_c[:, :, :], op0=ALU.add, op1=ALU.mult)

                    with dve.Fori(0, NT) as c:
                        chunk(c)
                    assert n[0] == CHUNK_STEPS, n[0]
                    for n, (b, tiles) in enumerate(LAST):
                        full2(dve, 0, "s", n)
                        part = slice(tiles[0], tiles[-1] + 1, tiles[1] - tiles[0])
                        k = len(tiles)
                        taken2(dve.tensor_tensor(out_all[:, b, part, :], psum2("s", n)[:, 0:k * P].rearrange("t (k d) -> t k d", k=k),
                                                 g_all[:, b, part, :], ALU.mult), "s", n)
                        done2(dve, 0, "s", n)
                        x_b = x_all[:, 1 + b * NG:1 + (b + 1) * NG, :, :].rearrange("p g k d -> p (g k) d")
                        dve.scalar_tensor_tensor(out=out_all[:, b, part, :], in0=out_all[:, b, part, :], scalar=0.5,
                                                 in1=x_b[:, part, :], op0=ALU.mult, op1=ALU.add).then_inc(out_ready, 1)







def layouts(i):
    import numpy as np

    c = np.ascontiguousarray
    both = lambda n: (i["L1_attn_f_" + n], i["L1_attn_b_" + n])
    xbc = slice(DI, 2 * DI + 2 * MN)
    iw = both("in_w")
    dt = slice(2 * DI + 2 * MN, None)
    return {
        "x": i["L0_attn_x"], "w_qkv": i["L0_attn_w_qkv"], "w_gate": i["L0_attn_w_gate"],
        "w_out": c(i["L0_attn_w_out"].reshape(NP, P, D).transpose(1, 0, 2)),
        "wg": c(i["L0_ffn_Wg"].T), "bg": i["L0_ffn_bg"], "bias": i["L0_ffn_bias"],
        "w1": c(i["L0_ffn_W1"].transpose(0, 2, 1)), "ws1": c(i["L0_ffn_Ws1"].T),
        "w2": c(i["L0_ffn_W2"].reshape(E0, D, HT, P).transpose(0, 3, 2, 1)),
        "ws2": c(i["L0_ffn_Ws2"].reshape(D, HT, P).transpose(2, 1, 0)),
        "b1": c(i["L0_ffn_b1"].reshape(E0, HT, P).transpose(2, 0, 1)),
        "bs1": c(i["L0_ffn_bs1"].reshape(HT, P).T), "b2": i["L0_ffn_b2"], "bs2": i["L0_ffn_bs2"].reshape(1, D),
        "inw": c(np.stack([w[xbc].T for w in iw], 1)),
        "zw": c(np.stack([w[0:DI].T for w in iw], 1)),
        "dtw": c(np.concatenate([iw[0][dt].T, i["L1_ffn_W_router"], iw[1][dt].T], 1)),
        "convw": c(np.stack([w.reshape(3, P, TAP).transpose(1, 0, 2) for w in both("conv_w")], 1)),
        "convb": c(np.stack([w.reshape(3, P).T for w in both("conv_b")], 1)),
        "dt_bias": c(np.stack(both("dt_bias"))), "A_log": c(np.stack(both("A_log"))), "Dp": c(np.stack(both("Dp"))),
        "outw": c(np.stack([w.T.reshape(2, P, D).transpose(1, 0, 2) for w in both("out_w")], 1)),
        "normw": c(np.stack([w.reshape(2, P).T for w in both("norm_w")], 1)),
        "e1w1": c(i["L1_ffn_W1"].transpose(1, 0, 2)), "e1b1": i["L1_ffn_b1"],
        "e1wo": c(i["L1_ffn_Wo"].reshape(HT, P, D).transpose(1, 0, 2)),
        "bo": i["L1_ffn_bo"], "gamma": i["L1_ffn_ln_gamma"], "beta": i["L1_ffn_ln_beta"],
    }


def kernel(**inputs):
    import numpy as np
    import concourse.bacc as bacc
    from concourse.bass_utils import run_bass_kernel_spmd

    nc = bacc.Bacc("TRN2", target_bir_lowering=False, num_devices=1)
    arrays = layouts({n: np.asarray(v) for n, v in inputs.items()})
    a = {n: nc.dram_tensor(f"in_{n}", v.shape, mybir.dt.from_np(v.dtype), kind="ExternalInput").ap()
         for n, v in arrays.items()}
    out = nc.dram_tensor("out_x", (B, T, D), F32, kind="ExternalOutput").ap()
    build(nc, a, out)
    r = run_bass_kernel_spmd(nc, [{f"in_{n}": v for n, v in arrays.items()}], core_ids=[0])
    return r.results[0]["out_x"]
```
